# Optimizing a Trainium2 kernel written in Bass

```python
import numpy as np
import jax
import jax.numpy as jnp

def _softmax(x, axis=-1):
    return jax.nn.softmax(x, axis=axis)

def _gelu(x):
    return jax.nn.gelu(x, approximate=True)

def _silu(x):
    return jax.nn.silu(x)

def _sigmoid(x):
    return jax.nn.sigmoid(x)

def _layernorm(x, axis=-1, eps=1e-05):
    m = jnp.mean(x, axis=axis, keepdims=True)
    v = jnp.var(x, axis=axis, keepdims=True)
    return (x - m) / jnp.sqrt(v + eps)

def _scatter_add(tgt, idx, src, axis=0):
    return tgt.at[idx].add(src)

def _segment_sum(src, seg, n):
    return jax.ops.segment_sum(src, seg, n)
kernel_name = 'mk_gps_d1_gnn_r8_1146cb'

def setup_inputs(seed: int=0):
    np.random.seed(seed)
    _w = jnp.asarray

    def _rec_inputs():
        import jax
        import jax.numpy as jnp
        _gk = jax.random.key(seed)
        x = -0.0003713 + 1 * jax.random.normal(jax.random.fold_in(_gk, 1), (6250, 256), jnp.float32)
        _s = jax.random.randint(jax.random.fold_in(_gk, 2), (100000,), 0, 6250, jnp.int32)
        _d = jax.random.randint(jax.random.fold_in(_gk, 3), (100000,), 0, 6250, jnp.int32)
        _loop = jnp.arange(6250, dtype=jnp.int32)
        src = jnp.concatenate([_s, _d, _loop])
        dst = jnp.concatenate([_d, _s, _loop])
        _o = jnp.argsort(dst, stable=True)
        src = src[_o]
        dst = dst[_o]
        return (x, src, dst)
    x, src, dst = _rec_inputs()

    def _L0_gnn_setup():
        import jax, jax.numpy as jnp
        import numpy as np
        N_NODES = 6250
        N_EDGES = 100000
        FEATURES = 256
        HEADS = 8
        HEAD_DIM = FEATURES // HEADS
        LAYERS = 3
        NEG_SLOPE_ATTN = 0.2
        NEG_SLOPE_ACT = 0.01

        def _gat_layer(x, W, al, ar, b, src, dst, apply_act):
            h = (x @ W).reshape(N_NODES, HEADS, HEAD_DIM)
            el = jnp.einsum('nhd,hd->nh', h, al)
            er = jnp.einsum('nhd,hd->nh', h, ar)
            e = jax.nn.leaky_relu(el[src] + er[dst], negative_slope=NEG_SLOPE_ATTN)
            m = jax.ops.segment_max(e, dst, num_segments=N_NODES)
            ex = jnp.exp(e - m[dst])
            s = jax.ops.segment_sum(ex, dst, num_segments=N_NODES)
            a = ex / s[dst]
            msg = h[src] * a[:, :, None]
            out = jax.ops.segment_sum(msg, dst, num_segments=N_NODES)
            out = out + b.reshape(1, HEADS, HEAD_DIM)
            out = out.reshape(N_NODES, FEATURES)
            if apply_act:
                out = jax.nn.leaky_relu(out, negative_slope=NEG_SLOPE_ACT)
            return out
        key = jax.random.key(seed)
        ks = jax.random.split(key, 7)
        x = jax.random.normal(ks[0], (N_NODES, FEATURES), dtype=jnp.float32)
        src = jax.random.randint(ks[1], (N_EDGES,), 0, N_NODES, dtype=jnp.int32)
        dst = jax.random.randint(ks[2], (N_EDGES,), 0, N_NODES, dtype=jnp.int32)
        W = jax.random.normal(ks[3], (LAYERS, FEATURES, FEATURES), dtype=jnp.float32) / np.sqrt(FEATURES)
        al = jax.random.normal(ks[4], (LAYERS, HEADS, HEAD_DIM), dtype=jnp.float32) * 0.1
        ar = jax.random.normal(ks[5], (LAYERS, HEADS, HEAD_DIM), dtype=jnp.float32) * 0.1
        b = jnp.zeros((LAYERS, FEATURES), dtype=jnp.float32)
        return {'x': x, 'src': src, 'dst': dst, 'W': W, 'al': al, 'ar': ar, 'b': b}
    _L0_gnn_all = _L0_gnn_setup()
    _L0_gnn_in = {k: v for k, v in _L0_gnn_all.items() if k in ('W', 'al', 'ar', 'b')}
    del _L0_gnn_all

    def _L0_mix_setup():
        import jax, jax.numpy as jnp
        import numpy as np
        HEADS = 8
        DIM_HEAD = 64
        EPS = 1e-05

        def _inst_norm_lastdim(t):
            mu = jnp.mean(t, axis=-1, keepdims=True)
            var = jnp.mean(jnp.square(t - mu), axis=-1, keepdims=True)
            return (t - mu) * jax.lax.rsqrt(var + EPS)
        key = jax.random.key(seed)
        k1, k2, k3, k4 = jax.random.split(key, 4)
        b, n, dim = (4, 1024, 256)
        inner = HEADS * DIM_HEAD
        x = jax.random.normal(k1, (b, n, dim), dtype=jnp.float32)
        Wqkv = jax.random.normal(k2, (3 * inner, dim), dtype=jnp.float32) * (1.0 / np.sqrt(dim))
        Wout = jax.random.normal(k3, (dim, inner), dtype=jnp.float32) * (1.0 / np.sqrt(inner))
        bout = jax.random.normal(k4, (dim,), dtype=jnp.float32) * 0.01
        return {'x': x, 'Wqkv': Wqkv, 'Wout': Wout, 'bout': bout}
    _L0_mix_all = _L0_mix_setup()
    _L0_mix_in = {k: v for k, v in _L0_mix_all.items() if k in ('Wqkv', 'Wout', 'bout')}
    del _L0_mix_all

    def _L0_ffn_setup():
        import jax, jax.numpy as jnp
        import numpy as np
        NUM_EXPERTS = 8
        TOP_K = 2
        B, S, D = (8, 1024, 256)

        def _moe(tokens, router_w, w1, b1, w2, b2):
            N = tokens.shape[0]
            E = router_w.shape[0]
            logits = tokens.astype(jnp.float32) @ router_w.astype(jnp.float32).T
            probs = jax.nn.softmax(logits, axis=-1)
            rw, re = jax.lax.top_k(probs, TOP_K)
            if TOP_K > 1:
                rw = rw / jnp.maximum(rw.sum(-1, keepdims=True), 1e-12)
            rw = rw.astype(tokens.dtype)
            combine = jnp.zeros((N, E), tokens.dtype).at[jnp.arange(N)[:, None], re].set(rw)
            out = tokens
            for e in range(E):
                h = jax.nn.gelu(tokens @ w1[e] + b1[e], approximate=False)
                y = h @ w2[e] + b2[e]
                out = out + combine[:, e:e + 1] * y
            return out
        key = jax.random.key(seed)
        ks = jax.random.split(key, 4)
        scale = 1.0 / np.sqrt(D).astype(np.float32)
        return {'input_embeddings': jax.random.normal(ks[0], (B, S, D), jnp.float32), 'router_w': jax.random.normal(ks[1], (NUM_EXPERTS, D), jnp.float32) * scale, 'w1': jax.random.normal(ks[2], (NUM_EXPERTS, D, D), jnp.float32) * scale, 'b1': jnp.zeros((NUM_EXPERTS, D), jnp.float32), 'w2': jax.random.normal(ks[3], (NUM_EXPERTS, D, D), jnp.float32) * scale, 'b2': jnp.zeros((NUM_EXPERTS, D), jnp.float32)}
    _L0_ffn_all = _L0_ffn_setup()
    _L0_ffn_in = {k: v for k, v in _L0_ffn_all.items() if k in ('router_w', 'w1', 'b1', 'w2', 'b2')}
    del _L0_ffn_all
    return {'x': x, 'src': src, 'dst': dst, 'L0_gnn_W': _L0_gnn_in['W'], 'L0_gnn_al': _L0_gnn_in['al'], 'L0_gnn_ar': _L0_gnn_in['ar'], 'L0_gnn_b': _L0_gnn_in['b'], 'L0_mix_Wqkv': _L0_mix_in['Wqkv'], 'L0_mix_Wout': _L0_mix_in['Wout'], 'L0_mix_bout': _L0_mix_in['bout'], 'L0_ffn_router_w': _L0_ffn_in['router_w'], 'L0_ffn_w1': _L0_ffn_in['w1'], 'L0_ffn_b1': _L0_ffn_in['b1'], 'L0_ffn_w2': _L0_ffn_in['w2'], 'L0_ffn_b2': _L0_ffn_in['b2']}

def reference(x, src, dst, L0_gnn_W, L0_gnn_al, L0_gnn_ar, L0_gnn_b, L0_mix_Wqkv, L0_mix_Wout, L0_mix_bout, L0_ffn_router_w, L0_ffn_w1, L0_ffn_b1, L0_ffn_w2, L0_ffn_b2):
    import jax
    import jax.numpy as jnp

    def _L0_gnn_ref(x, src, dst, W, al, ar, b):
        import jax, jax.numpy as jnp
        import numpy as np
        N_NODES = 6250
        N_EDGES = 100000
        FEATURES = 256
        HEADS = 8
        HEAD_DIM = FEATURES // HEADS
        LAYERS = 3
        NEG_SLOPE_ATTN = 0.2
        NEG_SLOPE_ACT = 0.01

        def _gat_layer(x, W, al, ar, b, src, dst, apply_act):
            h = (x @ W).reshape(N_NODES, HEADS, HEAD_DIM)
            el = jnp.einsum('nhd,hd->nh', h, al)
            er = jnp.einsum('nhd,hd->nh', h, ar)
            e = jax.nn.leaky_relu(el[src] + er[dst], negative_slope=NEG_SLOPE_ATTN)
            m = jax.ops.segment_max(e, dst, num_segments=N_NODES)
            ex = jnp.exp(e - m[dst])
            s = jax.ops.segment_sum(ex, dst, num_segments=N_NODES)
            a = ex / s[dst]
            msg = h[src] * a[:, :, None]
            out = jax.ops.segment_sum(msg, dst, num_segments=N_NODES)
            out = out + b.reshape(1, HEADS, HEAD_DIM)
            out = out.reshape(N_NODES, FEATURES)
            if apply_act:
                out = jax.nn.leaky_relu(out, negative_slope=NEG_SLOPE_ACT)
            return out
        for i in range(LAYERS):
            x = _gat_layer(x, W[i], al[i], ar[i], b[i], src, dst, apply_act=i + 1 < LAYERS)
        return x

    def _L0_mix_ref(x, Wqkv, Wout, bout):
        import jax, jax.numpy as jnp
        import numpy as np
        HEADS = 8
        DIM_HEAD = 64
        EPS = 1e-05

        def _inst_norm_lastdim(t):
            mu = jnp.mean(t, axis=-1, keepdims=True)
            var = jnp.mean(jnp.square(t - mu), axis=-1, keepdims=True)
            return (t - mu) * jax.lax.rsqrt(var + EPS)
        b, n, dim = x.shape
        qkv = jnp.einsum('bnc,fc->bnf', x, Wqkv)
        q, k, v = jnp.split(qkv, 3, axis=-1)

        def to_heads(t):
            return t.reshape(b, n, HEADS, DIM_HEAD).transpose(0, 2, 1, 3)
        q, k, v = (to_heads(q), to_heads(k), to_heads(v))
        k = _inst_norm_lastdim(k)
        v = _inst_norm_lastdim(v)
        dots = jnp.einsum('bhnd,bhne->bhde', k, v)
        out = jnp.einsum('bhnd,bhde->bhne', q, dots) / n
        out = out.transpose(0, 2, 1, 3).reshape(b, n, HEADS * DIM_HEAD)
        return jnp.einsum('bnf,cf->bnc', out, Wout) + bout

    def _L0_ffn_ref(input_embeddings, router_w, w1, b1, w2, b2):
        import jax, jax.numpy as jnp
        import numpy as np
        NUM_EXPERTS = 8
        TOP_K = 2
        B, S, D = (8, 1024, 256)

        def _moe(tokens, router_w, w1, b1, w2, b2):
            N = tokens.shape[0]
            E = router_w.shape[0]
            logits = tokens.astype(jnp.float32) @ router_w.astype(jnp.float32).T
            probs = jax.nn.softmax(logits, axis=-1)
            rw, re = jax.lax.top_k(probs, TOP_K)
            if TOP_K > 1:
                rw = rw / jnp.maximum(rw.sum(-1, keepdims=True), 1e-12)
            rw = rw.astype(tokens.dtype)
            combine = jnp.zeros((N, E), tokens.dtype).at[jnp.arange(N)[:, None], re].set(rw)
            out = tokens
            for e in range(E):
                h = jax.nn.gelu(tokens @ w1[e] + b1[e], approximate=False)
                y = h @ w2[e] + b2[e]
                out = out + combine[:, e:e + 1] * y
            return out
        b, s, d = input_embeddings.shape
        tokens = input_embeddings.reshape(b * s, d)
        return _moe(tokens, router_w, w1, b1, w2, b2).reshape(b, s, d)
    xn = _layernorm(x, axis=-1)
    x = x + _L0_gnn_ref(xn, src, dst, L0_gnn_W, L0_gnn_al, L0_gnn_ar, L0_gnn_b) + _L0_mix_ref(xn[None], L0_mix_Wqkv, L0_mix_Wout, L0_mix_bout)[0]
    x = x + _L0_ffn_ref(_layernorm(x, axis=-1)[None], L0_ffn_router_w, L0_ffn_w1, L0_ffn_b1, L0_ffn_w2, L0_ffn_b2)[0]
    return x

_drawn_inputs = setup_inputs


def setup_inputs(seed=0):
    import zlib

    import numpy as np

    out = dict(_drawn_inputs(seed))
    spreads = {'L0_gnn_b': (0.0, 0.1), 'L0_ffn_b1': (0.0, 0.347), 'L0_ffn_b2': (0.0, 0.1)}
    factors = {'L0_gnn_ar': 8.0, 'L0_mix_bout': 3.718}
    for name, (base, spread) in spreads.items():
        noise = np.random.default_rng([zlib.crc32(name.encode()), seed]).standard_normal(out[name].shape)
        drawn = base * np.exp(spread * noise) if base else spread * noise
        out[name] = jnp.asarray(drawn.astype(out[name].dtype))
    for name, factor in factors.items():
        out[name] = (out[name] * factor).astype(out[name].dtype)
    return out
```

```python
import concourse.bass as bass
from concourse import mybir
from contextlib import ExitStack

F32 = mybir.dt.float32
BF16 = mybir.dt.bfloat16
I32 = mybir.dt.int32
U32 = mybir.dt.uint32
ALU = mybir.AluOpType
ACT = mybir.ActivationFunctionType
AX = mybir.AxisListType

P = 128
NODES, FEAT = 6250, 256
EDGES = 2 * 100000 + NODES
HEADS, HD = 8, 32
LAYERS = 3
FC = FEAT // P
NT = -(-NODES // P)
NODES_PAD = NT * P
ET = -(-EDGES // P)
BV = 8
VISITS = -(-(ET + NT - 1) // BV) * BV
NB = VISITS // BV
TILES = VISITS - NT + 1
CH = -(-VISITS // P)
VP = CH * P
BE = BV * P
ROW = HEADS * (HD + 1)
EXT = ROW + HEADS
NEG = -1.0e30
EPS = 1e-5
MH, MD = 8, 64
INNER = MH * MD
PAIRS = INNER // P
EXPERTS = 8


def need(eng, sem, count):
    if not isinstance(count, int) or count > 0:
        eng.wait_ge(sem, count)


def steps(eng, total, unroll, step, tail=0):
    for n in range(unroll):
        step(n, n)
    rounds = (total - tail) // unroll
    with eng.Fori(1, rounds) as i:
        for u in range(unroll):
            step(i * unroll + u, u)
    for n in range(rounds * unroll, total):
        step(n, n % unroll)


def uses(n, slot, slots):
    return (n - slot) // slots


def slot_total(total, slot, slots):
    return (total - 1 - slot) // slots + 1


def heads_of(ap, width):
    return ap.rearrange("p (h k) -> p h k", k=width)


def constants(nc, T):
    with ExitStack() as ctx:
        made = ctx.enter_context(nc.semaphore("const_made"))
        with nc.Block() as block:
            @block.gpsimd
            def _(pool):
                pool.memset(T.ident[:, :], 0.0).then_inc(made, 1)
                pool.wait_ge(made, 1)
                pool.affine_select(out=T.ident[:, :], in_=T.ident[:, :], compare_op=ALU.not_equal, fill=1.0,
                                   base=0, pattern=[[-1, P]], channel_multiplier=1).then_inc(made, 1)
                pool.iota(T.row[:, :], pattern=[[1, P]], base=0, channel_multiplier=0,
                          allow_small_or_imprecise_dtypes=True).then_inc(made, 1)
                pool.iota(T.col[:, :], pattern=[[0, 1]], base=0, channel_multiplier=1,
                          allow_small_or_imprecise_dtypes=True).then_inc(made, 1)
                pool.wait_ge(made, 4)


def edge_tables(nc, T, dst_last, src_tiles, dst_tiles):
    with ExitStack() as ctx:
        def sb(name, shape, dt=F32):
            return ctx.enter_context(nc.sbuf_tensor(name, shape, dt))

        def sem(name):
            return ctx.enter_context(nc.semaphore(name))

        last = sb("last", [P, TILES], I32)
        tile_no = sb("tile_no", [P, TILES], I32)
        path = sb("path", [P, TILES])
        below = sb("below", [P, TILES])
        visit_i = sb("visit_i", [P, CH], I32)
        visit = sb("visit", [P, CH])
        tile_of = sb("tile_of", [P, CH])
        tile_idx = sb("tile_idx", [P, CH], I32)
        win_of = sb("win_of", [P, CH])
        win_i = sb("win_i", [P, CH], I32)
        win_base = sb("win_base", [P, CH])
        src_v = sb("src_v", [P, CH, P], I32)
        dst_v = sb("dst_v", [P, CH, P], I32)
        src_f = sb("src_f", [P, CH, P])
        loc = sb("loc", [P, CH, P])
        inside = sb("inside", [P, CH, P])
        locm = sb("locm", [P, CH, P])
        locb = sb("locb", [P, CH, P], BF16)
        key = sb("key", [P, CH, P])
        prev = sb("prev", [P, CH, P])
        edge = sb("edge", [1, 8])
        banks = [ctx.enter_context(nc.psum_tensor(f"tp{i}", [P, 512], F32)) for i in range(8)]
        loaded, iotas, step, gathered, turned, evacuated, stored, shifted, dtab = map(sem, (
            "tab_loaded", "tab_iotas", "tab_step", "tab_gathered", "tab_turned", "tab_evacuated",
            "tab_stored", "tab_shifted", "tab_dtab"))
        groups = [(4 * g, min(4, CH - 4 * g)) for g in range(-(-CH // 4))]
        NG = len(groups)
        done = {}

        with nc.Block() as block:
            @block.vector
            def _(dve):
                count = [0]

                def link(ins, name=None):
                    count[0] += 1
                    ins.then_inc(step, 1)
                    dve.wait_ge(step, count[0])
                    if name:
                        done[name] = count[0]

                dve.wait_ge(loaded, 16)
                link(dve.tensor_scalar(last[:, :], last[:, :], 7, None, ALU.arith_shift_right))
                dve.wait_ge(iotas, 2)
                link(dve.tensor_tensor(path[:, :], last[:, :], tile_no[:, :], ALU.add))
                link(dve.tensor_copy(visit[:, :], visit_i[:, :]))
                for c in range(CH):
                    link(dve.tensor_scalar(below[:, :], path[:, :], visit[:, c:c + 1], None, ALU.is_lt, ALU.add,
                                           accum_out=tile_of[:, c:c + 1]))
                link(dve.tensor_tensor(win_of[:, :], visit[:, :], tile_of[:, :], ALU.subtract))
                link(dve.tensor_scalar(tile_of[:, :], tile_of[:, :], float(TILES - 1), None, ALU.min))
                link(dve.tensor_scalar(win_of[:, :], win_of[:, :], float(NT - 1), None, ALU.min))
                link(dve.tensor_copy(tile_idx[:, :], tile_of[:, :]), "tile_idx")
                link(dve.tensor_copy(win_i[:, :], win_of[:, :]), "win")
                link(dve.tensor_scalar(win_base[:, :], win_of[:, :], -float(P), None, ALU.mult))
                link(dve.memset(edge[:, 0:1], -2.0))
                link(dve.memset(edge[:, 1:8], 0.0), "edge")
                dve.wait_ge(gathered, 2 * CH * 16)
                link(dve.tensor_copy(src_f[:, :, :], src_v[:, :, :]), "src_f")
                for c in range(CH):
                    link(dve.tensor_scalar(loc[:, c, :], dst_v[:, c, :], win_base[:, c:c + 1], None, ALU.add))
                link(dve.tensor_scalar(inside[:, :, :], loc[:, :, :], 0.0, None, ALU.is_ge))
                link(dve.scalar_tensor_tensor(inside[:, :, :], loc[:, :, :], float(P - 1), inside[:, :, :],
                                              ALU.is_le, ALU.mult))
                link(dve.scalar_tensor_tensor(locm[:, :, :], loc[:, :, :], 1.0, inside[:, :, :], ALU.add, ALU.mult))
                link(dve.tensor_scalar(locm[:, :, :], locm[:, :, :], -1.0, None, ALU.add))
                link(dve.tensor_copy(locb[:, :, :], locm[:, :, :]), "locm")
                link(dve.scalar_tensor_tensor(key[:, :, :], dst_v[:, :, :], 1.0, inside[:, :, :], ALU.add, ALU.mult))
                link(dve.tensor_scalar(key[:, :, :], key[:, :, :], -1.0, None, ALU.add), "key")
                dve.wait_ge(shifted, 16)
                link(dve.tensor_tensor(prev[:, :, :], key[:, :, :], prev[:, :, :], ALU.not_equal))
                link(dve.tensor_scalar(prev[:, :, :], prev[:, :, :], NEG, None, ALU.mult), "flag")

            @block.gpsimd
            def _(pool):
                pool.iota(tile_no[:, :], pattern=[[1, TILES]], base=0, channel_multiplier=0).then_inc(iotas, 1)
                pool.iota(visit_i[:, :], pattern=[[P, CH]], base=0, channel_multiplier=1).then_inc(iotas, 1)
                pool.wait_ge(step, done["tile_idx"])
                for c in range(CH):
                    for table, rows in ((src_v, src_tiles), (dst_v, dst_tiles)):
                        pool.indirect_dma_start(
                            table[:, c, :], None, rows,
                            bass.IndirectOffsetOnAxis(ap=tile_idx[:, c:c + 1].bitcast(U32), axis=0),
                        ).then_inc(gathered, 16)

            @block.tensor
            def _(pe):
                for table, name, off in ((src_f, "src_f", 0), (locm, "locm", NG)):
                    pe.wait_ge(step, done[name])
                    for g, (c0, k) in enumerate(groups):
                        for j in range(k):
                            t = nc.tensor.transpose(banks[off + g][:, j * P:(j + 1) * P], table[:, c0 + j, :],
                                                    T.ident[:, :])
                        t.then_inc(turned, 1)

            @block.scalar
            def _(act):
                for off, out in ((0, T.src_t), (NG, T.loc_t)):
                    for g, (c0, k) in enumerate(groups):
                        act.wait_ge(turned, off + g + 1)
                        nc.scalar.activation(out[:, c0 * P:(c0 + k) * P], banks[off + g][:, 0:k * P],
                                             ACT.Copy).then_inc(evacuated, 1)

            @block.sync
            def _(sp):
                sp.dma_start(last[:, :], dst_last[None, :].to_broadcast([P, TILES])).then_inc(loaded, 16)
                sp.wait_ge(step, done["win"])
                with nc.allow_non_contiguous_dma(reason="a table of one word per visit"):
                    sp.dma_start(T.win_d[:].rearrange("(c p) -> p c", p=P), win_i[:, :]).then_inc(dtab, 16)
                sp.wait_ge(dtab, 16)
                sp.dma_start(T.win[0:1, :], T.win_d[:][None, :]).then_inc(dtab, 16)
                sp.wait_ge(step, done["edge"])
                sp.dma_start(T.key_d[0:1][None, :], edge[0:1, 0:1]).then_inc(stored, 16)
                sp.dma_start(T.flag_d[VP * P:VP * P + 7][None, :], edge[0:1, 1:8]).then_inc(stored, 16)
                sp.wait_ge(step, done["locm"])
                sp.dma_start(T.loc_d[:].rearrange("(c p e) -> p c e", p=P, e=P), locb[:, :, :]).then_inc(stored, 16)
                sp.wait_ge(step, done["key"])
                sp.dma_start(T.key_d[1:1 + VP * P].rearrange("(c p e) -> p c e", p=P, e=P),
                             key[:, :, :]).then_inc(stored, 16)
                sp.wait_ge(stored, 64)
                sp.dma_start(prev[:, :, :], T.key_d[0:VP * P].rearrange("(c p e) -> p c e", p=P, e=P)).then_inc(shifted, 16)
                sp.wait_ge(step, done["flag"])
                sp.dma_start(T.flag_d[0:VP * P].rearrange("(c p e) -> p c e", p=P, e=P), prev[:, :, :]).then_inc(stored, 16)
                sp.wait_ge(stored, 80)
                sp.wait_ge(dtab, 32)
                sp.wait_ge(evacuated, 2 * NG)


def split_er(dve, T, tmp, sem, base):
    k = [base]

    def link(ins):
        k[0] += 1
        ins.then_inc(sem, 1)
        dve.wait_ge(sem, k[0])

    link(dve.tensor_copy(T.er3[:, :, 0, :], T.er[:, :, :]))
    link(dve.tensor_tensor(tmp, T.er[:, :, :], T.er3[:, :, 0, :], ALU.subtract))
    link(dve.tensor_copy(T.er3[:, :, 1, :], tmp))
    link(dve.tensor_tensor(tmp, tmp, T.er3[:, :, 1, :], ALU.subtract))
    link(dve.tensor_copy(T.er3[:, :, 2, :], tmp))


def weights(nc, T, W, al, ar, wkv_t):
    with ExitStack() as ctx:
        def sb(name, shape, dt=F32):
            return ctx.enter_context(nc.sbuf_tensor(name, shape, dt))

        w_in = sb("w_in", [P, LAYERS, FC, FEAT])
        a_in = sb("a_in", [P, 2, LAYERS, FEAT])
        prod = sb("prod", [P, FC, FEAT])
        mean = sb("mean", [P, FC, 2 * MH])
        loaded = ctx.enter_context(nc.semaphore("w_loaded"))
        step = ctx.enter_context(nc.semaphore("w_step"))
        with nc.Block() as block:
            @block.sync
            def _(sp):
                sp.dma_start(w_in[:, :, :, :], W.rearrange("l (c p) n -> p l c n", p=P)).then_inc(loaded, 16)
                for j, a in enumerate((al, ar)):
                    sp.dma_start(a_in[:, j, :, :], a.rearrange("l h d -> l (h d)")[None, :, :]
                                 .to_broadcast([P, LAYERS, FEAT])).then_inc(loaded, 16)
                sp.dma_start(T.wkv[:, :, :], wkv_t.rearrange("(c p) n -> p c n", p=P)).then_inc(loaded, 16)

            @block.vector
            def _(dve):
                n = [0]

                def link(ins):
                    n[0] += 1
                    ins.then_inc(step, 1)
                    dve.wait_ge(step, n[0])

                dve.wait_ge(loaded, 64)
                for l in range(LAYERS):
                    for c in range(FC):
                        w = T.wext[:, l, c, 0:ROW].rearrange("p (h k) -> p h k", k=HD + 1)
                        link(dve.tensor_copy(w[:, :, 0:HD], heads_of(w_in[:, l, c, :], HD)))
                        for j, out in ((0, w[:, :, HD:HD + 1]), (1, T.wext[:, l, c, ROW:EXT].unsqueeze(2))):
                            link(dve.tensor_tensor(prod[:, c, :], w_in[:, l, c, :], a_in[:, j, l, :], ALU.mult))
                            link(dve.tensor_reduce(out, heads_of(prod[:, c, :], HD), AX.X, ALU.add))
                wk = T.wkv[:, :, :].rearrange("p c (h d) -> p c h d", d=MD)
                link(dve.tensor_reduce(mean[:, :, :].unsqueeze(3), wk, AX.X, ALU.add))
                link(dve.tensor_scalar(mean[:, :, :], mean[:, :, :], 1.0 / MD, None, ALU.mult))
                for c in range(FC):
                    link(dve.tensor_tensor(wk[:, c], wk[:, c], mean[:, c, :].unsqueeze(2)
                                           .to_broadcast([P, 2 * MH, MD]), ALU.subtract))


def first_nodes(nc, T, x):
    with ExitStack() as ctx:
        def sb(name, shape, dt=F32):
            return ctx.enter_context(nc.sbuf_tensor(name, shape, dt))

        def sem(name):
            return ctx.enter_context(nc.semaphore(name))

        def ps(name, shape):
            return ctx.enter_context(nc.psum_tensor(name, shape, F32))

        S = 2
        xs = sb("xs", [P, S, FEAT])
        st = sb("st", [P, S, 6])
        mv = sb("mv", [P, S, 2])
        sd = sb("sd", [P, S, 2])
        xn = sb("xn", [P, S, FEAT])
        xt = sb("xt", [P, S, FC, P])
        rows = sb("rows", [P, S, ROW])
        kc = sb("kc", [P, S, INNER])
        vc = sb("vc", [P, S, INNER])
        sq = sb("sq", [P, S, 2 * INNER])
        var = sb("var", [P, S, 2 * MH])
        dev = sb("dev", [P, S, 2 * MH])
        wt = sb("wt", [P, S, MH])
        tmp = sb("tmp", [P, NT, HEADS])
        xt_ps = ps("xt_ps", [P, FC * P])
        kv_ps = [ps("k_ps", [P, INNER]), ps("v_ps", [P, INNER])]
        row_ps = ps("row_ps", [P, EXT])
        dot_ps = ps("dot_ps", [P, PAIRS * P])
        x_in = [sem(f"n_x_in{u}") for u in range(S)]
        row_stored = [sem(f"n_row_stored{u}") for u in range(S)]
        xt_stored = [sem(f"n_xt_stored{u}") for u in range(S)]
        stat, var_eps, rooted, inv, xn_done, turned, xt_done, kv_done, row_done, row_out, er_done, \
            squared, k_out, sums, sums2, rooted2, inv2, wt_done, v_done, dots, added, split, passed = map(sem, (
                "n_stat", "n_var_eps", "n_rooted", "n_inv", "n_xn", "n_turned", "n_xt", "n_kv", "n_row",
                "n_row_out", "n_er", "n_squared", "n_k_out", "n_sums", "n_sums2",
                "n_rooted2", "n_inv2", "n_wt", "n_v", "n_dots", "n_added", "n_split", "n_passed"))

        with nc.Block() as block:
            @block.sync
            def _(sp):
                def step(n, u):
                    need(sp, xn_done, n - 1)
                    sp.dma_start(xs[:, u, :], x[bass.ds(n * P, P), :]).then_inc(x_in[u], 16)
                steps(sp, NT, S, step)

            @block.gpsimd
            def _(pool):
                def step(n, u):
                    need(pool, xt_done, n + 1)
                    pool.dma_start(T.xt_d[bass.ds(n * P, P), :], xt[:, u, :, :].rearrange("p c n -> p (c n)")
                                   ).then_inc(xt_stored[u], 16)
                    need(pool, row_out, n + 1)
                    pool.dma_start(T.rows_d[0][bass.ds(n * P, P), :], rows[:, u, :]).then_inc(row_stored[u], 16)
                steps(pool, NT, S, step)
                for u in range(S):
                    pool.wait_ge(xt_stored[u], 16 * slot_total(NT, u, S))
                    pool.wait_ge(row_stored[u], 16 * slot_total(NT, u, S))

            @block.vector
            def _(dve):
                def norm(n, u):
                    need(dve, x_in[u], (n // 2 if isinstance(n, int) else (n - u) // 2) * 16 + 16)
                    dve.bn_stats(st[:, u, :], xs[:, u, :]).then_inc(stat, 1)
                    need(dve, stat, 2 * n + 1)
                    dve.sem_inc(passed, 1)
                    dve.bn_aggr(mv[:, u, :], st[:, u, :]).then_inc(stat, 1)
                    need(dve, stat, 2 * n + 2)
                    need(dve, rooted, n - 1)
                    dve.tensor_scalar(sd[:, u, 0:1], mv[:, u, 1:2], EPS, None, ALU.add).then_inc(var_eps, 1)

                def norm_end(n, u):
                    need(dve, rooted, n + 1)
                    dve.reciprocal(sd[:, u, 1:2], sd[:, u, 1:2]).then_inc(inv, 1)
                    need(dve, inv, n + 1)
                    need(dve, turned, n - 1)
                    dve.tensor_scalar(xn[:, u, :], xs[:, u, :], mv[:, u, 0:1], sd[:, u, 1:2], ALU.subtract,
                                      ALU.mult).then_inc(xn_done, 1)

                def mix(n, u):
                    need(dve, squared, 2 * n + 2)
                    dve.tensor_reduce(var[:, u, :].unsqueeze(2), sq[:, u, :].rearrange("p (h d) -> p h d", d=MD),
                                      AX.X, ALU.add).then_inc(sums, 1)
                    need(dve, sums, n + 1)
                    dve.tensor_scalar(var[:, u, :], var[:, u, :], 1.0 / MD, EPS, ALU.mult, ALU.add).then_inc(sums2, 1)

                def mix_end(n, u):
                    need(dve, rooted2, n + 1)
                    dve.reciprocal(dev[:, u, :], dev[:, u, :]).then_inc(inv2, 1)
                    need(dve, inv2, n + 1)
                    dve.tensor_tensor(wt[:, u, :], dev[:, u, 0:MH], dev[:, u, MH:2 * MH], ALU.mult).then_inc(wt_done, 1)
                    need(dve, wt_done, n + 1)
                    need(dve, dots, n - 1)
                    dve.tensor_tensor(vc[:, u, :].rearrange("p (h d) -> p h d", d=MD),
                                      kv_ps[1][:, :].rearrange("p (h d) -> p h d", d=MD),
                                      wt[:, u, :].unsqueeze(2).to_broadcast([P, MH, MD]), ALU.mult).then_inc(v_done, 1)

                def add(n):
                    need(dve, dots, n + 1)
                    need(dve, added, n + 1)
                    dve.tensor_tensor(T.dots[:, :], T.dots[:, :], dot_ps[:, :], ALU.add).then_inc(added, 1)

                dve.memset(T.dots[:, :], 0.0).then_inc(added, 1)
                norm(0, 0)
                norm_end(0, 0)

                def step(n, u):
                    more = not isinstance(n, int) or n + 1 < NT
                    if more:
                        norm(n + 1, 1 - u)
                    mix(n, u)
                    if more:
                        norm_end(n + 1, 1 - u)
                    if not isinstance(n, int) or n > 0:
                        add(n - 1)
                    mix_end(n, u)
                steps(dve, NT, S, step, tail=1)
                add(NT - 1)
                dve.wait_ge(er_done, NT)
                split_er(dve, T, tmp[:, :, :], split, 0)

            @block.scalar
            def _(act):
                def root(n, u):
                    need(act, var_eps, n + 1)
                    need(act, inv, n - 1)
                    nc.scalar.activation(sd[:, u, 1:2], sd[:, u, 0:1], ACT.Sqrt).then_inc(rooted, 1)

                root(0, 0)

                def step(n, u):
                    need(act, turned, n + 1)
                    need(act, row_done, n - 1)
                    need(act, xt_stored[u], 16 * uses(n, u, S))
                    nc.scalar.activation(xt[:, u, :, :].rearrange("p c n -> p (c n)"), xt_ps[:, :],
                                         ACT.Copy).then_inc(xt_done, 1)
                    if not isinstance(n, int) or n + 1 < NT:
                        root(n + 1, 1 - u)
                    need(act, sums, n - 1)
                    need(act, kv_done, 2 * n + 1)
                    nc.scalar.activation(sq[:, u, 0:INNER], kv_ps[0][:, :], ACT.Square).then_inc(squared, 1)
                    need(act, kv_done, 2 * n + 2)
                    nc.scalar.activation(sq[:, u, INNER:2 * INNER], kv_ps[1][:, :], ACT.Square).then_inc(squared, 1)
                    need(act, dots, n - 1)
                    nc.scalar.activation(kc[:, u, :], kv_ps[0][:, :], ACT.Copy).then_inc(k_out, 1)
                    need(act, row_done, n + 1)
                    need(act, row_stored[u], 16 * uses(n, u, S))
                    nc.scalar.activation(rows[:, u, :], row_ps[:, 0:ROW], ACT.Copy).then_inc(row_out, 1)
                    nc.scalar.activation(T.er_flat[:, bass.ds(n * HEADS, HEADS)], row_ps[:, ROW:EXT],
                                         ACT.Copy).then_inc(er_done, 1)
                    need(act, sums2, n + 1)
                    need(act, inv2, n - 1)
                    nc.scalar.activation(dev[:, u, :], var[:, u, :], ACT.Sqrt).then_inc(rooted2, 1)
                steps(act, NT, S, step, tail=1)

            @block.tensor
            def _(pe):
                def step(n, u):
                    need(pe, xn_done, n + 1)
                    need(pe, xt_done, n)
                    for c in range(FC):
                        t = nc.tensor.transpose(xt_ps[:, c * P:(c + 1) * P], xn[:, u, c * P:(c + 1) * P], T.ident[:, :])
                    t.then_inc(turned, 1)
                    if not isinstance(n, int) or n > 0:
                        dot(n - 1, 1 - u)
                    need(pe, xt_done, n + 1)
                    need(pe, k_out, n)
                    need(pe, v_done, n)
                    for j in range(2):
                        for c in range(FC):
                            t = nc.tensor.matmul(kv_ps[j][:, :], xt[:, u, c, :],
                                                 T.wkv[:, c, j * INNER:(j + 1) * INNER],
                                                 start=(c == 0), stop=(c == FC - 1))
                        t.then_inc(kv_done, 1)
                    need(pe, row_out, n)
                    need(pe, er_done, n)
                    for c in range(FC):
                        t = nc.tensor.matmul(row_ps[:, :], xt[:, u, c, :], T.wext[:, 0, c, :],
                                             start=(c == 0), stop=(c == FC - 1))
                    t.then_inc(row_done, 1)

                def dot(n, u):
                    need(pe, v_done, n + 1)
                    need(pe, k_out, n + 1)
                    need(pe, added, n + 1)
                    for q in range(PAIRS):
                        t = nc.tensor.matmul(dot_ps[:, q * P:(q + 1) * P], vc[:, u, q * P:(q + 1) * P],
                                             kc[:, u, q * P:(q + 1) * P], start=True, stop=True)
                    t.then_inc(dots, 1)

                steps(pe, NT, S, step, tail=1)
                dot(NT - 1, (NT - 1) % S)


def mix_matrix(nc, T, wq, wo_t):
    with ExitStack() as ctx:
        def sb(name, shape, dt=F32):
            return ctx.enter_context(nc.sbuf_tensor(name, shape, dt))

        wq_sb = sb("wq_sb", [P, PAIRS, FEAT])
        wo_sb = sb("wo_sb", [P, PAIRS, FEAT])
        diag = sb("diag", [P, PAIRS, P])
        a_sb = sb("a_sb", [P, PAIRS, FEAT])
        a_ps = [ctx.enter_context(nc.psum_tensor(f"a_ps{q}", [P, FEAT], F32)) for q in range(PAIRS)]
        g_ps = [ctx.enter_context(nc.psum_tensor(f"g_ps{q}", [P, FEAT], F32)) for q in range(FC)]
        loaded, cleared, diag_done, a_done, a_out, g_done, g_out = [
            ctx.enter_context(nc.semaphore("m_" + s)) for s in
            ("loaded", "cleared", "diag", "a", "a_out", "g", "g_out")]
        with nc.Block() as block:
            @block.sync
            def _(sp):
                sp.dma_start(wq_sb[:, :, :], wq.rearrange("(q p) n -> p q n", p=P)).then_inc(loaded, 16)
                sp.dma_start(wo_sb[:, :, :], wo_t.rearrange("(q p) n -> p q n", p=P)).then_inc(loaded, 16)

            @block.vector
            def _(dve):
                dve.memset(diag[:, :, :], 0.0).then_inc(cleared, 1)
                dve.wait_ge(cleared, 1)
                d = T.dots[:, :].rearrange("p (q n) -> p q n", n=P)
                for h in range(2):
                    s = slice(h * MD, (h + 1) * MD)
                    dve.tensor_scalar(diag[s, :, s], d[s, :, s], 1.0 / NODES, None, ALU.mult).then_inc(diag_done, 1)
                for q in range(PAIRS):
                    dve.wait_ge(a_done, q + 1)
                    dve.tensor_copy(a_sb[:, q, :], a_ps[q][:, :]).then_inc(a_out, 1)
                for c in range(FC):
                    dve.wait_ge(g_done, c + 1)
                    dve.tensor_copy(T.mixw[:, c, :], g_ps[c][:, :]).then_inc(g_out, 1)

            @block.tensor
            def _(pe):
                pe.wait_ge(loaded, 32)
                pe.wait_ge(diag_done, 2)
                for q in range(PAIRS):
                    nc.tensor.matmul(a_ps[q][:, :], diag[:, q, :], wo_sb[:, q, :], start=True,
                                     stop=True).then_inc(a_done, 1)
                pe.wait_ge(a_out, PAIRS)
                for c in range(FC):
                    for q in range(PAIRS):
                        t = nc.tensor.matmul(g_ps[c][:, :], wq_sb[:, q, c * P:(c + 1) * P], a_sb[:, q, :],
                                             start=(q == 0), stop=(q == PAIRS - 1))
                    t.then_inc(g_done, 1)


def edge_pass(nc, T, S, l):
    N0 = l * NB
    GS = S.slots

    with nc.Block() as block:
        @block.gpsimd
        def _(pool):
            def fetch_indices(n, u):
                pool.tensor_copy(S.idx[:, u, :], T.src_t[:, bass.ds(n * BV, BV)]).then_inc(S.idx_ready, 1)

            if l == 0:
                pool.memset(T.acc[:, :], 0.0).then_inc(S.acc_cleared, 1)
            fetch_indices(0, 0)

            def step(n, u):
                need(pool, S.summed, BV * (N0 + n - GS + 1))
                if not isinstance(n, int) or n + 1 < NB:
                    nxt = (u + 1) % GS
                    if isinstance(n, int) and n + 1 < GS:
                        if l > 0:
                            need(pool, S.gathered[nxt], 16 * BV * (NB // GS) * l)
                    else:
                        need(pool, S.gathered[nxt], 16 * BV * ((NB // GS) * l + (n + 1 - nxt) // GS))
                    fetch_indices(n + 1, nxt)
                need(pool, S.idx_ready, N0 + n + 1)
                pool.sem_inc(S.issuing, 1)
                for v in range(BV):
                    pool.indirect_dma_start(
                        S.rows[:, u, v, :], None, T.rows_d[l],
                        bass.IndirectOffsetOnAxis(ap=S.idx[:, u, v:v + 1].bitcast(U32), axis=0),
                    ).then_inc(S.gathered[u], 16)
            steps(pool, NB, GS, step, tail=1)

        @block.sync
        def _(sp):
            def step(n, u):
                need(sp, S.resc_made, N0 + n - GS + 1)
                sp.dma_start(S.loc_row[:, u, :], T.loc_d[bass.ds(n * BE, BE)][None, :].to_broadcast([P, BE])
                             ).then_inc(S.tables[u], 16)
                sp.dma_start(S.flags[:, u, :], T.flag_d[bass.ds(n * BE, BE + 1)][None, :]
                             .to_broadcast([HEADS, BE + 1])).then_inc(S.tables[u], 16)
            steps(sp, NB, GS, step, tail=1)

        @block.vector
        def _(dve):
            def one_hot_t(n, u):
                need(dve, S.tables[u], 32 * ((NB // GS) * l + (n - u) // GS + 1))
                need(dve, S.er_ready, N0 + n - 1)
                dve.tensor_scalar(S.hot_t[:, u % 2, :], S.loc_row[:, u, :], T.col[:, 0:1], None,
                                  ALU.is_equal).then_inc(S.hot_t_ready, 1)

            def logits(n, u):
                e = S.e[:, u % 2, :]
                need(dve, S.er_ready, N0 + n + 1)
                dve.tensor_reduce(S.er_e[:, :].rearrange("p (v h) -> p v h", h=HEADS).unsqueeze(3),
                                  S.er_ps[:, 0:BV * 3 * HEADS].rearrange("p (v k h) -> p v h k", k=3, h=HEADS),
                                  AX.X, ALU.add).then_inc(S.er_summed, 1)
                need(dve, S.er_summed, N0 + n + 1)
                need(dve, S.gathered[u], 16 * BV * ((NB // GS) * l + (n - u) // GS + 1))
                need(dve, S.max_t_ready, N0 + n - 1)
                el = S.rows[:, u, :, :].rearrange("p v (h k) -> p v h k", k=HD + 1)[:, :, :, HD]
                dve.tensor_tensor(S.pre[:, :].rearrange("p (v h) -> p v h", h=HEADS), el,
                                  S.er_e[:, :].rearrange("p (v h) -> p v h", h=HEADS), ALU.add).then_inc(S.pre_ready, 1)
                need(dve, S.pre_ready, N0 + n + 1)
                dve.scalar_tensor_tensor(e, S.pre[:, :], 0.2, S.pre[:, :], ALU.mult, ALU.max).then_inc(S.e_ready, 1)

            def maxima(n, u):
                m, b = S.fwd[:, u % 2, :], S.bwd[:, u % 2, :]
                first = isinstance(n, int) and n == 0
                need(dve, S.e_t_ready, N0 + n + 1)
                carry = S.fwd[:, 1 - u % 2, BE - 1:BE]
                dve.tensor_tensor_scan(m, S.flags[:, u, 0:BE], S.e_ps[0:HEADS, :], NEG if first else carry,
                                       ALU.add, ALU.max).then_inc(S.fwd_ready, 1)
                need(dve, S.fwd_ready, N0 + n + 1)
                need(dve, S.max_t_ready, N0 + n - 1)
                dve.tensor_tensor_scan(b[:, ::-1], S.flags[:, u, 1:BE + 1][:, ::-1], m[:, ::-1], NEG,
                                       ALU.add, ALU.max).then_inc(S.bwd_ready, 1)
                dve.tensor_scalar(S.goes_on[:, :], S.flags[:, u, 0:1], 0.0, None, ALU.is_equal).then_inc(S.flag_read, 1)
                need(dve, S.resc_ready, N0 + n)
                dve.tensor_tensor(S.hot0[:, :], T.row[0:HEADS, :], S.loc_row[0:HEADS, u, 0:1].to_broadcast([HEADS, P]),
                                  ALU.is_equal)
                need(dve, S.bwd_ready, N0 + n + 1)
                dve.tensor_tensor(S.drop[:, :], b[:, 0:1] if first else carry, b[:, 0:1],
                                  ALU.subtract).then_inc(S.drop_ready, 1)
                need(dve, S.drop_ready, N0 + n + 1)
                need(dve, S.flag_read, N0 + n + 1)
                dve.tensor_scalar(S.drop_diag[:, :], T.ident[0:HEADS, 0:HEADS], S.drop[:, :], S.goes_on[:, :],
                                  ALU.mult, ALU.mult).then_inc(S.resc_made, 1)

            def one_hot(n, u):
                need(dve, S.summed, BV * (N0 + n - 1))
                dve.tensor_tensor(S.hot[:, u % 2, :, :], T.row[:, :].unsqueeze(1).to_broadcast([P, BV, P]),
                                  T.loc_t[:, bass.ds(n * BV, BV)].unsqueeze(2).to_broadcast([P, BV, P]),
                                  ALU.is_equal).then_inc(S.hot_ready, 1)

            def below_max(n, u):
                need(dve, S.max_t_ready, N0 + n + 1)
                need(dve, S.resc_exp, N0 + n + 1)
                need(dve, S.weighted, N0 + n - 1)
                dve.tensor_tensor(S.below[:, u % 2, :], S.e[:, u % 2, :], S.max_ps[:, 0:BV * HEADS],
                                  ALU.subtract).then_inc(S.below_ready, 1)

            def window(d):
                return T.acc[:, bass.ds(d * ROW, ROW)]

            def add_up(n, u):
                for v in range(BV):
                    d = dve.value_load(T.win[0:1, bass.ds(n * BV + v, 1)], min_val=0, max_val=NT - 1)
                    need(dve, S.summed, BV * (N0 + n) + v + 1)
                    need(dve, S.added, (BV + 1) * (N0 + n) + v + 1)
                    dve.tensor_tensor(window(d), window(d), S.sum_ps[v % 4][:, 0:ROW], ALU.add).then_inc(S.added, 1)

            def rescale(n, u):
                d = dve.value_load(T.win[0:1, bass.ds(n * BV, 1)], min_val=0, max_val=NT - 1)
                need(dve, S.resc_exp, N0 + n + 1)
                need(dve, S.added, (BV + 1) * (N0 + n))
                dve.tensor_tensor(heads_of(window(d), HD + 1), heads_of(window(d), HD + 1),
                                  S.resc[:, u % 2, :].unsqueeze(2).to_broadcast([P, HEADS, HD + 1]),
                                  ALU.mult).then_inc(S.added, 1)

            def weigh(n, u):
                need(dve, S.exp_done, N0 + n + 1)
                r = S.rows[:, u, :, :].rearrange("p v (h k) -> p (v h) k", k=HD + 1)
                dve.tensor_tensor(r[:, :, 0:HD], r[:, :, 0:HD], r[:, :, HD:HD + 1].to_broadcast([P, BV * HEADS, HD]),
                                  ALU.mult).then_inc(S.weighted, 1)

            if l == 0:
                dve.wait_ge(S.acc_cleared, 1)
            else:
                dve.wait_ge(S.acc_cleared, l + 1)
            one_hot_t(0, 0)
            logits(0, 0)
            maxima(0, 0)

            def step(n, u):
                more = not isinstance(n, int) or n + 1 < NB
                nxt = (u + 1) % GS
                if more:
                    one_hot_t(n + 1, nxt)
                one_hot(n, u)
                below_max(n, u)
                if not isinstance(n, int) or n > 0:
                    add_up(n - 1, (u - 1) % GS)
                rescale(n, u)
                if more:
                    logits(n + 1, nxt)
                weigh(n, u)
                if more:
                    maxima(n + 1, nxt)
            steps(dve, NB, GS, step, tail=1)
            add_up(NB - 1, GS - 1)
            dve.wait_ge(S.added, (BV + 1) * (N0 + NB))

        @block.scalar
        def _(act):
            def step(n, u):
                need(act, S.below_ready, N0 + n + 1)
                w = S.rows[:, u, :, :].rearrange("p v (h k) -> p (v h) k", k=HD + 1)[:, :, HD]
                nc.scalar.activation(w, S.below[:, u % 2, :], ACT.Exp).then_inc(S.exp_done, 1)
                if not isinstance(n, int) or n + 1 < NB:
                    rescale(n + 1, (u + 1) % GS)

            def rescale(n, u):
                need(act, S.max_t_ready, N0 + n + 1)
                need(act, S.added, (BV + 1) * (N0 + n - 2) + 1)
                nc.scalar.activation(S.resc[:, u % 2, :], S.resc_ps[:, 64:64 + HEADS], ACT.Exp).then_inc(S.resc_exp, 1)

            rescale(0, 0)
            steps(act, NB, GS, step, tail=1)

        @block.tensor
        def _(pe):
            def er_by_edge(n, u):
                need(pe, S.er_summed, N0 + n)
                need(pe, S.hot_t_ready, N0 + n + 1)
                for v in range(BV):
                    d = pe.value_load(T.win[0:1, bass.ds(n * BV + v, 1)], min_val=0, max_val=NT - 1)
                    t = nc.tensor.matmul(S.er_ps[:, v * 3 * HEADS:(v + 1) * 3 * HEADS],
                                         S.hot_t[:, u % 2, v * P:(v + 1) * P],
                                         T.er3_flat[:, bass.ds(d * 3 * HEADS, 3 * HEADS)], start=True, stop=True)
                t.then_inc(S.er_ready, 1)

            def turn_logits(n, u):
                need(pe, S.fwd_ready, N0 + n)
                need(pe, S.e_ready, N0 + n + 1)
                for v in range(BV):
                    t = nc.tensor.transpose(S.e_ps[0:HEADS, v * P:(v + 1) * P],
                                            S.e[:, u % 2, v * HEADS:(v + 1) * HEADS], T.ident[:, :])
                t.then_inc(S.e_t_ready, 1)

            def turn_maxima(n, u):
                need(pe, S.below_ready, N0 + n)
                need(pe, S.resc_exp, N0 + n)
                need(pe, S.bwd_ready, N0 + n + 1)
                need(pe, S.resc_made, N0 + n + 1)
                nc.tensor.matmul(S.resc_ps[:, 64:64 + HEADS], S.hot0[:, :], S.drop_diag[:, :], start=True,
                                 stop=True).then_inc(S.resc_ready, 1)
                for v in range(BV):
                    t = nc.tensor.transpose(S.max_ps[:, v * HEADS:(v + 1) * HEADS],
                                            S.bwd[:, u % 2, v * P:(v + 1) * P], T.ident[0:HEADS, 0:HEADS])
                t.then_inc(S.max_t_ready, 1)

            def sum_up(n, u, v0, v1):
                if v0 == 0:
                    need(pe, S.hot_ready, N0 + n + 1)
                    need(pe, S.weighted, N0 + n + 1)
                for v in range(v0, v1):
                    need(pe, S.added, (BV + 1) * (N0 + n) + v - 4 + 2 if v >= 4 else (BV + 1) * (N0 + n - 1) + v + 4 + 2)
                    nc.tensor.matmul(S.sum_ps[v % 4][:, 0:ROW], S.hot[:, u % 2, v, :], S.rows[:, u, v, :],
                                     start=True, stop=True).then_inc(S.summed, 1)

            er_by_edge(0, 0)
            turn_logits(0, 0)
            turn_maxima(0, 0)

            def step(n, u):
                more = not isinstance(n, int) or n + 1 < NB
                before = not isinstance(n, int) or n > 0
                nxt, prv = (u + 1) % GS, (u - 1) % GS
                if before:
                    sum_up(n - 1, prv, 0, 4)
                if more:
                    er_by_edge(n + 1, nxt)
                if before:
                    sum_up(n - 1, prv, 4, BV)
                if more:
                    turn_logits(n + 1, nxt)
                    turn_maxima(n + 1, nxt)
            steps(pe, NB, GS, step, tail=1)
            sum_up(NB - 1, GS - 1, 0, BV)


class EdgeBuffers:
    def __init__(self, nc, ctx):
        def sb(name, shape, dt=F32):
            return ctx.enter_context(nc.sbuf_tensor(name, shape, dt))

        def ps(name, cols):
            return ctx.enter_context(nc.psum_tensor(name, [P, cols], F32))

        self.slots = GS = 4
        self.idx = sb("idx", [P, GS, BV], I32)
        self.rows = sb("g_rows", [P, GS, BV, ROW])
        self.loc_row = sb("loc_row", [P, GS, BE], BF16)
        self.flags = sb("flags", [HEADS, GS, BE + 1])
        self.hot_t = sb("hot_t", [P, 2, BE], BF16)
        self.hot = sb("hot", [P, 2, BV, P])
        self.er_e = sb("er_e", [P, BV * HEADS])
        self.pre = sb("pre", [P, BV * HEADS])
        self.e = sb("e", [P, 2, BV * HEADS])
        self.below = sb("below_m", [P, 2, BV * HEADS])
        self.fwd = sb("fwd", [HEADS, 2, BE])
        self.bwd = sb("bwd", [HEADS, 2, BE])
        self.goes_on = sb("goes_on", [HEADS, 1])
        self.drop = sb("drop", [HEADS, 1])
        self.drop_diag = sb("drop_diag", [HEADS, HEADS])
        self.hot0 = sb("hot0", [HEADS, P])
        self.resc = sb("resc", [P, 2, HEADS])
        self.e_ps = ps("e_ps", BE)
        self.er_ps = ps("er_ps", 512)
        self.max_ps = self.resc_ps = ps("max_ps", 512)
        self.sum_ps = [ps(f"sum_ps{i}", 512) for i in range(4)]

        def sem(name):
            return ctx.enter_context(nc.semaphore("e_" + name))

        self.acc_cleared = sem("acc_cleared")
        self.idx_ready = sem("idx_ready")
        self.issuing = sem("issuing")
        self.summed = sem("summed")
        self.hot_t_ready = sem("hot_t_ready")
        self.er_ready = sem("er_ready")
        self.er_summed = sem("er_summed")
        self.pre_ready = sem("pre_ready")
        self.e_ready = sem("e_ready")
        self.e_t_ready = sem("e_t_ready")
        self.fwd_ready = sem("fwd_ready")
        self.bwd_ready = sem("bwd_ready")
        self.flag_read = sem("flag_read")
        self.resc_ready = sem("resc_ready")
        self.drop_ready = sem("drop_ready")
        self.resc_made = sem("resc_made")
        self.hot_ready = sem("hot_ready")
        self.max_t_ready = sem("max_t_ready")
        self.below_ready = sem("below_ready")
        self.weighted = sem("weighted")
        self.exp_done = sem("exp_done")
        self.resc_exp = sem("resc_exp")
        self.added = sem("added")
        self.gathered = [ctx.enter_context(nc.semaphore(f"e_gathered{u}")) for u in range(GS)]
        self.tables = [ctx.enter_context(nc.semaphore(f"e_tables{u}")) for u in range(GS)]


def next_nodes(nc, T, S, l, bias):
    with ExitStack() as ctx:
        def sb(name, shape, dt=F32):
            return ctx.enter_context(nc.sbuf_tensor(f"u{l}_{name}", shape, dt))

        def sem(name):
            return ctx.enter_context(nc.semaphore(f"u{l}_{name}"))

        b_sb = sb("b", [P, FEAT])
        den = sb("den", [P, 2, HEADS])
        y = sb("y", [P, 2, FEAT])
        z = sb("z", [P, 2, FEAT])
        zt = sb("zt", [P, 2, FC, P])
        rows = sb("rows", [P, 2, ROW])
        tmp = sb("tmp", [P, NT, HEADS])
        zt_ps = [S.sum_ps[0], S.sum_ps[1]]
        row_ps = [S.sum_ps[2], S.sum_ps[3]]
        loaded, den1, den2, div, biased, leaky, turned, zt_done, row_done, row_out, er_done, split = map(sem, (
            "loaded", "den1", "den2", "div", "biased", "leaky", "turned", "zt", "row", "row_out", "er",
            "split"))
        stored = [sem("stored0"), sem("stored1")]
        with nc.Block() as block:
            @block.sync
            def _(sp):
                sp.dma_start(b_sb[:, :], bias[l:l + 1, :].to_broadcast([P, FEAT])).then_inc(loaded, 16)

                def step(n, u):
                    need(sp, row_out, n + 1)
                    sp.dma_start(T.rows_d[l + 1][bass.ds(n * P, P), :], rows[:, u, :]).then_inc(stored[u], 16)
                steps(sp, NT, 2, step)
                for u in range(2):
                    sp.wait_ge(stored[u], 16 * slot_total(NT, u, 2))

            @block.vector
            def _(dve):
                dve.wait_ge(loaded, 16)

                def step(n, u):
                    w = heads_of(T.acc[:, bass.ds(n * ROW, ROW)], HD + 1)
                    dve.tensor_scalar(den[:, u, :].unsqueeze(2), w[:, :, HD:HD + 1], 1e-30, None,
                                      ALU.max).then_inc(den1, 1)
                    need(dve, den1, n + 1)
                    dve.reciprocal(den[:, u, :], den[:, u, :]).then_inc(den2, 1)
                    need(dve, den2, n + 1)
                    dve.tensor_tensor(heads_of(y[:, u, :], HD), w[:, :, 0:HD],
                                      den[:, u, :].unsqueeze(2).to_broadcast([P, HEADS, HD]), ALU.mult).then_inc(div, 1)
                    need(dve, div, n + 1)
                    dve.tensor_tensor(y[:, u, :], y[:, u, :], b_sb[:, :], ALU.add).then_inc(biased, 1)
                    need(dve, biased, n + 1)
                    need(dve, turned, n - 1)
                    dve.scalar_tensor_tensor(z[:, u, :], y[:, u, :], 0.01, y[:, u, :], ALU.mult,
                                             ALU.max).then_inc(leaky, 1)
                steps(dve, NT, 2, step)
                dve.wait_ge(er_done, NT)
                split_er(dve, T, tmp[:, :, :], split, 0)

            @block.scalar
            def _(act):
                def step(n, u):
                    need(act, turned, n + 1)
                    need(act, row_done, n - 1)
                    nc.scalar.activation(zt[:, u, :, :].rearrange("p c n -> p (c n)"), zt_ps[u][:, 0:FEAT],
                                         ACT.Copy).then_inc(zt_done, 1)
                    need(act, row_done, n + 1)
                    need(act, stored[u], 16 * uses(n, u, 2))
                    nc.scalar.activation(rows[:, u, :], row_ps[u][:, 0:ROW], ACT.Copy).then_inc(row_out, 1)
                    nc.scalar.activation(T.er_flat[:, bass.ds(n * HEADS, HEADS)], row_ps[u][:, ROW:EXT],
                                         ACT.Copy).then_inc(er_done, 1)
                steps(act, NT, 2, step)

            @block.tensor
            def _(pe):
                def step(n, u):
                    turn(n, u)
                    if not isinstance(n, int) or n > 0:
                        row(n - 1, 1 - u)

                def turn(n, u):
                    need(pe, leaky, n + 1)
                    need(pe, zt_done, n - 1)
                    for c in range(FC):
                        t = nc.tensor.transpose(zt_ps[u][:, c * P:(c + 1) * P], z[:, u, c * P:(c + 1) * P],
                                                T.ident[:, :])
                    t.then_inc(turned, 1)

                def row(n, u):
                    need(pe, zt_done, n + 1)
                    need(pe, er_done, n - 1)
                    for c in range(FC):
                        t = nc.tensor.matmul(row_ps[u][:, 0:EXT], zt[:, u, c, :], T.wext[:, l + 1, c, :],
                                             start=(c == 0), stop=(c == FC - 1))
                    t.then_inc(row_done, 1)
                steps(pe, NT, 2, step)
                row(NT - 1, (NT - 1) % 2)

            @block.gpsimd
            def _(pool):
                pool.wait_ge(div, NT)
                pool.memset(T.acc[:, :], 0.0).then_inc(S.acc_cleared, 1)


def feed_forward(nc, T, bias, x, bout, router_t, w1, b1, w2, b2, out):
    with ExitStack() as ctx:
        def sb(name, shape, dt=F32):
            return ctx.enter_context(nc.sbuf_tensor("f_" + name, shape, dt))

        def sem(name):
            return ctx.enter_context(nc.semaphore("f_" + name))

        def ps(name):
            return ctx.enter_context(nc.psum_tensor("f_" + name + "_ps", [P, 512], F32))

        w1_sb = sb("w1", [P, EXPERTS, FC, FEAT])
        w2_sb = sb("w2", [P, EXPERTS, FC, FEAT])
        b1_sb = sb("b1", [P, EXPERTS, FC])
        b2_sb = sb("b2", [EXPERTS, FEAT])
        rt_sb = sb("rt", [P, FC, EXPERTS])
        bias_sb = sb("bias", [P, FEAT])
        bo_sb = sb("bo", [P, FEAT])
        xin = sb("x", [P, 2, FEAT])
        xt = sb("xt", [P, 2, FC, P])
        den = sb("den", [P, HEADS])
        x1 = sb("x1", [P, 2, FEAT])
        st = sb("st", [P, 6])
        mv = sb("mv", [P, 2])
        sd = sb("sd", [P, 2])
        tok = sb("tok", [P, 2, FEAT])
        tt = sb("tt", [P, 2, FC, P])
        neg = sb("neg", [P, 2])
        lg = sb("lg", [P, EXPERTS])
        prob = sb("prob", [P, EXPERTS])
        top = sb("top", [P, 8])
        top_i = sb("top_i", [P, 8], U32)
        top_f = sb("top_f", [P, 8])
        two = sb("two", [P, 2])
        pick = sb("pick", [P, EXPERTS])
        comb = sb("comb", [P, 2, EXPERTS])
        comb_t = sb("comb_t", [EXPERTS, P])
        hid = sb("hid", [P, 2, FC, P])
        res = sb("res", [P, 2, FEAT])
        mix_ps, turn_ps, lg_ps, b2_ps = ps("mix"), ps("turn"), ps("lg"), ps("b2")
        h_ps = [ps("h0"), ps("h1")]
        y_ps = [ps("y0"), ps("y1")]
        loaded, w_in, mixed, front, rooted, turned, tt_done, lg_done, exp_done, comb_done, comb_turned, comb_out, \
            b2_done, hidden, gelu, multiplied, added, begun, passed = map(sem, (
                "loaded", "w_in", "mixed", "front", "rooted", "turned", "tt", "lg", "exp", "comb", "comb_turned",
                "comb_out", "b2d", "hidden", "gelu", "mult", "added", "begun", "passed"))
        stored = [sem("stored0"), sem("stored1")]
        x_in = [sem("x_in0"), sem("x_in1")]
        K = 23

        with nc.Block() as block:
            @block.sync
            def _(sp):
                for dst, src in ((bias_sb[:, :], bias[LAYERS - 1:LAYERS, :].to_broadcast([P, FEAT])),
                                 (bo_sb[:, :], bout[None, :].to_broadcast([P, FEAT])),
                                 (rt_sb[:, :, :], router_t.rearrange("(c p) n -> p c n", p=P)),
                                 (b2_sb[:, :], b2)):
                    sp.dma_start(dst, src).then_inc(loaded, 16)
                with nc.allow_non_contiguous_dma(reason="a bias by partition"):
                    sp.dma_start(b1_sb[:, :, :], b1.rearrange("e (c p) -> p e c", p=P)).then_inc(loaded, 16)
                sp.dma_start(w1_sb[:, :, :, :], w1.rearrange("e (c p) n -> p e c n", p=P)).then_inc(w_in, 16)
                sp.dma_start(w2_sb[:, :, :, :], w2.rearrange("e (c p) n -> p e c n", p=P)).then_inc(w_in, 16)

                def step(n, u):
                    need(sp, front, K * (n - 1))
                    sp.dma_start(xin[:, u, :], x[bass.ds(n * P, P), :]).then_inc(x_in[u], 16)
                    sp.dma_start(xt[:, u, :, :].rearrange("p c n -> p (c n)"), T.xt_d[bass.ds(n * P, P), :]
                                 ).then_inc(x_in[u], 16)
                steps(sp, NT, 2, step)

            @block.gpsimd
            def _(pool):
                def step(n, u):
                    need(pool, added, EXPERTS * (n + 1))
                    k = NODES - (NT - 1) * P if isinstance(n, int) and n == NT - 1 else P
                    pool.dma_start(out[bass.ds(n * P, k), :], res[0:k, u, :]).then_inc(stored[u], 16)
                steps(pool, NT, 2, step, tail=1)
                for u in range(2):
                    pool.wait_ge(stored[u], 16 * slot_total(NT, u, 2))

            @block.vector
            def _(dve):
                def before(n, u):
                    k = [0]

                    def link(ins, carry=False):
                        k[0] += 1
                        ins.then_inc(front, 1)
                        dve.wait_ge(front, K * n + k[0])
                        if carry:
                            dve.sem_inc(passed, 1)

                    w = heads_of(T.acc[:, bass.ds(n * ROW, ROW)], HD + 1)
                    y = x1[:, u, :]
                    link(dve.tensor_scalar(den[:, :].unsqueeze(2), w[:, :, HD:HD + 1], 1e-30, None, ALU.max))
                    link(dve.reciprocal(den[:, :], den[:, :]))
                    link(dve.tensor_tensor(heads_of(y, HD), w[:, :, 0:HD],
                                           den[:, :].unsqueeze(2).to_broadcast([P, HEADS, HD]), ALU.mult))
                    link(dve.tensor_tensor(y, y, bias_sb[:, :], ALU.add))
                    need(dve, x_in[u], ((n - u) // 2) * 32 + 32)
                    link(dve.tensor_tensor(y, y, xin[:, u, :], ALU.add))
                    need(dve, mixed, n + 1)
                    link(dve.tensor_tensor(y, y, mix_ps[:, 0:FEAT], ALU.add))
                    link(dve.tensor_tensor(y, y, bo_sb[:, :], ALU.add))
                    link(dve.bn_stats(st[:, :], y), carry=True)
                    link(dve.bn_aggr(mv[:, :], st[:, :]))
                    link(dve.tensor_scalar(sd[:, 0:1], mv[:, 1:2], EPS, None, ALU.add))
                    assert k[0] == 10
                    need(dve, rooted, n + 1)
                    link(dve.reciprocal(sd[:, 1:2], sd[:, 1:2]))
                    link(dve.tensor_scalar(tok[:, u, :], y, mv[:, 0:1], sd[:, 1:2], ALU.subtract, ALU.mult))
                    assert k[0] == 12
                    need(dve, lg_done, n + 1)
                    link(dve.tensor_reduce(neg[:, 0:1], lg_ps[:, 0:EXPERTS], AX.X, ALU.max, negate=True))
                    assert k[0] == 13
                    need(dve, exp_done, n + 1)
                    link(dve.reciprocal(neg[:, 1:2], neg[:, 1:2]))
                    link(dve.tensor_scalar(prob[:, :], lg[:, :], neg[:, 1:2], None, ALU.mult), carry=True)
                    link(dve.max(top[:, :], prob[:, :]), carry=True)
                    link(dve.max_index(top_i[:, :], top[:, :], prob[:, :]))
                    link(dve.tensor_copy(top_f[:, :], top_i[:, :]))
                    link(dve.tensor_scalar(two[:, 0:1], top[:, 0:1], top[:, 1:2], 1e-12, ALU.add, ALU.max))
                    link(dve.reciprocal(two[:, 1:2], two[:, 0:1]))
                    link(dve.tensor_scalar(top[:, 0:2], top[:, 0:2], two[:, 1:2], None, ALU.mult))
                    link(dve.tensor_scalar(pick[:, :], T.row[:, 0:EXPERTS], top_f[:, 0:1], top[:, 0:1],
                                           ALU.is_equal, ALU.mult))
                    link(dve.tensor_scalar(comb[:, u, :], T.row[:, 0:EXPERTS], top_f[:, 1:2], top[:, 1:2],
                                           ALU.is_equal, ALU.mult))
                    assert k[0] == K
                    dve.tensor_tensor(comb[:, u, :], comb[:, u, :], pick[:, :], ALU.add).then_inc(comb_done, 1)

                def begin(n, u):
                    need(dve, b2_done, n + 1)
                    need(dve, stored[u], 16 * uses(n, u, 2))
                    dve.tensor_tensor(res[:, u, :], x1[:, u, :], tok[:, u, :], ALU.add).then_inc(begun, 1)
                    need(dve, begun, 2 * n + 1)
                    dve.tensor_tensor(res[:, u, :], res[:, u, :], b2_ps[:, 0:FEAT], ALU.add).then_inc(begun, 1)

                def expert(n, u, e):
                    need(dve, multiplied, EXPERTS * n + e + 1)
                    if e == 0:
                        need(dve, begun, 2 * n + 2)
                    else:
                        need(dve, added, EXPERTS * n + e)
                    dve.scalar_tensor_tensor(res[:, u, :], y_ps[e % 2][:, 0:FEAT], comb[:, u, e:e + 1], res[:, u, :],
                                             ALU.mult, ALU.add).then_inc(added, 1)

                dve.wait_ge(loaded, 80)
                before(0, 0)

                def step(n, u):
                    begin(n, u)
                    for e in range(4):
                        expert(n, u, e)
                    if not isinstance(n, int) or n + 1 < NT:
                        before(n + 1, 1 - u)
                    for e in range(4, EXPERTS):
                        expert(n, u, e)
                steps(dve, NT, 2, step, tail=1)

            @block.scalar
            def _(act):
                def before(n, u):
                    need(act, front, K * n + 10)
                    nc.scalar.activation(sd[:, 1:2], sd[:, 0:1], ACT.Sqrt).then_inc(rooted, 1)
                    need(act, turned, n + 1)
                    nc.scalar.activation(tt[:, u, :, :].rearrange("p c n -> p (c n)"), turn_ps[:, 0:FEAT],
                                         ACT.Copy).then_inc(tt_done, 1)
                    need(act, front, K * n + 13)
                    nc.scalar.activation(lg[:, :], lg_ps[:, 0:EXPERTS], ACT.Exp, bias=neg[:, 0:1],
                                         accum_out=neg[:, 1:2]).then_inc(exp_done, 1)
                    need(act, comb_turned, n + 1)
                    nc.scalar.activation(comb_t[:, :], turn_ps[0:EXPERTS, FEAT:FEAT + P], ACT.Copy).then_inc(comb_out, 1)

                def expert(n, u, e):
                    k = EXPERTS * n + e
                    for j in range(FC):
                        need(act, hidden, 2 * k + j + 1)
                        if j == 0:
                            need(act, multiplied, k - 1)
                        nc.scalar.activation(hid[:, e % 2, j, :], h_ps[j][:, 0:P], ACT.Gelu,
                                             bias=b1_sb[:, e, j:j + 1]).then_inc(gelu, 1)

                act.wait_ge(loaded, 80)
                before(0, 0)

                def step(n, u):
                    for e in range(4):
                        expert(n, u, e)
                    if not isinstance(n, int) or n + 1 < NT:
                        before(n + 1, 1 - u)
                    for e in range(4, EXPERTS):
                        expert(n, u, e)
                steps(act, NT, 2, step, tail=1)

            @block.tensor
            def _(pe):
                def before(n, u):
                    need(pe, x_in[u], ((n - u) // 2) * 32 + 32)
                    need(pe, front, K * n)
                    for c in range(FC):
                        t = nc.tensor.matmul(mix_ps[:, 0:FEAT], xt[:, u, c, :], T.mixw[:, c, :],
                                             start=(c == 0), stop=(c == FC - 1))
                    t.then_inc(mixed, 1)
                    need(pe, front, K * n + 12)
                    need(pe, comb_out, n)
                    for c in range(FC):
                        t = nc.tensor.transpose(turn_ps[:, c * P:(c + 1) * P], tok[:, u, c * P:(c + 1) * P],
                                                T.ident[:, :])
                    t.then_inc(turned, 1)
                    need(pe, tt_done, n + 1)
                    for c in range(FC):
                        t = nc.tensor.matmul(lg_ps[:, 0:EXPERTS], tt[:, u, c, :], rt_sb[:, c, :],
                                             start=(c == 0), stop=(c == FC - 1))
                    t.then_inc(lg_done, 1)
                    need(pe, comb_done, n + 1)
                    nc.tensor.transpose(turn_ps[0:EXPERTS, FEAT:FEAT + P], comb[:, u, :],
                                        T.ident[:, :]).then_inc(comb_turned, 1)
                    need(pe, comb_out, n + 1)
                    need(pe, begun, 2 * n)
                    nc.tensor.matmul(b2_ps[:, 0:FEAT], comb_t[:, :], b2_sb[:, :], start=True,
                                     stop=True).then_inc(b2_done, 1)

                def expand(n, u, e):
                    k = EXPERTS * n + e
                    for j in range(FC):
                        need(pe, gelu, 2 * (k - 1) + j + 1)
                        for c in range(FC):
                            t = nc.tensor.matmul(h_ps[j][:, 0:P], w1_sb[:, e, c, j * P:(j + 1) * P], tt[:, u, c, :],
                                                 start=(c == 0), stop=(c == FC - 1))
                        t.then_inc(hidden, 1)

                def contract(n, u, e):
                    k = EXPERTS * n + e
                    need(pe, gelu, 2 * k + 2)
                    need(pe, added, k - 1)
                    for j in range(FC):
                        t = nc.tensor.matmul(y_ps[e % 2][:, 0:FEAT], hid[:, e % 2, j, :], w2_sb[:, e, j, :],
                                             start=(j == 0), stop=(j == FC - 1))
                    t.then_inc(multiplied, 1)

                pe.wait_ge(loaded, 80)
                before(0, 0)
                pe.wait_ge(w_in, 32)

                def step(n, u):
                    for e in range(4):
                        expand(n, u, e)
                        if e > 0:
                            contract(n, u, e - 1)
                    contract(n, u, 3)
                    if not isinstance(n, int) or n + 1 < NT:
                        before(n + 1, 1 - u)
                    for e in range(4, EXPERTS):
                        expand(n, u, e)
                        if e > 4:
                            contract(n, u, e - 1)
                    contract(n, u, EXPERTS - 1)
                steps(pe, NT, 2, step, tail=1)


class Shared:
    pass


def program(nc, x, src_tiles, dst_tiles, dst_last, W, al, ar, b, wkv_t, wq, wo_t, bout, router_t, w1, b1, w2, b2,
            out):
    T = Shared()
    T.rows_d = [nc.dram_tensor(f"rows{l}_d", (NODES_PAD, ROW), F32, kind="Internal").ap() for l in range(LAYERS)]
    T.xt_d = nc.dram_tensor("xt_d", (NODES_PAD, FEAT), F32, kind="Internal").ap()
    T.loc_d = nc.dram_tensor("loc_d", (VP * P,), BF16, kind="Internal").ap()
    T.flag_d = nc.dram_tensor("flag_d", (VP * P + 8,), F32, kind="Internal").ap()
    T.key_d = nc.dram_tensor("key_d", (VP * P + 8,), F32, kind="Internal").ap()
    T.win_d = nc.dram_tensor("win_d", (VP,), I32, kind="Internal").ap()
    with ExitStack() as ctx:
        def sb(name, shape, dt=F32):
            return ctx.enter_context(nc.sbuf_tensor(name, shape, dt))

        T.ident = sb("ident", [P, P])
        T.row = sb("row", [P, P])
        T.col = sb("col", [P, 1])
        T.wext = sb("wext", [P, LAYERS, FC, EXT])
        T.mixw = sb("mixw", [P, FC, FEAT])
        T.er = sb("er", [P, NT, HEADS])
        T.er_flat = T.er[:, :, :].rearrange("p t h -> p (t h)")
        T.er3 = sb("er3", [P, NT, 3, HEADS], BF16)
        T.er3_flat = T.er3[:, :, :, :].rearrange("p t k h -> p (t k h)")
        T.src_t = sb("src_t", [P, VP], I32)
        T.loc_t = sb("loc_t", [P, VP])
        T.win = sb("win", [1, VP], I32)
        constants(nc, T)
        edge_tables(nc, T, dst_last, src_tiles, dst_tiles)
        with ExitStack() as early:
            T.wkv = early.enter_context(nc.sbuf_tensor("wkv", [P, FC, 2 * INNER], F32))
            T.dots = early.enter_context(nc.sbuf_tensor("dots", [P, PAIRS * P], F32))
            weights(nc, T, W, al, ar, wkv_t)
            first_nodes(nc, T, x)
            mix_matrix(nc, T, wq, wo_t)
        T.acc = sb("acc", [P, NT * ROW])
        with ExitStack() as mid:
            S = EdgeBuffers(nc, mid)
            for l in range(LAYERS):
                edge_pass(nc, T, S, l)
                if l + 1 < LAYERS:
                    next_nodes(nc, T, S, l, b)
        feed_forward(nc, T, b, x, bout, router_t, w1, b1, w2, b2, out)


def kernel(x, src, dst, L0_gnn_W, L0_gnn_al, L0_gnn_ar, L0_gnn_b, L0_mix_Wqkv, L0_mix_Wout, L0_mix_bout,
           L0_ffn_router_w, L0_ffn_w1, L0_ffn_b1, L0_ffn_w2, L0_ffn_b2):
    import numpy as np
    import concourse.bacc as bacc
    from concourse.bass_utils import run_bass_kernel_spmd

    def laid(a):
        return np.ascontiguousarray(a)

    x, src, dst = np.asarray(x), np.asarray(src), np.asarray(dst)
    x_pad = np.zeros((NODES_PAD, FEAT), x.dtype)
    x_pad[:NODES] = x
    src_tiles = np.zeros((TILES * P,), src.dtype)
    src_tiles[:EDGES] = src
    dst_tiles = np.full((TILES * P,), NODES_PAD - 1, dst.dtype)
    dst_tiles[:EDGES] = dst
    src_tiles, dst_tiles = src_tiles.reshape(TILES, P), dst_tiles.reshape(TILES, P)
    wqkv = np.asarray(L0_mix_Wqkv)
    ins = {
        "x": x_pad, "src_tiles": src_tiles, "dst_tiles": dst_tiles, "dst_last": laid(dst_tiles[:, P - 1]),
        "W": laid(L0_gnn_W), "al": laid(L0_gnn_al), "ar": laid(L0_gnn_ar), "b": laid(L0_gnn_b),
        "wkv_t": laid(wqkv[INNER:].T), "wq": laid(wqkv[:INNER]), "wo_t": laid(np.asarray(L0_mix_Wout).T),
        "bout": laid(L0_mix_bout), "router_t": laid(np.asarray(L0_ffn_router_w).T),
        "w1": laid(L0_ffn_w1), "b1": laid(L0_ffn_b1), "w2": laid(L0_ffn_w2), "b2": laid(L0_ffn_b2),
    }
    nc = bacc.Bacc("TRN2", target_bir_lowering=False, num_devices=1)
    arrays = {f"in_{k}": a for k, a in ins.items()}
    args = {k: nc.dram_tensor(f"in_{k}", a.shape, mybir.dt.from_np(a.dtype), kind="ExternalInput").ap()
            for k, a in ins.items()}
    out = nc.dram_tensor("out", (NODES, FEAT), F32, kind="ExternalOutput").ap()
    program(nc, out=out, **args)
    r = run_bass_kernel_spmd(nc, [arrays], core_ids=[0])
    return r.results[0]["out"]
```

```python
import concourse.bass as bass
from concourse import mybir
from contextlib import ExitStack

F32 = mybir.dt.float32
BF16 = mybir.dt.bfloat16
I32 = mybir.dt.int32
U32 = mybir.dt.uint32
ALU = mybir.AluOpType
ACT = mybir.ActivationFunctionType
AX = mybir.AxisListType

P = 128
NODES, FEAT = 6250, 256
EDGES = 2 * 100000 + NODES
HEADS, HD = 8, 32
LAYERS = 3
FC = FEAT // P
NT = -(-NODES // P)
NODES_PAD = NT * P
ET = -(-EDGES // P)
BT = 6
BE = BT * P
SLOTS = 6
NB = -(-(-(-ET // BT) + NT - 1) // SLOTS) * SLOTS
GROUPS = NB - NT + 1
CH = -(-NB // P)
VP = CH * P
ROW = HEADS * (HD + 1)
EXT = ROW + HEADS
NEG = -1.0e30
EPS = 1e-5
MH, MD = 8, 64
INNER = MH * MD
PAIRS = INNER // P
EXPERTS = 8


def need(eng, sem, count):
    if not isinstance(count, int) or count > 0:
        eng.wait_ge(sem, count)


def steps(eng, total, unroll, step, tail=0):
    for n in range(unroll):
        step(n, n)
    rounds = (total - tail) // unroll
    with eng.Fori(1, rounds) as i:
        for u in range(unroll):
            step(i * unroll + u, u)
    for n in range(rounds * unroll, total):
        step(n, n % unroll)


def uses(n, slot, slots):
    return (n - slot) // slots


def slot_total(total, slot, slots):
    return (total - 1 - slot) // slots + 1


def heads_of(ap, width):
    return ap.rearrange("p (h k) -> p h k", k=width)


def constants(nc, T):
    with ExitStack() as ctx:
        made = ctx.enter_context(nc.semaphore("const_made"))
        with nc.Block() as block:
            @block.gpsimd
            def _(pool):
                pool.memset(T.ident[:, :], 0.0).then_inc(made, 1)
                pool.wait_ge(made, 1)
                pool.affine_select(out=T.ident[:, :], in_=T.ident[:, :], compare_op=ALU.not_equal, fill=1.0,
                                   base=0, pattern=[[-1, P]], channel_multiplier=1).then_inc(made, 1)
                pool.iota(T.row[:, :], pattern=[[1, P]], base=0, channel_multiplier=0,
                          allow_small_or_imprecise_dtypes=True).then_inc(made, 1)
                pool.iota(T.col[:, :], pattern=[[0, 1]], base=0, channel_multiplier=1,
                          allow_small_or_imprecise_dtypes=True).then_inc(made, 1)
                pool.memset(T.one[:, :], 1.0).then_inc(made, 1)
                pool.wait_ge(made, 5)


def edge_tables(nc, T, dst_last, src_groups, dst_groups):
    with ExitStack() as ctx:
        def sb(name, shape, dt=F32):
            return ctx.enter_context(nc.sbuf_tensor(name, shape, dt))

        def sem(name):
            return ctx.enter_context(nc.semaphore(name))

        last = sb("last", [P, GROUPS], I32)
        group_no = sb("group_no", [P, GROUPS], I32)
        path = sb("path", [P, GROUPS])
        below = sb("below", [P, GROUPS])
        visit_i = sb("visit_i", [P, CH], I32)
        visit = sb("visit", [P, CH])
        group_of = sb("group_of", [P, CH])
        group_idx = sb("group_idx", [P, CH], I32)
        win_of = sb("win_of", [P, CH])
        win_i = sb("win_i", [P, CH], I32)
        win_base = sb("win_base", [P, CH])
        src_v = sb("src_v", [P, CH, BE], I32)
        dst_v = sb("dst_v", [P, CH, BE], I32)
        src_f = sb("src_f", [P, CH, BE])
        loc = sb("loc", [P, CH, BE])
        inside = sb("inside", [P, CH, BE])
        locm = sb("locm", [P, CH, BE])
        locb = sb("locb", [P, CH, BE], BF16)
        key = sb("key", [P, CH, BE])
        prev = sb("prev", [P, CH, BE])
        edge = sb("edge", [1, 8])
        banks = [ctx.enter_context(nc.psum_tensor(f"tp{i}", [P, 512], F32)) for i in range(8)]
        loaded, iotas, step, gathered, turned, evacuated, stored, shifted, dtab = map(sem, (
            "tab_loaded", "tab_iotas", "tab_step", "tab_gathered", "tab_turned", "tab_evacuated",
            "tab_stored", "tab_shifted", "tab_dtab"))
        done = {}
        blocks = [(j, c) for j in range(BT) for c in range(CH)]
        lots = [(w, blocks[i:i + 4]) for w in range(2) for i in range(0, len(blocks), 4)]

        with nc.Block() as block:
            @block.vector
            def _(dve):
                count = [0]

                def link(ins, name=None):
                    count[0] += 1
                    ins.then_inc(step, 1)
                    dve.wait_ge(step, count[0])
                    if name:
                        done[name] = count[0]

                dve.wait_ge(loaded, 16)
                link(dve.tensor_scalar(last[:, :], last[:, :], 7, None, ALU.arith_shift_right))
                dve.wait_ge(iotas, 2)
                link(dve.tensor_tensor(path[:, :], last[:, :], group_no[:, :], ALU.add))
                link(dve.tensor_copy(visit[:, :], visit_i[:, :]))
                for c in range(CH):
                    link(dve.tensor_scalar(below[:, :], path[:, :], visit[:, c:c + 1], None, ALU.is_lt, ALU.add,
                                           accum_out=group_of[:, c:c + 1]))
                link(dve.tensor_tensor(win_of[:, :], visit[:, :], group_of[:, :], ALU.subtract))
                link(dve.tensor_scalar(group_of[:, :], group_of[:, :], float(GROUPS - 1), None, ALU.min))
                link(dve.tensor_scalar(win_of[:, :], win_of[:, :], float(NT - 1), None, ALU.min))
                link(dve.tensor_copy(group_idx[:, :], group_of[:, :]), "group_idx")
                link(dve.tensor_copy(win_i[:, :], win_of[:, :]), "win")
                link(dve.tensor_scalar(win_base[:, :], win_of[:, :], -float(P), None, ALU.mult))
                link(dve.memset(edge[:, 0:1], -2.0))
                link(dve.memset(edge[:, 1:8], 0.0), "edge")
                dve.wait_ge(gathered, 2 * CH * 16)
                link(dve.tensor_copy(src_f[:, :, :], src_v[:, :, :]), "src_f")
                for c in range(CH):
                    link(dve.tensor_scalar(loc[:, c, :], dst_v[:, c, :], win_base[:, c:c + 1], None, ALU.add))
                link(dve.tensor_scalar(inside[:, :, :], loc[:, :, :], 0.0, None, ALU.is_ge))
                link(dve.scalar_tensor_tensor(inside[:, :, :], loc[:, :, :], float(P - 1), inside[:, :, :],
                                              ALU.is_le, ALU.mult))
                link(dve.scalar_tensor_tensor(locm[:, :, :], loc[:, :, :], 1.0, inside[:, :, :], ALU.add, ALU.mult))
                link(dve.tensor_scalar(locm[:, :, :], locm[:, :, :], -1.0, None, ALU.add), "locm")
                link(dve.tensor_copy(locb[:, :, :], locm[:, :, :]), "locb")
                link(dve.scalar_tensor_tensor(key[:, :, :], dst_v[:, :, :], 1.0, inside[:, :, :], ALU.add, ALU.mult))
                link(dve.tensor_scalar(key[:, :, :], key[:, :, :], -1.0, None, ALU.add), "key")
                dve.wait_ge(shifted, 16)
                link(dve.tensor_tensor(prev[:, :, :], key[:, :, :], prev[:, :, :], ALU.not_equal))
                link(dve.tensor_scalar(prev[:, :, :], prev[:, :, :], NEG, None, ALU.mult), "flag")

            @block.gpsimd
            def _(pool):
                pool.iota(group_no[:, :], pattern=[[1, GROUPS]], base=0, channel_multiplier=0).then_inc(iotas, 1)
                pool.iota(visit_i[:, :], pattern=[[P, CH]], base=0, channel_multiplier=1).then_inc(iotas, 1)
                pool.wait_ge(step, done["group_idx"])
                for c in range(CH):
                    for table, rows in ((src_v, src_groups), (dst_v, dst_groups)):
                        pool.indirect_dma_start(
                            table[:, c, :], None, rows,
                            bass.IndirectOffsetOnAxis(ap=group_idx[:, c:c + 1].bitcast(U32), axis=0),
                        ).then_inc(gathered, 16)

            @block.tensor
            def _(pe):
                for i, (w, lot) in enumerate(lots):
                    pe.wait_ge(step, done["locm" if w else "src_f"])
                    if i >= 8:
                        pe.wait_ge(evacuated, sum(len(lot) for _, lot in lots[:i - 7]))
                    for k, (j, c) in enumerate(lot):
                        t = nc.tensor.transpose(banks[i % 8][:, k * P:(k + 1) * P],
                                                (locm if w else src_f)[:, c, j * P:(j + 1) * P], T.ident[:, :])
                    t.then_inc(turned, 1)

            @block.scalar
            def _(act):
                for i, (w, lot) in enumerate(lots):
                    act.wait_ge(turned, i + 1)
                    for k, (j, c) in enumerate(lot):
                        out = (T.neg_loc if w else T.src_t)[:, c * P:(c + 1) * P, j]
                        nc.scalar.activation(out, banks[i % 8][:, k * P:(k + 1) * P], ACT.Copy,
                                             scale=-1.0 if w else 1.0).then_inc(evacuated, 1)

            @block.sync
            def _(sp):
                by_visit = "(c p e) -> p c e"
                sp.dma_start(last[:, :], dst_last[None, :].to_broadcast([P, GROUPS])).then_inc(loaded, 16)
                sp.wait_ge(step, done["win"])
                with nc.allow_non_contiguous_dma(reason="a table of one word per visit"):
                    sp.dma_start(T.win_d[:].rearrange("(c p) -> p c", p=P), win_i[:, :]).then_inc(dtab, 16)
                sp.wait_ge(dtab, 16)
                sp.dma_start(T.win[0:1, :], T.win_d[:][None, :]).then_inc(dtab, 16)
                sp.wait_ge(step, done["edge"])
                sp.dma_start(T.key_d[0:1][None, :], edge[0:1, 0:1]).then_inc(stored, 16)
                sp.dma_start(T.flag_d[VP * BE:VP * BE + 7][None, :], edge[0:1, 1:8]).then_inc(stored, 16)
                sp.wait_ge(step, done["locb"])
                sp.dma_start(T.loc_d[:].rearrange(by_visit, p=P, e=BE), locb[:, :, :]).then_inc(stored, 16)
                sp.wait_ge(step, done["key"])
                sp.dma_start(T.key_d[1:1 + VP * BE].rearrange(by_visit, p=P, e=BE), key[:, :, :]).then_inc(stored, 16)
                sp.wait_ge(stored, 64)
                sp.dma_start(prev[:, :, :], T.key_d[0:VP * BE].rearrange(by_visit, p=P, e=BE)).then_inc(shifted, 16)
                sp.wait_ge(step, done["flag"])
                sp.dma_start(T.flag_d[0:VP * BE].rearrange(by_visit, p=P, e=BE), prev[:, :, :]).then_inc(stored, 16)
                sp.wait_ge(stored, 80)
                sp.wait_ge(dtab, 32)
                sp.wait_ge(evacuated, 2 * len(blocks))


def split_er(dve, T, tmp, sem, base):
    k = [base]

    def link(ins):
        k[0] += 1
        ins.then_inc(sem, 1)
        dve.wait_ge(sem, k[0])

    link(dve.tensor_copy(T.er3[:, :, 0, :], T.er[:, :, :]))
    link(dve.tensor_tensor(tmp, T.er[:, :, :], T.er3[:, :, 0, :], ALU.subtract))
    link(dve.tensor_copy(T.er3[:, :, 1, :], tmp))
    link(dve.tensor_tensor(tmp, tmp, T.er3[:, :, 1, :], ALU.subtract))
    link(dve.tensor_copy(T.er3[:, :, 2, :], tmp))


def weights(nc, T, W, al, ar, wkv_t):
    with ExitStack() as ctx:
        def sb(name, shape, dt=F32):
            return ctx.enter_context(nc.sbuf_tensor(name, shape, dt))

        w_in = sb("w_in", [P, LAYERS, FC, FEAT])
        a_in = sb("a_in", [P, 2, LAYERS, FEAT])
        prod = sb("prod", [P, FC, FEAT])
        mean = sb("mean", [P, FC, 2 * MH])
        loaded = ctx.enter_context(nc.semaphore("w_loaded"))
        step = ctx.enter_context(nc.semaphore("w_step"))
        with nc.Block() as block:
            @block.sync
            def _(sp):
                sp.dma_start(w_in[:, :, :, :], W.rearrange("l (c p) n -> p l c n", p=P)).then_inc(loaded, 16)
                for j, a in enumerate((al, ar)):
                    sp.dma_start(a_in[:, j, :, :], a.rearrange("l h d -> l (h d)")[None, :, :]
                                 .to_broadcast([P, LAYERS, FEAT])).then_inc(loaded, 16)
                sp.dma_start(T.wkv[:, :, :], wkv_t.rearrange("(c p) n -> p c n", p=P)).then_inc(loaded, 16)

            @block.vector
            def _(dve):
                n = [0]

                def link(ins):
                    n[0] += 1
                    ins.then_inc(step, 1)
                    dve.wait_ge(step, n[0])

                dve.wait_ge(loaded, 64)
                for l in range(LAYERS):
                    for c in range(FC):
                        w = T.wext[:, l, c, 0:ROW].rearrange("p (h k) -> p h k", k=HD + 1)
                        link(dve.tensor_copy(w[:, :, 0:HD], heads_of(w_in[:, l, c, :], HD)))
                        for j, out in ((0, w[:, :, HD:HD + 1]), (1, T.wext[:, l, c, ROW:EXT].unsqueeze(2))):
                            link(dve.tensor_tensor(prod[:, c, :], w_in[:, l, c, :], a_in[:, j, l, :], ALU.mult))
                            link(dve.tensor_reduce(out, heads_of(prod[:, c, :], HD), AX.X, ALU.add))
                wk = T.wkv[:, :, :].rearrange("p c (h d) -> p c h d", d=MD)
                link(dve.tensor_reduce(mean[:, :, :].unsqueeze(3), wk, AX.X, ALU.add))
                link(dve.tensor_scalar(mean[:, :, :], mean[:, :, :], 1.0 / MD, None, ALU.mult))
                for c in range(FC):
                    link(dve.tensor_tensor(wk[:, c], wk[:, c], mean[:, c, :].unsqueeze(2)
                                           .to_broadcast([P, 2 * MH, MD]), ALU.subtract))


def first_nodes(nc, T, x):
    with ExitStack() as ctx:
        def sb(name, shape, dt=F32):
            return ctx.enter_context(nc.sbuf_tensor(name, shape, dt))

        def sem(name):
            return ctx.enter_context(nc.semaphore(name))

        def ps(name, shape):
            return ctx.enter_context(nc.psum_tensor(name, shape, F32))

        S = 2
        xs = sb("xs", [P, S, FEAT])
        st = sb("st", [P, S, 6])
        mv = sb("mv", [P, S, 2])
        sd = sb("sd", [P, S, 2])
        xn = sb("xn", [P, S, FEAT])
        xt = sb("xt", [P, S, FC, P])
        rows = sb("rows", [P, S, ROW])
        kc = sb("kc", [P, S, INNER])
        vc = sb("vc", [P, S, INNER])
        sq = sb("sq", [P, S, 2 * INNER])
        var = sb("var", [P, S, 2 * MH])
        dev = sb("dev", [P, S, 2 * MH])
        wt = sb("wt", [P, S, MH])
        tmp = sb("tmp", [P, NT, HEADS])
        xt_ps = ps("xt_ps", [P, FC * P])
        kv_ps = [ps("k_ps", [P, INNER]), ps("v_ps", [P, INNER])]
        row_ps = ps("row_ps", [P, EXT])
        dot_ps = ps("dot_ps", [P, PAIRS * P])
        x_in = [sem(f"n_x_in{u}") for u in range(S)]
        row_stored = [sem(f"n_row_stored{u}") for u in range(S)]
        xt_stored = [sem(f"n_xt_stored{u}") for u in range(S)]
        stat, var_eps, rooted, inv, xn_done, turned, xt_done, kv_done, row_done, row_out, er_done, \
            squared, k_out, sums, sums2, rooted2, inv2, wt_done, v_done, dots, added, split, passed = map(sem, (
                "n_stat", "n_var_eps", "n_rooted", "n_inv", "n_xn", "n_turned", "n_xt", "n_kv", "n_row",
                "n_row_out", "n_er", "n_squared", "n_k_out", "n_sums", "n_sums2",
                "n_rooted2", "n_inv2", "n_wt", "n_v", "n_dots", "n_added", "n_split", "n_passed"))

        with nc.Block() as block:
            @block.sync
            def _(sp):
                def step(n, u):
                    need(sp, xn_done, n - 1)
                    sp.dma_start(xs[:, u, :], x[bass.ds(n * P, P), :]).then_inc(x_in[u], 16)
                steps(sp, NT, S, step)

            @block.gpsimd
            def _(pool):
                def step(n, u):
                    need(pool, xt_done, n + 1)
                    pool.dma_start(T.xt_d[bass.ds(n * P, P), :], xt[:, u, :, :].rearrange("p c n -> p (c n)")
                                   ).then_inc(xt_stored[u], 16)
                    need(pool, row_out, n + 1)
                    pool.dma_start(T.rows_d[0][bass.ds(n * P, P), :], rows[:, u, :]).then_inc(row_stored[u], 16)
                steps(pool, NT, S, step)
                for u in range(S):
                    pool.wait_ge(xt_stored[u], 16 * slot_total(NT, u, S))
                    pool.wait_ge(row_stored[u], 16 * slot_total(NT, u, S))

            @block.vector
            def _(dve):
                def norm(n, u):
                    need(dve, x_in[u], (n // 2 if isinstance(n, int) else (n - u) // 2) * 16 + 16)
                    dve.bn_stats(st[:, u, :], xs[:, u, :]).then_inc(stat, 1)
                    need(dve, stat, 2 * n + 1)
                    dve.sem_inc(passed, 1)
                    dve.bn_aggr(mv[:, u, :], st[:, u, :]).then_inc(stat, 1)
                    need(dve, stat, 2 * n + 2)
                    need(dve, rooted, n - 1)
                    dve.tensor_scalar(sd[:, u, 0:1], mv[:, u, 1:2], EPS, None, ALU.add).then_inc(var_eps, 1)

                def norm_end(n, u):
                    need(dve, rooted, n + 1)
                    dve.reciprocal(sd[:, u, 1:2], sd[:, u, 1:2]).then_inc(inv, 1)
                    need(dve, inv, n + 1)
                    need(dve, turned, n - 1)
                    dve.tensor_scalar(xn[:, u, :], xs[:, u, :], mv[:, u, 0:1], sd[:, u, 1:2], ALU.subtract,
                                      ALU.mult).then_inc(xn_done, 1)

                def mix(n, u):
                    need(dve, squared, 2 * n + 2)
                    dve.tensor_reduce(var[:, u, :].unsqueeze(2), sq[:, u, :].rearrange("p (h d) -> p h d", d=MD),
                                      AX.X, ALU.add).then_inc(sums, 1)
                    need(dve, sums, n + 1)
                    dve.tensor_scalar(var[:, u, :], var[:, u, :], 1.0 / MD, EPS, ALU.mult, ALU.add).then_inc(sums2, 1)

                def mix_end(n, u):
                    need(dve, rooted2, n + 1)
                    dve.reciprocal(dev[:, u, :], dev[:, u, :]).then_inc(inv2, 1)
                    need(dve, inv2, n + 1)
                    dve.tensor_tensor(wt[:, u, :], dev[:, u, 0:MH], dev[:, u, MH:2 * MH], ALU.mult).then_inc(wt_done, 1)
                    need(dve, wt_done, n + 1)
                    need(dve, dots, n - 1)
                    dve.tensor_tensor(vc[:, u, :].rearrange("p (h d) -> p h d", d=MD),
                                      kv_ps[1][:, :].rearrange("p (h d) -> p h d", d=MD),
                                      wt[:, u, :].unsqueeze(2).to_broadcast([P, MH, MD]), ALU.mult).then_inc(v_done, 1)

                def add(n):
                    need(dve, dots, n + 1)
                    need(dve, added, n + 1)
                    dve.tensor_tensor(T.dots[:, :], T.dots[:, :], dot_ps[:, :], ALU.add).then_inc(added, 1)

                dve.memset(T.dots[:, :], 0.0).then_inc(added, 1)
                norm(0, 0)
                norm_end(0, 0)

                def step(n, u):
                    more = not isinstance(n, int) or n + 1 < NT
                    if more:
                        norm(n + 1, 1 - u)
                    mix(n, u)
                    if more:
                        norm_end(n + 1, 1 - u)
                    if not isinstance(n, int) or n > 0:
                        add(n - 1)
                    mix_end(n, u)
                steps(dve, NT, S, step, tail=1)
                add(NT - 1)
                dve.wait_ge(er_done, NT)
                split_er(dve, T, tmp[:, :, :], split, 0)

            @block.scalar
            def _(act):
                def root(n, u):
                    need(act, var_eps, n + 1)
                    need(act, inv, n - 1)
                    nc.scalar.activation(sd[:, u, 1:2], sd[:, u, 0:1], ACT.Sqrt).then_inc(rooted, 1)

                root(0, 0)

                def step(n, u):
                    need(act, turned, n + 1)
                    need(act, row_done, n - 1)
                    need(act, xt_stored[u], 16 * uses(n, u, S))
                    nc.scalar.activation(xt[:, u, :, :].rearrange("p c n -> p (c n)"), xt_ps[:, :],
                                         ACT.Copy).then_inc(xt_done, 1)
                    if not isinstance(n, int) or n + 1 < NT:
                        root(n + 1, 1 - u)
                    need(act, sums, n - 1)
                    need(act, kv_done, 2 * n + 1)
                    nc.scalar.activation(sq[:, u, 0:INNER], kv_ps[0][:, :], ACT.Square).then_inc(squared, 1)
                    need(act, kv_done, 2 * n + 2)
                    nc.scalar.activation(sq[:, u, INNER:2 * INNER], kv_ps[1][:, :], ACT.Square).then_inc(squared, 1)
                    need(act, dots, n - 1)
                    nc.scalar.activation(kc[:, u, :], kv_ps[0][:, :], ACT.Copy).then_inc(k_out, 1)
                    need(act, row_done, n + 1)
                    need(act, row_stored[u], 16 * uses(n, u, S))
                    nc.scalar.activation(rows[:, u, :], row_ps[:, 0:ROW], ACT.Copy).then_inc(row_out, 1)
                    nc.scalar.activation(T.er_flat[:, bass.ds(n * HEADS, HEADS)], row_ps[:, ROW:EXT],
                                         ACT.Copy).then_inc(er_done, 1)
                    need(act, sums2, n + 1)
                    need(act, inv2, n - 1)
                    nc.scalar.activation(dev[:, u, :], var[:, u, :], ACT.Sqrt).then_inc(rooted2, 1)
                steps(act, NT, S, step, tail=1)

            @block.tensor
            def _(pe):
                def step(n, u):
                    need(pe, xn_done, n + 1)
                    need(pe, xt_done, n)
                    for c in range(FC):
                        t = nc.tensor.transpose(xt_ps[:, c * P:(c + 1) * P], xn[:, u, c * P:(c + 1) * P], T.ident[:, :])
                    t.then_inc(turned, 1)
                    if not isinstance(n, int) or n > 0:
                        dot(n - 1, 1 - u)
                    need(pe, xt_done, n + 1)
                    need(pe, k_out, n)
                    need(pe, v_done, n)
                    for j in range(2):
                        for c in range(FC):
                            t = nc.tensor.matmul(kv_ps[j][:, :], xt[:, u, c, :],
                                                 T.wkv[:, c, j * INNER:(j + 1) * INNER],
                                                 start=(c == 0), stop=(c == FC - 1))
                        t.then_inc(kv_done, 1)
                    need(pe, row_out, n)
                    need(pe, er_done, n)
                    for c in range(FC):
                        t = nc.tensor.matmul(row_ps[:, :], xt[:, u, c, :], T.wext[:, 0, c, :],
                                             start=(c == 0), stop=(c == FC - 1))
                    t.then_inc(row_done, 1)

                def dot(n, u):
                    need(pe, v_done, n + 1)
                    need(pe, k_out, n + 1)
                    need(pe, added, n + 1)
                    for q in range(PAIRS):
                        t = nc.tensor.matmul(dot_ps[:, q * P:(q + 1) * P], vc[:, u, q * P:(q + 1) * P],
                                             kc[:, u, q * P:(q + 1) * P], start=True, stop=True)
                    t.then_inc(dots, 1)

                steps(pe, NT, S, step, tail=1)
                dot(NT - 1, (NT - 1) % S)


def mix_matrix(nc, T, wq, wo_t):
    with ExitStack() as ctx:
        def sb(name, shape, dt=F32):
            return ctx.enter_context(nc.sbuf_tensor(name, shape, dt))

        wq_sb = sb("wq_sb", [P, PAIRS, FEAT])
        wo_sb = sb("wo_sb", [P, PAIRS, FEAT])
        diag = sb("diag", [P, PAIRS, P])
        a_sb = sb("a_sb", [P, PAIRS, FEAT])
        a_ps = [ctx.enter_context(nc.psum_tensor(f"a_ps{q}", [P, FEAT], F32)) for q in range(PAIRS)]
        g_ps = [ctx.enter_context(nc.psum_tensor(f"g_ps{q}", [P, FEAT], F32)) for q in range(FC)]
        loaded, cleared, diag_done, a_done, a_out, g_done, g_out = [
            ctx.enter_context(nc.semaphore("m_" + s)) for s in
            ("loaded", "cleared", "diag", "a", "a_out", "g", "g_out")]
        with nc.Block() as block:
            @block.sync
            def _(sp):
                sp.dma_start(wq_sb[:, :, :], wq.rearrange("(q p) n -> p q n", p=P)).then_inc(loaded, 16)
                sp.dma_start(wo_sb[:, :, :], wo_t.rearrange("(q p) n -> p q n", p=P)).then_inc(loaded, 16)

            @block.vector
            def _(dve):
                dve.memset(diag[:, :, :], 0.0).then_inc(cleared, 1)
                dve.wait_ge(cleared, 1)
                d = T.dots[:, :].rearrange("p (q n) -> p q n", n=P)
                for h in range(2):
                    s = slice(h * MD, (h + 1) * MD)
                    dve.tensor_scalar(diag[s, :, s], d[s, :, s], 1.0 / NODES, None, ALU.mult).then_inc(diag_done, 1)
                for q in range(PAIRS):
                    dve.wait_ge(a_done, q + 1)
                    dve.tensor_copy(a_sb[:, q, :], a_ps[q][:, :]).then_inc(a_out, 1)
                for c in range(FC):
                    dve.wait_ge(g_done, c + 1)
                    dve.tensor_copy(T.mixw[:, c, :], g_ps[c][:, :]).then_inc(g_out, 1)

            @block.tensor
            def _(pe):
                pe.wait_ge(loaded, 32)
                pe.wait_ge(diag_done, 2)
                for q in range(PAIRS):
                    nc.tensor.matmul(a_ps[q][:, :], diag[:, q, :], wo_sb[:, q, :], start=True,
                                     stop=True).then_inc(a_done, 1)
                pe.wait_ge(a_out, PAIRS)
                for c in range(FC):
                    for q in range(PAIRS):
                        t = nc.tensor.matmul(g_ps[c][:, :], wq_sb[:, q, c * P:(c + 1) * P], a_sb[:, q, :],
                                             start=(q == 0), stop=(q == PAIRS - 1))
                    t.then_inc(g_done, 1)


def edge_pass(nc, T, S, l):
    N0 = l * NB
    GS = SLOTS

    def landed(n, u):
        return (NB // GS) * l + uses(n, u, GS) + 1

    with nc.Block() as block:
        @block.gpsimd
        def _(pool):
            def fetch_indices(n, u):
                if not isinstance(n, int) or landed(n, u) > 1:
                    need(pool, S.gathered[u], 16 * BT * (landed(n, u) - 1))
                pool.tensor_copy(S.idx[:, u, :], T.src_t[:, bass.ds(n, 1), :].rearrange("p a j -> p (a j)")
                                 ).then_inc(S.idx_ready, 1)

            if l == 0:
                pool.memset(T.acc[:, :], 0.0).then_inc(S.acc_cleared, 1)
            fetch_indices(0, 0)

            def step(n, u):
                if not isinstance(n, int) or n + 1 < NB:
                    fetch_indices(n + 1, (u + 1) % GS)
                need(pool, S.summed, N0 + n - GS + 1)
                need(pool, S.idx_ready, N0 + n + 1)
                pool.sem_inc(S.issuing, 1)
                for j in range(BT):
                    pool.indirect_dma_start(
                        S.rows[:, u, j, :], None, T.rows_d[l],
                        bass.IndirectOffsetOnAxis(ap=S.idx[:, u, j:j + 1].bitcast(U32), axis=0),
                    ).then_inc(S.gathered[u], 16)
            steps(pool, NB, GS, step, tail=1)

        @block.sync
        def _(sp):
            def step(n, u):
                need(sp, S.resc_made, N0 + n - GS + 1)
                sp.dma_start(S.loc_row[:, u, :], T.loc_d[bass.ds(n * BE, BE)][None, :].to_broadcast([P, BE])
                             ).then_inc(S.tables[u], 16)
                sp.dma_start(S.flags[:, u, :], T.flag_d[bass.ds(n * BE, BE + 1)][None, :]
                             .to_broadcast([HEADS, BE + 1])).then_inc(S.tables[u], 16)
            steps(sp, NB, GS, step, tail=1)

        @block.vector
        def _(dve):
            def one_hot_t(n, u):
                need(dve, S.tables[u], 32 * landed(n, u))
                need(dve, S.er_ready, N0 + n - 1)
                dve.tensor_scalar(S.hot_t[:, u % 2, :], S.loc_row[:, u, :], T.col[:, 0:1], None,
                                  ALU.is_equal).then_inc(S.hot_t_ready, 1)

            def er_by_edge(n, u):
                need(dve, S.er_ready, N0 + n + 1)
                dve.tensor_reduce(heads_of(S.er_e[:, :], HEADS).unsqueeze(3),
                                  S.er_ps[u % 2][:, 0:BT * 3 * HEADS].rearrange("p (v k h) -> p v h k", k=3, h=HEADS),
                                  AX.X, ALU.add).then_inc(S.er_summed, 1)

            def add_el(n, u):
                need(dve, S.er_summed, N0 + n + 1)
                need(dve, S.gathered[u], 16 * BT * landed(n, u))
                el = S.rows[:, u, :, :].rearrange("p v (h k) -> p v h k", k=HD + 1)[:, :, :, HD]
                dve.tensor_tensor(heads_of(S.pre[:, :], HEADS), el, heads_of(S.er_e[:, :], HEADS),
                                  ALU.add).then_inc(S.pre_ready, 1)

            def leaky(n, u):
                need(dve, S.pre_ready, N0 + n + 1)
                need(dve, S.below_ready, N0 + n - 1)
                dve.scalar_tensor_tensor(S.e[:, u % 2, :], S.pre[:, :], 0.2, S.pre[:, :], ALU.mult, ALU.max).then_inc(S.e_ready, 1)

            def maxima(n, u, ahead):
                m, b = S.fwd[:, u % 2, :], S.bwd[:, u % 2, :]
                first = isinstance(n, int) and n == 0
                need(dve, S.e_t_ready, N0 + n + 1)
                carry = S.fwd[:, 1 - u % 2, BE - 1:BE]
                dve.tensor_tensor_scan(m, S.flags[:, u, 0:BE], S.e_ps[0:HEADS, :], NEG if first else carry,
                                       ALU.add, ALU.max).then_inc(S.fwd_ready, 1)
                dve.tensor_scalar(S.goes_on[:, :], S.flags[:, u, 0:1], 0.0, None, ALU.is_equal).then_inc(S.flag_read, 1)
                need(dve, S.resc_ready, N0 + n)
                dve.tensor_tensor(S.hot0[:, :], T.row[0:HEADS, :], S.loc_row[0:HEADS, u, 0:1].to_broadcast([HEADS, P]),
                                  ALU.is_equal).then_inc(S.hot0_ready, 1)
                if ahead:
                    one_hot_t(n + 1, (u + 1) % GS)
                need(dve, S.fwd_ready, N0 + n + 1)
                need(dve, S.max_t_ready, N0 + n - 1)
                dve.tensor_tensor_scan(b[:, ::-1], S.flags[:, u, 1:BE + 1][:, ::-1], m[:, ::-1], NEG,
                                       ALU.add, ALU.max).then_inc(S.bwd_ready, 1)

            def drop_of(n, u):
                b = S.bwd[:, u % 2, :]
                first = isinstance(n, int) and n == 0
                carry = b[:, 0:1] if first else S.fwd[:, 1 - u % 2, BE - 1:BE]
                need(dve, S.bwd_ready, N0 + n + 1)
                dve.tensor_tensor(S.drop[:, :], carry, b[:, 0:1], ALU.subtract).then_inc(S.drop_ready, 1)
                need(dve, S.drop_ready, N0 + n + 1)
                need(dve, S.flag_read, N0 + n + 1)
                dve.tensor_scalar(S.drop_diag[:, :], T.ident[0:HEADS, 0:HEADS], S.drop[:, :], S.goes_on[:, :],
                                  ALU.mult, ALU.mult).then_inc(S.resc_made, 1)

            def below_max(n, u):
                need(dve, S.max_t_ready, N0 + n + 1)
                need(dve, S.exp_done, N0 + n - 1)
                dve.tensor_tensor(S.below[:, u % 2, :], S.e[:, u % 2, :], S.max_ps[:, 0:BT * HEADS],
                                  ALU.subtract).then_inc(S.below_ready, 1)

            def window_of(n):
                return dve.value_load(T.win[0:1, bass.ds(n, 1)], min_val=0, max_val=NT - 1)

            def rescale_sum(n, u, d):
                w = T.acc[:, bass.ds(d * ROW, ROW)]
                need(dve, S.resc_exp, N0 + n + 1)
                need(dve, S.added, 2 * (N0 + n))
                dve.tensor_tensor(heads_of(w, HD + 1), heads_of(w, HD + 1),
                                  S.resc[:, u % 2, :].unsqueeze(2).to_broadcast([P, HEADS, HD + 1]),
                                  ALU.mult).then_inc(S.added, 1)

            def add_sum(n, u, d):
                w = T.acc[:, bass.ds(d * ROW, ROW)]
                need(dve, S.summed, N0 + n + 1)
                need(dve, S.added, 2 * (N0 + n) + 1)
                dve.tensor_tensor(w, w, S.sum_ps[u % 2][:, 0:ROW], ALU.add).then_inc(S.added, 1)

            def weigh(n, u):
                need(dve, S.exp_done, N0 + n + 1)
                r = S.rows[:, u, :, :].rearrange("p v (h k) -> p (v h) k", k=HD + 1)
                dve.tensor_tensor(r[:, :, 0:HD], r[:, :, 0:HD], r[:, :, HD:HD + 1].to_broadcast([P, BT * HEADS, HD]),
                                  ALU.mult).then_inc(S.weighted, 1)

            def running(n, u, count):
                has = lambda k: not isinstance(n, int) or 0 <= n + k < count
                nxt, prv = (u + 1) % GS, (u - 2) % GS
                d = window_of(n - 2) if has(-2) else None
                if has(0):
                    maxima(n, u, has(1))
                    drop_of(n, u)
                if has(1):
                    er_by_edge(n + 1, nxt)
                if has(-2):
                    rescale_sum(n - 2, prv, d)
                if has(1):
                    add_el(n + 1, nxt)
                if has(0):
                    below_max(n, u)
                if has(-2):
                    add_sum(n - 2, prv, d)
                if has(1):
                    leaky(n + 1, nxt)

            dve.wait_ge(S.acc_cleared, l + 1)
            one_hot_t(0, 0)
            er_by_edge(0, 0)
            add_el(0, 0)
            leaky(0, 0)
            running(0, 0, NB)

            def step(n, u):
                weigh(n, u)
                running(n + 1, (u + 1) % GS, NB)
            steps(dve, NB, GS, step, tail=2)
            running(NB + 1, 1, NB)
            dve.wait_ge(S.added, 2 * (N0 + NB))

        @block.scalar
        def _(act):
            def one_hot(n, u):
                need(act, S.squares_read, N0 + n)
                for j in range(BT):
                    nc.scalar.activation(S.square[:, j, :], T.row[:, :], ACT.Square,
                                         bias=T.neg_loc[:, bass.ds(n, 1), j]).then_inc(S.squared, 1)
                need(act, S.squared, BT * (N0 + n + 1))
                need(act, S.summed, N0 + n - 1)
                nc.scalar.activation(S.hot[:, u % 2, :, :], S.square[:, :, :], ACT.Relu, scale=-1.0,
                                     bias=T.one[:, 0:1]).then_inc(S.squares_read, 1)

            def rescale(n, u):
                need(act, S.resc_ready, N0 + n + 1)
                need(act, S.added, 2 * (N0 + n - 2) + 1)
                nc.scalar.activation(S.resc[:, u % 2, :], S.resc_ps[:, 0:HEADS], ACT.Exp).then_inc(S.resc_exp, 1)

            def weights_of(n, u):
                need(act, S.below_ready, N0 + n + 1)
                w = S.rows[:, u, :, :].rearrange("p v (h k) -> p (v h) k", k=HD + 1)[:, :, HD]
                nc.scalar.activation(w, S.below[:, u % 2, :], ACT.Exp).then_inc(S.exp_done, 1)

            rescale(0, 0)
            one_hot(0, 0)

            def step(n, u):
                weights_of(n, u)
                if not isinstance(n, int) or n + 1 < NB:
                    one_hot(n + 1, (u + 1) % GS)
                    rescale(n + 1, (u + 1) % GS)
            steps(act, NB, GS, step, tail=1)

        @block.tensor
        def _(pe):
            def window_of(n):
                return pe.value_load(T.win[0:1, bass.ds(n, 1)], min_val=0, max_val=NT - 1)

            def er_by_edge(n, u, d):
                need(pe, S.er_summed, N0 + n - 1)
                need(pe, S.hot_t_ready, N0 + n + 1)
                for v in range(BT):
                    t = nc.tensor.matmul(S.er_ps[u % 2][:, v * 3 * HEADS:(v + 1) * 3 * HEADS],
                                         S.hot_t[:, u % 2, v * P:(v + 1) * P],
                                         T.er3_flat[:, bass.ds(d * 3 * HEADS, 3 * HEADS)], start=True, stop=True)
                t.then_inc(S.er_ready, 1)

            def turn_logits(n, u):
                need(pe, S.fwd_ready, N0 + n)
                need(pe, S.e_ready, N0 + n + 1)
                for v in range(BT):
                    t = nc.tensor.transpose(S.e_ps[0:HEADS, v * P:(v + 1) * P],
                                            S.e[:, u % 2, v * HEADS:(v + 1) * HEADS], T.ident[:, :])
                t.then_inc(S.e_t_ready, 1)

            def turn_maxima(n, u):
                need(pe, S.below_ready, N0 + n)
                need(pe, S.resc_exp, N0 + n)
                need(pe, S.bwd_ready, N0 + n + 1)
                need(pe, S.resc_made, N0 + n + 1)
                nc.tensor.matmul(S.resc_ps[:, 0:HEADS], S.hot0[:, :], S.drop_diag[:, :], start=True,
                                 stop=True).then_inc(S.resc_ready, 1)
                for v in range(BT):
                    t = nc.tensor.transpose(S.max_ps[:, v * HEADS:(v + 1) * HEADS],
                                            S.bwd[:, u % 2, v * P:(v + 1) * P], T.ident[0:HEADS, 0:HEADS])
                t.then_inc(S.max_t_ready, 1)

            def sum_up(n, u, v0, v1):
                if v0 == 0:
                    need(pe, S.squares_read, N0 + n + 1)
                    need(pe, S.weighted, N0 + n + 1)
                    need(pe, S.added, 2 * (N0 + n - 1))
                for v in range(v0, v1):
                    t = nc.tensor.matmul(S.sum_ps[u % 2][:, 0:ROW], S.hot[:, u % 2, v, :], S.rows[:, u, v, :],
                                         start=(v == 0), stop=(v == BT - 1))
                if v1 == BT:
                    t.then_inc(S.summed, 1)

            er_by_edge(0, 0, window_of(0))
            turn_logits(0, 0)
            er_by_edge(1, 1, window_of(1))
            turn_maxima(0, 0)

            def step(n, u):
                more = not isinstance(n, int) or n + 1 < NB
                nxt, prv = (u + 1) % GS, (u - 1) % GS
                if more:
                    turn_logits(n + 1, nxt)
                ahead = not isinstance(n, int) or n + 2 < NB
                d = window_of(n + 2) if ahead else None
                sum_up(n, u, 0, BT // 2)
                if ahead:
                    er_by_edge(n + 2, (u + 2) % GS, d)
                if more:
                    turn_maxima(n + 1, nxt)
                sum_up(n, u, BT // 2, BT)
            steps(pe, NB, GS, step, tail=2)


class EdgeBuffers:

    def __init__(self, nc, ctx):
        def sb(name, shape, dt=F32):
            return ctx.enter_context(nc.sbuf_tensor(name, shape, dt))

        def ps(name, cols=512):
            return ctx.enter_context(nc.psum_tensor(name, [P, cols], F32))

        def sem(name):
            return ctx.enter_context(nc.semaphore("e_" + name))

        self.idx = sb("idx", [P, SLOTS, BT], I32)
        self.rows = sb("g_rows", [P, SLOTS, BT, ROW])
        self.loc_row = sb("loc_row", [P, SLOTS, BE], BF16)
        self.flags = sb("flags", [HEADS, SLOTS, BE + 1])
        self.hot_t = sb("hot_t", [P, 2, BE], BF16)
        self.square = sb("square", [P, BT, P])
        self.hot = sb("hot", [P, 2, BT, P])
        self.er_e = sb("er_e", [P, BT * HEADS])
        self.pre = sb("pre", [P, BT * HEADS])
        self.e = sb("e", [P, 2, BT * HEADS])
        self.below = sb("below_m", [P, 2, BT * HEADS])
        self.fwd = sb("fwd", [HEADS, 2, BE])
        self.bwd = sb("bwd", [HEADS, 2, BE])
        self.goes_on = sb("goes_on", [HEADS, 1])
        self.drop = sb("drop", [HEADS, 1])
        self.drop_diag = sb("drop_diag", [HEADS, HEADS])
        self.hot0 = sb("hot0", [HEADS, P])
        self.resc = sb("resc", [P, 2, HEADS])
        self.e_ps = ps("e_ps", BE)
        self.er_ps = [ps(f"er_ps{i}") for i in range(2)]
        self.max_ps = ps("max_ps")
        self.resc_ps = ps("resc_ps")
        self.sum_ps = [ps(f"sum_ps{i}") for i in range(2)]
        self.acc_cleared = sem("acc_cleared")
        self.idx_ready = sem("idx_ready")
        self.issuing = sem("issuing")
        self.summed = sem("summed")
        self.hot_t_ready = sem("hot_t_ready")
        self.er_ready = sem("er_ready")
        self.er_summed = sem("er_summed")
        self.pre_ready = sem("pre_ready")
        self.e_ready = sem("e_ready")
        self.e_t_ready = sem("e_t_ready")
        self.fwd_ready = sem("fwd_ready")
        self.bwd_ready = sem("bwd_ready")
        self.flag_read = sem("flag_read")
        self.hot0_ready = sem("hot0_ready")
        self.resc_ready = sem("resc_ready")
        self.drop_ready = sem("drop_ready")
        self.resc_made = sem("resc_made")
        self.squared = sem("squared")
        self.squares_read = sem("squares_read")
        self.max_t_ready = sem("max_t_ready")
        self.below_ready = sem("below_ready")
        self.weighted = sem("weighted")
        self.exp_done = sem("exp_done")
        self.resc_exp = sem("resc_exp")
        self.added = sem("added")
        self.gathered = [sem(f"gathered{u}") for u in range(SLOTS)]
        self.tables = [sem(f"tables{u}") for u in range(SLOTS)]


def next_nodes(nc, T, S, l, bias):
    with ExitStack() as ctx:
        def sb(name, shape, dt=F32):
            return ctx.enter_context(nc.sbuf_tensor(f"u{l}_{name}", shape, dt))

        def sem(name):
            return ctx.enter_context(nc.semaphore(f"u{l}_{name}"))

        b_sb = sb("b", [P, FEAT])
        den = sb("den", [P, 2, HEADS])
        y = sb("y", [P, 2, FEAT])
        z = sb("z", [P, 2, FEAT])
        zt = sb("zt", [P, 2, FC, P])
        rows = sb("rows", [P, 2, ROW])
        tmp = sb("tmp", [P, NT, HEADS])
        zt_ps = [S.sum_ps[0], S.sum_ps[1]]
        row_ps = S.er_ps
        loaded, den1, den2, div, biased, leaky, turned, zt_done, row_done, row_out, er_done, split = map(sem, (
            "loaded", "den1", "den2", "div", "biased", "leaky", "turned", "zt", "row", "row_out", "er",
            "split"))
        stored = [sem("stored0"), sem("stored1")]
        with nc.Block() as block:
            @block.sync
            def _(sp):
                sp.dma_start(b_sb[:, :], bias[l:l + 1, :].to_broadcast([P, FEAT])).then_inc(loaded, 16)

                def step(n, u):
                    need(sp, row_out, n + 1)
                    sp.dma_start(T.rows_d[l + 1][bass.ds(n * P, P), :], rows[:, u, :]).then_inc(stored[u], 16)
                steps(sp, NT, 2, step)
                for u in range(2):
                    sp.wait_ge(stored[u], 16 * slot_total(NT, u, 2))

            @block.vector
            def _(dve):
                dve.wait_ge(loaded, 16)

                def step(n, u):
                    w = heads_of(T.acc[:, bass.ds(n * ROW, ROW)], HD + 1)
                    dve.tensor_scalar(den[:, u, :].unsqueeze(2), w[:, :, HD:HD + 1], 1e-30, None,
                                      ALU.max).then_inc(den1, 1)
                    need(dve, den1, n + 1)
                    dve.reciprocal(den[:, u, :], den[:, u, :]).then_inc(den2, 1)
                    need(dve, den2, n + 1)
                    dve.tensor_tensor(heads_of(y[:, u, :], HD), w[:, :, 0:HD],
                                      den[:, u, :].unsqueeze(2).to_broadcast([P, HEADS, HD]), ALU.mult).then_inc(div, 1)
                    need(dve, div, n + 1)
                    dve.tensor_tensor(y[:, u, :], y[:, u, :], b_sb[:, :], ALU.add).then_inc(biased, 1)
                    need(dve, biased, n + 1)
                    need(dve, turned, n - 1)
                    dve.scalar_tensor_tensor(z[:, u, :], y[:, u, :], 0.01, y[:, u, :], ALU.mult,
                                             ALU.max).then_inc(leaky, 1)
                steps(dve, NT, 2, step)
                dve.wait_ge(er_done, NT)
                split_er(dve, T, tmp[:, :, :], split, 0)

            @block.scalar
            def _(act):
                def step(n, u):
                    need(act, turned, n + 1)
                    need(act, row_done, n - 1)
                    nc.scalar.activation(zt[:, u, :, :].rearrange("p c n -> p (c n)"), zt_ps[u][:, 0:FEAT],
                                         ACT.Copy).then_inc(zt_done, 1)
                    need(act, row_done, n + 1)
                    need(act, stored[u], 16 * uses(n, u, 2))
                    nc.scalar.activation(rows[:, u, :], row_ps[u][:, 0:ROW], ACT.Copy).then_inc(row_out, 1)
                    nc.scalar.activation(T.er_flat[:, bass.ds(n * HEADS, HEADS)], row_ps[u][:, ROW:EXT],
                                         ACT.Copy).then_inc(er_done, 1)
                steps(act, NT, 2, step)

            @block.tensor
            def _(pe):
                def step(n, u):
                    turn(n, u)
                    if not isinstance(n, int) or n > 0:
                        row(n - 1, 1 - u)

                def turn(n, u):
                    need(pe, leaky, n + 1)
                    need(pe, zt_done, n - 1)
                    for c in range(FC):
                        t = nc.tensor.transpose(zt_ps[u][:, c * P:(c + 1) * P], z[:, u, c * P:(c + 1) * P],
                                                T.ident[:, :])
                    t.then_inc(turned, 1)

                def row(n, u):
                    need(pe, zt_done, n + 1)
                    need(pe, er_done, n - 1)
                    for c in range(FC):
                        t = nc.tensor.matmul(row_ps[u][:, 0:EXT], zt[:, u, c, :], T.wext[:, l + 1, c, :],
                                             start=(c == 0), stop=(c == FC - 1))
                    t.then_inc(row_done, 1)
                steps(pe, NT, 2, step)
                row(NT - 1, (NT - 1) % 2)

            @block.gpsimd
            def _(pool):
                pool.wait_ge(div, NT)
                pool.memset(T.acc[:, :], 0.0).then_inc(S.acc_cleared, 1)


def feed_forward(nc, T, bias, x, bout, router_t, w1, b1, w2, b2, out):
    with ExitStack() as ctx:
        def sb(name, shape, dt=F32):
            return ctx.enter_context(nc.sbuf_tensor("f_" + name, shape, dt))

        def sem(name):
            return ctx.enter_context(nc.semaphore("f_" + name))

        def ps(name):
            return ctx.enter_context(nc.psum_tensor("f_" + name + "_ps", [P, 512], F32))

        w1_sb = sb("w1", [P, EXPERTS, FC, FEAT])
        w2_sb = sb("w2", [P, EXPERTS, FC, FEAT])
        b1_sb = sb("b1", [P, EXPERTS, FC])
        b2_sb = sb("b2", [EXPERTS, FEAT])
        rt_sb = sb("rt", [P, FC, EXPERTS])
        bias_sb = sb("bias", [P, FEAT])
        bo_sb = sb("bo", [P, FEAT])
        xin = sb("x", [P, 2, FEAT])
        xt = sb("xt", [P, 2, FC, P])
        den = sb("den", [P, HEADS])
        x1 = sb("x1", [P, 2, FEAT])
        st = sb("st", [P, 6])
        mv = sb("mv", [P, 2])
        sd = sb("sd", [P, 2])
        tok = sb("tok", [P, 2, FEAT])
        tt = sb("tt", [P, 2, FC, P])
        neg = sb("neg", [P, 2])
        lg = sb("lg", [P, EXPERTS])
        prob = sb("prob", [P, EXPERTS])
        top = sb("top", [P, 8])
        top_i = sb("top_i", [P, 8], U32)
        top_f = sb("top_f", [P, 8])
        two = sb("two", [P, 2])
        pick = sb("pick", [P, EXPERTS])
        comb = sb("comb", [P, 2, EXPERTS])
        comb_t = sb("comb_t", [EXPERTS, P])
        hid = sb("hid", [P, 2, FC, P])
        res = sb("res", [P, 2, FEAT])
        mix_ps, turn_ps, lg_ps, b2_ps = ps("mix"), ps("turn"), ps("lg"), ps("b2")
        h_ps = [ps("h0"), ps("h1")]
        y_ps = [ps("y0"), ps("y1")]
        loaded, w_in, mixed, front, rooted, turned, tt_done, lg_done, exp_done, comb_done, comb_turned, comb_out, \
            b2_done, hidden, gelu, multiplied, added, begun, passed = map(sem, (
                "loaded", "w_in", "mixed", "front", "rooted", "turned", "tt", "lg", "exp", "comb", "comb_turned",
                "comb_out", "b2d", "hidden", "gelu", "mult", "added", "begun", "passed"))
        stored = [sem("stored0"), sem("stored1")]
        x_in = [sem("x_in0"), sem("x_in1")]
        K = 23

        with nc.Block() as block:
            @block.sync
            def _(sp):
                for dst, src in ((bias_sb[:, :], bias[LAYERS - 1:LAYERS, :].to_broadcast([P, FEAT])),
                                 (bo_sb[:, :], bout[None, :].to_broadcast([P, FEAT])),
                                 (rt_sb[:, :, :], router_t.rearrange("(c p) n -> p c n", p=P)),
                                 (b2_sb[:, :], b2)):
                    sp.dma_start(dst, src).then_inc(loaded, 16)
                with nc.allow_non_contiguous_dma(reason="a bias by partition"):
                    sp.dma_start(b1_sb[:, :, :], b1.rearrange("e (c p) -> p e c", p=P)).then_inc(loaded, 16)
                sp.dma_start(w1_sb[:, :, :, :], w1.rearrange("e (c p) n -> p e c n", p=P)).then_inc(w_in, 16)
                sp.dma_start(w2_sb[:, :, :, :], w2.rearrange("e (c p) n -> p e c n", p=P)).then_inc(w_in, 16)

                def step(n, u):
                    need(sp, front, K * (n - 1))
                    sp.dma_start(xin[:, u, :], x[bass.ds(n * P, P), :]).then_inc(x_in[u], 16)
                    sp.dma_start(xt[:, u, :, :].rearrange("p c n -> p (c n)"), T.xt_d[bass.ds(n * P, P), :]
                                 ).then_inc(x_in[u], 16)
                steps(sp, NT, 2, step)

            @block.gpsimd
            def _(pool):
                def step(n, u):
                    need(pool, added, EXPERTS * (n + 1))
                    k = NODES - (NT - 1) * P if isinstance(n, int) and n == NT - 1 else P
                    pool.dma_start(out[bass.ds(n * P, k), :], res[0:k, u, :]).then_inc(stored[u], 16)
                steps(pool, NT, 2, step, tail=1)
                for u in range(2):
                    pool.wait_ge(stored[u], 16 * slot_total(NT, u, 2))

            @block.vector
            def _(dve):
                def before(n, u):
                    k = [0]

                    def link(ins, carry=False):
                        k[0] += 1
                        ins.then_inc(front, 1)
                        dve.wait_ge(front, K * n + k[0])
                        if carry:
                            dve.sem_inc(passed, 1)

                    w = heads_of(T.acc[:, bass.ds(n * ROW, ROW)], HD + 1)
                    y = x1[:, u, :]
                    link(dve.tensor_scalar(den[:, :].unsqueeze(2), w[:, :, HD:HD + 1], 1e-30, None, ALU.max))
                    link(dve.reciprocal(den[:, :], den[:, :]))
                    link(dve.tensor_tensor(heads_of(y, HD), w[:, :, 0:HD],
                                           den[:, :].unsqueeze(2).to_broadcast([P, HEADS, HD]), ALU.mult))
                    link(dve.tensor_tensor(y, y, bias_sb[:, :], ALU.add))
                    need(dve, x_in[u], ((n - u) // 2) * 32 + 32)
                    link(dve.tensor_tensor(y, y, xin[:, u, :], ALU.add))
                    need(dve, mixed, n + 1)
                    link(dve.tensor_tensor(y, y, mix_ps[:, 0:FEAT], ALU.add))
                    link(dve.tensor_tensor(y, y, bo_sb[:, :], ALU.add))
                    link(dve.bn_stats(st[:, :], y), carry=True)
                    link(dve.bn_aggr(mv[:, :], st[:, :]))
                    link(dve.tensor_scalar(sd[:, 0:1], mv[:, 1:2], EPS, None, ALU.add))
                    assert k[0] == 10
                    need(dve, rooted, n + 1)
                    link(dve.reciprocal(sd[:, 1:2], sd[:, 1:2]))
                    link(dve.tensor_scalar(tok[:, u, :], y, mv[:, 0:1], sd[:, 1:2], ALU.subtract, ALU.mult))
                    assert k[0] == 12
                    need(dve, lg_done, n + 1)
                    link(dve.tensor_reduce(neg[:, 0:1], lg_ps[:, 0:EXPERTS], AX.X, ALU.max, negate=True))
                    assert k[0] == 13
                    need(dve, exp_done, n + 1)
                    link(dve.reciprocal(neg[:, 1:2], neg[:, 1:2]))
                    link(dve.tensor_scalar(prob[:, :], lg[:, :], neg[:, 1:2], None, ALU.mult), carry=True)
                    link(dve.max(top[:, :], prob[:, :]), carry=True)
                    link(dve.max_index(top_i[:, :], top[:, :], prob[:, :]))
                    link(dve.tensor_copy(top_f[:, :], top_i[:, :]))
                    link(dve.tensor_scalar(two[:, 0:1], top[:, 0:1], top[:, 1:2], 1e-12, ALU.add, ALU.max))
                    link(dve.reciprocal(two[:, 1:2], two[:, 0:1]))
                    link(dve.tensor_scalar(top[:, 0:2], top[:, 0:2], two[:, 1:2], None, ALU.mult))
                    link(dve.tensor_scalar(pick[:, :], T.row[:, 0:EXPERTS], top_f[:, 0:1], top[:, 0:1],
                                           ALU.is_equal, ALU.mult))
                    link(dve.tensor_scalar(comb[:, u, :], T.row[:, 0:EXPERTS], top_f[:, 1:2], top[:, 1:2],
                                           ALU.is_equal, ALU.mult))
                    assert k[0] == K
                    dve.tensor_tensor(comb[:, u, :], comb[:, u, :], pick[:, :], ALU.add).then_inc(comb_done, 1)

                def begin(n, u):
                    need(dve, b2_done, n + 1)
                    need(dve, stored[u], 16 * uses(n, u, 2))
                    dve.tensor_tensor(res[:, u, :], x1[:, u, :], tok[:, u, :], ALU.add).then_inc(begun, 1)
                    need(dve, begun, 2 * n + 1)
                    dve.tensor_tensor(res[:, u, :], res[:, u, :], b2_ps[:, 0:FEAT], ALU.add).then_inc(begun, 1)

                def expert(n, u, e):
                    need(dve, multiplied, EXPERTS * n + e + 1)
                    if e == 0:
                        need(dve, begun, 2 * n + 2)
                    else:
                        need(dve, added, EXPERTS * n + e)
                    dve.scalar_tensor_tensor(res[:, u, :], y_ps[e % 2][:, 0:FEAT], comb[:, u, e:e + 1], res[:, u, :],
                                             ALU.mult, ALU.add).then_inc(added, 1)

                dve.wait_ge(loaded, 80)
                before(0, 0)

                def step(n, u):
                    begin(n, u)
                    for e in range(4):
                        expert(n, u, e)
                    if not isinstance(n, int) or n + 1 < NT:
                        before(n + 1, 1 - u)
                    for e in range(4, EXPERTS):
                        expert(n, u, e)
                steps(dve, NT, 2, step, tail=1)

            @block.scalar
            def _(act):
                def before(n, u):
                    need(act, front, K * n + 10)
                    nc.scalar.activation(sd[:, 1:2], sd[:, 0:1], ACT.Sqrt).then_inc(rooted, 1)
                    need(act, turned, n + 1)
                    nc.scalar.activation(tt[:, u, :, :].rearrange("p c n -> p (c n)"), turn_ps[:, 0:FEAT],
                                         ACT.Copy).then_inc(tt_done, 1)
                    need(act, front, K * n + 13)
                    nc.scalar.activation(lg[:, :], lg_ps[:, 0:EXPERTS], ACT.Exp, bias=neg[:, 0:1],
                                         accum_out=neg[:, 1:2]).then_inc(exp_done, 1)
                    need(act, comb_turned, n + 1)
                    nc.scalar.activation(comb_t[:, :], turn_ps[0:EXPERTS, FEAT:FEAT + P], ACT.Copy).then_inc(comb_out, 1)

                def expert(n, u, e):
                    k = EXPERTS * n + e
                    for j in range(FC):
                        need(act, hidden, 2 * k + j + 1)
                        if j == 0:
                            need(act, multiplied, k - 1)
                        nc.scalar.activation(hid[:, e % 2, j, :], h_ps[j][:, 0:P], ACT.Gelu,
                                             bias=b1_sb[:, e, j:j + 1]).then_inc(gelu, 1)

                act.wait_ge(loaded, 80)
                before(0, 0)

                def step(n, u):
                    for e in range(4):
                        expert(n, u, e)
                    if not isinstance(n, int) or n + 1 < NT:
                        before(n + 1, 1 - u)
                    for e in range(4, EXPERTS):
                        expert(n, u, e)
                steps(act, NT, 2, step, tail=1)

            @block.tensor
            def _(pe):
                def before(n, u):
                    need(pe, x_in[u], ((n - u) // 2) * 32 + 32)
                    need(pe, front, K * n)
                    for c in range(FC):
                        t = nc.tensor.matmul(mix_ps[:, 0:FEAT], xt[:, u, c, :], T.mixw[:, c, :],
                                             start=(c == 0), stop=(c == FC - 1))
                    t.then_inc(mixed, 1)
                    need(pe, front, K * n + 12)
                    need(pe, comb_out, n)
                    for c in range(FC):
                        t = nc.tensor.transpose(turn_ps[:, c * P:(c + 1) * P], tok[:, u, c * P:(c + 1) * P],
                                                T.ident[:, :])
                    t.then_inc(turned, 1)
                    need(pe, tt_done, n + 1)
                    for c in range(FC):
                        t = nc.tensor.matmul(lg_ps[:, 0:EXPERTS], tt[:, u, c, :], rt_sb[:, c, :],
                                             start=(c == 0), stop=(c == FC - 1))
                    t.then_inc(lg_done, 1)
                    need(pe, comb_done, n + 1)
                    nc.tensor.transpose(turn_ps[0:EXPERTS, FEAT:FEAT + P], comb[:, u, :],
                                        T.ident[:, :]).then_inc(comb_turned, 1)
                    need(pe, comb_out, n + 1)
                    need(pe, begun, 2 * n)
                    nc.tensor.matmul(b2_ps[:, 0:FEAT], comb_t[:, :], b2_sb[:, :], start=True,
                                     stop=True).then_inc(b2_done, 1)

                def expand(n, u, e):
                    k = EXPERTS * n + e
                    for j in range(FC):
                        need(pe, gelu, 2 * (k - 1) + j + 1)
                        for c in range(FC):
                            t = nc.tensor.matmul(h_ps[j][:, 0:P], w1_sb[:, e, c, j * P:(j + 1) * P], tt[:, u, c, :],
                                                 start=(c == 0), stop=(c == FC - 1))
                        t.then_inc(hidden, 1)

                def contract(n, u, e):
                    k = EXPERTS * n + e
                    need(pe, gelu, 2 * k + 2)
                    need(pe, added, k - 1)
                    for j in range(FC):
                        t = nc.tensor.matmul(y_ps[e % 2][:, 0:FEAT], hid[:, e % 2, j, :], w2_sb[:, e, j, :],
                                             start=(j == 0), stop=(j == FC - 1))
                    t.then_inc(multiplied, 1)

                pe.wait_ge(loaded, 80)
                before(0, 0)
                pe.wait_ge(w_in, 32)

                def step(n, u):
                    for e in range(4):
                        expand(n, u, e)
                        if e > 0:
                            contract(n, u, e - 1)
                    contract(n, u, 3)
                    if not isinstance(n, int) or n + 1 < NT:
                        before(n + 1, 1 - u)
                    for e in range(4, EXPERTS):
                        expand(n, u, e)
                        if e > 4:
                            contract(n, u, e - 1)
                    contract(n, u, EXPERTS - 1)
                steps(pe, NT, 2, step, tail=1)


class Shared:
    pass


def program(nc, x, src_groups, dst_groups, dst_last, W, al, ar, b, wkv_t, wq, wo_t, bout, router_t, w1, b1, w2, b2,
            out):
    T = Shared()
    T.rows_d = [nc.dram_tensor(f"rows{l}_d", (NODES_PAD, ROW), F32, kind="Internal").ap() for l in range(LAYERS)]
    T.xt_d = nc.dram_tensor("xt_d", (NODES_PAD, FEAT), F32, kind="Internal").ap()
    T.loc_d = nc.dram_tensor("loc_d", (VP * BE,), BF16, kind="Internal").ap()
    T.flag_d = nc.dram_tensor("flag_d", (VP * BE + 8,), F32, kind="Internal").ap()
    T.key_d = nc.dram_tensor("key_d", (VP * BE + 8,), F32, kind="Internal").ap()
    T.win_d = nc.dram_tensor("win_d", (VP,), I32, kind="Internal").ap()
    with ExitStack() as ctx:
        def sb(name, shape, dt=F32):
            return ctx.enter_context(nc.sbuf_tensor(name, shape, dt))

        T.ident = sb("ident", [P, P])
        T.row = sb("row", [P, P])
        T.col = sb("col", [P, 1])
        T.one = sb("one", [P, 1])
        T.wext = sb("wext", [P, LAYERS, FC, EXT])
        T.mixw = sb("mixw", [P, FC, FEAT])
        T.er = sb("er", [P, NT, HEADS])
        T.er_flat = T.er[:, :, :].rearrange("p t h -> p (t h)")
        T.er3 = sb("er3", [P, NT, 3, HEADS], BF16)
        T.er3_flat = T.er3[:, :, :, :].rearrange("p t k h -> p (t k h)")
        T.src_t = sb("src_t", [P, VP, BT], I32)
        T.neg_loc = sb("neg_loc", [P, VP, BT])
        T.win = sb("win", [1, VP], I32)
        constants(nc, T)
        edge_tables(nc, T, dst_last, src_groups, dst_groups)
        with ExitStack() as early:
            T.wkv = early.enter_context(nc.sbuf_tensor("wkv", [P, FC, 2 * INNER], F32))
            T.dots = early.enter_context(nc.sbuf_tensor("dots", [P, PAIRS * P], F32))
            weights(nc, T, W, al, ar, wkv_t)
            first_nodes(nc, T, x)
            mix_matrix(nc, T, wq, wo_t)
        T.acc = sb("acc", [P, NT * ROW])
        with ExitStack() as mid:
            S = EdgeBuffers(nc, mid)
            for l in range(LAYERS):
                edge_pass(nc, T, S, l)
                if l + 1 < LAYERS:
                    next_nodes(nc, T, S, l, b)
        feed_forward(nc, T, b, x, bout, router_t, w1, b1, w2, b2, out)


def kernel(x, src, dst, L0_gnn_W, L0_gnn_al, L0_gnn_ar, L0_gnn_b, L0_mix_Wqkv, L0_mix_Wout, L0_mix_bout,
           L0_ffn_router_w, L0_ffn_w1, L0_ffn_b1, L0_ffn_w2, L0_ffn_b2):
    import numpy as np
    import concourse.bacc as bacc
    from concourse.bass_utils import run_bass_kernel_spmd

    def laid(a):
        return np.ascontiguousarray(a)

    x, src, dst = np.asarray(x), np.asarray(src), np.asarray(dst)
    x_pad = np.zeros((NODES_PAD, FEAT), x.dtype)
    x_pad[:NODES] = x
    src_groups = np.zeros((GROUPS * BE,), src.dtype)
    src_groups[:EDGES] = src
    dst_groups = np.full((GROUPS * BE,), NODES_PAD - 1, dst.dtype)
    dst_groups[:EDGES] = dst
    src_groups, dst_groups = src_groups.reshape(GROUPS, BE), dst_groups.reshape(GROUPS, BE)
    wqkv = np.asarray(L0_mix_Wqkv)
    ins = {
        "x": x_pad, "src_groups": src_groups, "dst_groups": dst_groups, "dst_last": laid(dst_groups[:, BE - 1]),
        "W": laid(L0_gnn_W), "al": laid(L0_gnn_al), "ar": laid(L0_gnn_ar), "b": laid(L0_gnn_b),
        "wkv_t": laid(wqkv[INNER:].T), "wq": laid(wqkv[:INNER]), "wo_t": laid(np.asarray(L0_mix_Wout).T),
        "bout": laid(L0_mix_bout), "router_t": laid(np.asarray(L0_ffn_router_w).T),
        "w1": laid(L0_ffn_w1), "b1": laid(L0_ffn_b1), "w2": laid(L0_ffn_w2), "b2": laid(L0_ffn_b2),
    }
    nc = bacc.Bacc("TRN2", target_bir_lowering=False, num_devices=1)
    arrays = {f"in_{k}": a for k, a in ins.items()}
    args = {k: nc.dram_tensor(f"in_{k}", a.shape, mybir.dt.from_np(a.dtype), kind="ExternalInput").ap()
            for k, a in ins.items()}
    out = nc.dram_tensor("out", (NODES, FEAT), F32, kind="ExternalOutput").ap()
    program(nc, out=out, **args)
    r = run_bass_kernel_spmd(nc, [arrays], core_ids=[0])
    return r.results[0]["out"]
```

```python
import concourse.bass as bass
from concourse import mybir
from contextlib import ExitStack

F32 = mybir.dt.float32
BF16 = mybir.dt.bfloat16
I32 = mybir.dt.int32
U32 = mybir.dt.uint32
ALU = mybir.AluOpType
ACT = mybir.ActivationFunctionType
AX = mybir.AxisListType

P = 128
NODES, FEAT = 6250, 256
EDGES = 2 * 100000 + NODES
HEADS, HD = 8, 32
LAYERS = 3
FC = FEAT // P
NT = -(-NODES // P)
NODES_PAD = NT * P
ET = -(-EDGES // P)
BT = 6
BE = BT * P
SLOTS = 6
NB = -(-(-(-ET // BT) + NT - 1) // SLOTS) * SLOTS
GROUPS = NB - NT + 1
CH = -(-NB // P)
VP = CH * P
ROW = HEADS * (HD + 1)
EXT = ROW + HEADS
NEG = -1.0e30
EPS = 1e-5
MH, MD = 8, 64
INNER = MH * MD
PAIRS = INNER // P
EXPERTS = 8
CHUNK_TILES = 7
assert NT % CHUNK_TILES == 0


def need(eng, sem, count):
    if not isinstance(count, int) or count > 0:
        eng.wait_ge(sem, count)


def steps(eng, total, unroll, step, tail=0):
    for n in range(unroll):
        step(n, n)
    rounds = (total - tail) // unroll
    with eng.Fori(1, rounds) as i:
        for u in range(unroll):
            step(i * unroll + u, u)
    for n in range(rounds * unroll, total):
        step(n, n % unroll)


def uses(n, slot, slots):
    return (n - slot) // slots


def slot_total(total, slot, slots):
    return (total - 1 - slot) // slots + 1


def heads_of(ap, width):
    return ap.rearrange("p (h k) -> p h k", k=width)


def constants(nc, T):
    with ExitStack() as ctx:
        made = ctx.enter_context(nc.semaphore("const_made"))
        with nc.Block() as block:
            @block.gpsimd
            def _(pool):
                pool.memset(T.ident[:, :], 0.0).then_inc(made, 1)
                pool.wait_ge(made, 1)
                pool.affine_select(out=T.ident[:, :], in_=T.ident[:, :], compare_op=ALU.not_equal, fill=1.0,
                                   base=0, pattern=[[-1, P]], channel_multiplier=1).then_inc(made, 1)
                pool.iota(T.row[:, :], pattern=[[1, P]], base=0, channel_multiplier=0,
                          allow_small_or_imprecise_dtypes=True).then_inc(made, 1)
                pool.iota(T.col[:, :], pattern=[[0, 1]], base=0, channel_multiplier=1,
                          allow_small_or_imprecise_dtypes=True).then_inc(made, 1)
                pool.memset(T.one[:, :], 1.0).then_inc(made, 1)
                pool.wait_ge(made, 5)


def edge_tables(nc, T, dst_last, src_groups, dst_groups):
    with ExitStack() as ctx:
        def sb(name, shape, dt=F32):
            return ctx.enter_context(nc.sbuf_tensor(name, shape, dt))

        def sem(name):
            return ctx.enter_context(nc.semaphore(name))

        last = sb("last", [P, GROUPS], I32)
        group_no = sb("group_no", [P, GROUPS], I32)
        path = sb("path", [P, GROUPS])
        below = sb("below", [P, GROUPS])
        visit_i = sb("visit_i", [P, CH], I32)
        visit = sb("visit", [P, CH])
        group_of = sb("group_of", [P, CH])
        group_idx = sb("group_idx", [P, CH], I32)
        win_of = sb("win_of", [P, CH])
        win_i = sb("win_i", [P, CH], I32)
        win_base = sb("win_base", [P, CH])
        src_v = sb("src_v", [P, CH, BE], I32)
        dst_v = sb("dst_v", [P, CH, BE], I32)
        src_f = sb("src_f", [P, CH, BE])
        loc = sb("loc", [P, CH, BE])
        inside = sb("inside", [P, CH, BE])
        locm = sb("locm", [P, CH, BE])
        locb = sb("locb", [P, CH, BE], BF16)
        key = sb("key", [P, CH, BE])
        prev = sb("prev", [P, CH, BE])
        edge = sb("edge", [1, 8])
        banks = [ctx.enter_context(nc.psum_tensor(f"tp{i}", [P, 512], F32)) for i in range(8)]
        loaded, iotas, step, gathered, turned, evacuated, stored, shifted, dtab = map(sem, (
            "tab_loaded", "tab_iotas", "tab_step", "tab_gathered", "tab_turned", "tab_evacuated",
            "tab_stored", "tab_shifted", "tab_dtab"))
        done = {}
        blocks = [(j, c) for j in range(BT) for c in range(CH)]
        lots = [(w, blocks[i:i + 4]) for w in range(2) for i in range(0, len(blocks), 4)]

        with nc.Block() as block:
            @block.vector
            def _(dve):
                count = [0]

                def link(ins, name=None):
                    count[0] += 1
                    ins.then_inc(step, 1)
                    dve.wait_ge(step, count[0])
                    if name:
                        done[name] = count[0]

                dve.wait_ge(loaded, 16)
                link(dve.tensor_scalar(last[:, :], last[:, :], 7, None, ALU.arith_shift_right))
                dve.wait_ge(iotas, 2)
                link(dve.tensor_tensor(path[:, :], last[:, :], group_no[:, :], ALU.add))
                link(dve.tensor_copy(visit[:, :], visit_i[:, :]))
                for c in range(CH):
                    link(dve.tensor_scalar(below[:, :], path[:, :], visit[:, c:c + 1], None, ALU.is_lt, ALU.add,
                                           accum_out=group_of[:, c:c + 1]))
                link(dve.tensor_tensor(win_of[:, :], visit[:, :], group_of[:, :], ALU.subtract))
                link(dve.tensor_scalar(group_of[:, :], group_of[:, :], float(GROUPS - 1), None, ALU.min))
                link(dve.tensor_scalar(win_of[:, :], win_of[:, :], float(NT - 1), None, ALU.min))
                link(dve.tensor_copy(group_idx[:, :], group_of[:, :]), "group_idx")
                link(dve.tensor_copy(win_i[:, :], win_of[:, :]), "win")
                link(dve.tensor_scalar(win_base[:, :], win_of[:, :], -float(P), None, ALU.mult))
                link(dve.memset(edge[:, 0:1], -2.0))
                link(dve.memset(edge[:, 1:8], 0.0), "edge")
                dve.wait_ge(gathered, 2 * CH * 16)
                link(dve.tensor_copy(src_f[:, :, :], src_v[:, :, :]), "src_f")
                for c in range(CH):
                    link(dve.tensor_scalar(loc[:, c, :], dst_v[:, c, :], win_base[:, c:c + 1], None, ALU.add))
                link(dve.tensor_scalar(inside[:, :, :], loc[:, :, :], 0.0, None, ALU.is_ge))
                link(dve.scalar_tensor_tensor(inside[:, :, :], loc[:, :, :], float(P - 1), inside[:, :, :],
                                              ALU.is_le, ALU.mult))
                link(dve.scalar_tensor_tensor(locm[:, :, :], loc[:, :, :], 1.0, inside[:, :, :], ALU.add, ALU.mult))
                link(dve.tensor_scalar(locm[:, :, :], locm[:, :, :], -1.0, None, ALU.add), "locm")
                link(dve.tensor_copy(locb[:, :, :], locm[:, :, :]), "locb")
                link(dve.scalar_tensor_tensor(key[:, :, :], dst_v[:, :, :], 1.0, inside[:, :, :], ALU.add, ALU.mult))
                link(dve.tensor_scalar(key[:, :, :], key[:, :, :], -1.0, None, ALU.add), "key")
                dve.wait_ge(shifted, 16)
                link(dve.tensor_tensor(prev[:, :, :], key[:, :, :], prev[:, :, :], ALU.not_equal))
                link(dve.tensor_scalar(prev[:, :, :], prev[:, :, :], NEG, None, ALU.mult), "flag")

            @block.gpsimd
            def _(pool):
                pool.iota(group_no[:, :], pattern=[[1, GROUPS]], base=0, channel_multiplier=0).then_inc(iotas, 1)
                pool.iota(visit_i[:, :], pattern=[[P, CH]], base=0, channel_multiplier=1).then_inc(iotas, 1)
                pool.wait_ge(step, done["group_idx"])
                for c in range(CH):
                    for table, rows in ((src_v, src_groups), (dst_v, dst_groups)):
                        pool.indirect_dma_start(
                            table[:, c, :], None, rows,
                            bass.IndirectOffsetOnAxis(ap=group_idx[:, c:c + 1].bitcast(U32), axis=0),
                        ).then_inc(gathered, 16)

            @block.tensor
            def _(pe):
                for i, (w, lot) in enumerate(lots):
                    pe.wait_ge(step, done["locm" if w else "src_f"])
                    if i >= 8:
                        pe.wait_ge(evacuated, sum(len(lot) for _, lot in lots[:i - 7]))
                    for k, (j, c) in enumerate(lot):
                        t = nc.tensor.transpose(banks[i % 8][:, k * P:(k + 1) * P],
                                                (locm if w else src_f)[:, c, j * P:(j + 1) * P], T.ident[:, :])
                    t.then_inc(turned, 1)

            @block.scalar
            def _(act):
                for i, (w, lot) in enumerate(lots):
                    act.wait_ge(turned, i + 1)
                    for k, (j, c) in enumerate(lot):
                        out = (T.neg_loc if w else T.src_t)[:, c * P:(c + 1) * P, j]
                        nc.scalar.activation(out, banks[i % 8][:, k * P:(k + 1) * P], ACT.Copy,
                                             scale=-1.0 if w else 1.0).then_inc(evacuated, 1)

            @block.sync
            def _(sp):
                by_visit = "(c p e) -> p c e"
                sp.dma_start(last[:, :], dst_last[None, :].to_broadcast([P, GROUPS])).then_inc(loaded, 16)
                sp.wait_ge(step, done["win"])
                with nc.allow_non_contiguous_dma(reason="a table of one word per visit"):
                    sp.dma_start(T.win_d[:].rearrange("(c p) -> p c", p=P), win_i[:, :]).then_inc(dtab, 16)
                sp.wait_ge(dtab, 16)
                sp.dma_start(T.win[0:1, :], T.win_d[:][None, :]).then_inc(dtab, 16)
                sp.wait_ge(step, done["edge"])
                sp.dma_start(T.key_d[0:1][None, :], edge[0:1, 0:1]).then_inc(stored, 16)
                sp.dma_start(T.flag_d[VP * BE:VP * BE + 7][None, :], edge[0:1, 1:8]).then_inc(stored, 16)
                sp.wait_ge(step, done["locb"])
                sp.dma_start(T.loc_d[:].rearrange(by_visit, p=P, e=BE), locb[:, :, :]).then_inc(stored, 16)
                sp.wait_ge(step, done["key"])
                sp.dma_start(T.key_d[1:1 + VP * BE].rearrange(by_visit, p=P, e=BE), key[:, :, :]).then_inc(stored, 16)
                sp.wait_ge(stored, 64)
                sp.dma_start(prev[:, :, :], T.key_d[0:VP * BE].rearrange(by_visit, p=P, e=BE)).then_inc(shifted, 16)
                sp.wait_ge(step, done["flag"])
                sp.dma_start(T.flag_d[0:VP * BE].rearrange(by_visit, p=P, e=BE), prev[:, :, :]).then_inc(stored, 16)
                sp.wait_ge(stored, 80)
                sp.wait_ge(dtab, 32)
                sp.wait_ge(evacuated, 2 * len(blocks))


def split_er(dve, T, tmp, sem, base):
    k = [base]

    def link(ins):
        k[0] += 1
        ins.then_inc(sem, 1)
        dve.wait_ge(sem, k[0])

    link(dve.tensor_copy(T.er3[:, :, 0, :], T.er[:, :, :]))
    link(dve.tensor_tensor(tmp, T.er[:, :, :], T.er3[:, :, 0, :], ALU.subtract))
    link(dve.tensor_copy(T.er3[:, :, 1, :], tmp))
    link(dve.tensor_tensor(tmp, tmp, T.er3[:, :, 1, :], ALU.subtract))
    link(dve.tensor_copy(T.er3[:, :, 2, :], tmp))


def weights(nc, T, W, al, ar, wkv_t):
    with ExitStack() as ctx:
        def sb(name, shape, dt=F32):
            return ctx.enter_context(nc.sbuf_tensor(name, shape, dt))

        w_in = sb("w_in", [P, LAYERS, FC, FEAT])
        a_in = sb("a_in", [P, 2, LAYERS, FEAT])
        prod = sb("prod", [P, FC, FEAT])
        mean = sb("mean", [P, FC, 2 * MH])
        loaded = ctx.enter_context(nc.semaphore("w_loaded"))
        step = ctx.enter_context(nc.semaphore("w_step"))
        with nc.Block() as block:
            @block.sync
            def _(sp):
                sp.dma_start(w_in[:, :, :, :], W.rearrange("l (c p) n -> p l c n", p=P)).then_inc(loaded, 16)
                for j, a in enumerate((al, ar)):
                    sp.dma_start(a_in[:, j, :, :], a.rearrange("l h d -> l (h d)")[None, :, :]
                                 .to_broadcast([P, LAYERS, FEAT])).then_inc(loaded, 16)
                sp.dma_start(T.wkv[:, :, :], wkv_t.rearrange("(c p) n -> p c n", p=P)).then_inc(loaded, 16)

            @block.vector
            def _(dve):
                n = [0]

                def link(ins):
                    n[0] += 1
                    ins.then_inc(step, 1)
                    dve.wait_ge(step, n[0])

                dve.wait_ge(loaded, 64)
                for l in range(LAYERS):
                    for c in range(FC):
                        w = T.wext[:, l, c, 0:ROW].rearrange("p (h k) -> p h k", k=HD + 1)
                        link(dve.tensor_copy(w[:, :, 0:HD], heads_of(w_in[:, l, c, :], HD)))
                        for j, out in ((0, w[:, :, HD:HD + 1]), (1, T.wext[:, l, c, ROW:EXT].unsqueeze(2))):
                            link(dve.tensor_tensor(prod[:, c, :], w_in[:, l, c, :], a_in[:, j, l, :], ALU.mult))
                            link(dve.tensor_reduce(out, heads_of(prod[:, c, :], HD), AX.X, ALU.add))
                wk = T.wkv[:, :, :].rearrange("p c (h d) -> p c h d", d=MD)
                link(dve.tensor_reduce(mean[:, :, :].unsqueeze(3), wk, AX.X, ALU.add))
                link(dve.tensor_scalar(mean[:, :, :], mean[:, :, :], 1.0 / MD, None, ALU.mult))
                for c in range(FC):
                    link(dve.tensor_tensor(wk[:, c], wk[:, c], mean[:, c, :].unsqueeze(2)
                                           .to_broadcast([P, 2 * MH, MD]), ALU.subtract))


def first_nodes(nc, T, x):
    with ExitStack() as ctx:
        def sb(name, shape, dt=F32):
            return ctx.enter_context(nc.sbuf_tensor(name, shape, dt))

        def sem(name):
            return ctx.enter_context(nc.semaphore(name))

        def ps(name, shape):
            return ctx.enter_context(nc.psum_tensor(name, shape, F32))

        S = 2
        xs = sb("xs", [P, S, FEAT])
        st = sb("st", [P, S, 6])
        mv = sb("mv", [P, S, 2])
        sd = sb("sd", [P, S, 2])
        xn = sb("xn", [P, S, FEAT])
        xt = sb("xt", [P, S, FC, P])
        rows = sb("rows", [P, S, ROW])
        kc = sb("kc", [P, S, INNER])
        vc = sb("vc", [P, S, INNER])
        sq = sb("sq", [P, S, 2 * INNER])
        var = sb("var", [P, S, 2 * MH])
        dev = sb("dev", [P, S, 2 * MH])
        wt = sb("wt", [P, S, MH])
        tmp = sb("tmp", [P, NT, HEADS])
        xt_ps = ps("xt_ps", [P, FC * P])
        kv_ps = [ps("k_ps", [P, INNER]), ps("v_ps", [P, INNER])]
        row_ps = ps("row_ps", [P, EXT])
        dot_ps = ps("dot_ps", [P, PAIRS * P])
        x_in = [sem(f"n_x_in{u}") for u in range(S)]
        row_stored = [sem(f"n_row_stored{u}") for u in range(S)]
        xt_stored = [sem(f"n_xt_stored{u}") for u in range(S)]
        stat, var_eps, rooted, inv, xn_done, turned, xt_done, kv_done, row_done, row_out, er_done, \
            squared, k_out, sums, sums2, rooted2, inv2, wt_done, v_done, dots, added, split, passed = map(sem, (
                "n_stat", "n_var_eps", "n_rooted", "n_inv", "n_xn", "n_turned", "n_xt", "n_kv", "n_row",
                "n_row_out", "n_er", "n_squared", "n_k_out", "n_sums", "n_sums2",
                "n_rooted2", "n_inv2", "n_wt", "n_v", "n_dots", "n_added", "n_split", "n_passed"))

        with nc.Block() as block:
            @block.sync
            def _(sp):
                def step(n, u):
                    need(sp, xn_done, n - 1)
                    sp.dma_start(xs[:, u, :], x[bass.ds(n * P, P), :]).then_inc(x_in[u], 16)
                steps(sp, NT, S, step)

            @block.gpsimd
            def _(pool):
                def step(n, u):
                    need(pool, xt_done, n + 1)
                    pool.dma_start(T.xt_d[bass.ds(n * P, P), :], xt[:, u, :, :].rearrange("p c n -> p (c n)")
                                   ).then_inc(xt_stored[u], 16)
                    need(pool, row_out, n + 1)
                    pool.dma_start(T.rows_d[0][bass.ds(n * P, P), :], rows[:, u, :]).then_inc(row_stored[u], 16)
                steps(pool, NT, S, step)
                for u in range(S):
                    pool.wait_ge(xt_stored[u], 16 * slot_total(NT, u, S))
                    pool.wait_ge(row_stored[u], 16 * slot_total(NT, u, S))

            @block.vector
            def _(dve):
                def norm(n, u):
                    need(dve, x_in[u], (n // 2 if isinstance(n, int) else (n - u) // 2) * 16 + 16)
                    dve.bn_stats(st[:, u, :], xs[:, u, :]).then_inc(stat, 1)
                    need(dve, stat, 2 * n + 1)
                    dve.sem_inc(passed, 1)
                    dve.bn_aggr(mv[:, u, :], st[:, u, :]).then_inc(stat, 1)
                    need(dve, stat, 2 * n + 2)
                    need(dve, rooted, n - 1)
                    dve.tensor_scalar(sd[:, u, 0:1], mv[:, u, 1:2], EPS, None, ALU.add).then_inc(var_eps, 1)

                def norm_end(n, u):
                    need(dve, rooted, n + 1)
                    dve.reciprocal(sd[:, u, 1:2], sd[:, u, 1:2]).then_inc(inv, 1)
                    need(dve, inv, n + 1)
                    need(dve, turned, n - 1)
                    dve.tensor_scalar(xn[:, u, :], xs[:, u, :], mv[:, u, 0:1], sd[:, u, 1:2], ALU.subtract,
                                      ALU.mult).then_inc(xn_done, 1)

                def mix(n, u):
                    need(dve, squared, 2 * n + 2)
                    dve.tensor_reduce(var[:, u, :].unsqueeze(2), sq[:, u, :].rearrange("p (h d) -> p h d", d=MD),
                                      AX.X, ALU.add).then_inc(sums, 1)
                    need(dve, sums, n + 1)
                    dve.tensor_scalar(var[:, u, :], var[:, u, :], 1.0 / MD, EPS, ALU.mult, ALU.add).then_inc(sums2, 1)

                def mix_end(n, u):
                    need(dve, rooted2, n + 1)
                    dve.reciprocal(dev[:, u, :], dev[:, u, :]).then_inc(inv2, 1)
                    need(dve, inv2, n + 1)
                    dve.tensor_tensor(wt[:, u, :], dev[:, u, 0:MH], dev[:, u, MH:2 * MH], ALU.mult).then_inc(wt_done, 1)
                    need(dve, wt_done, n + 1)
                    need(dve, dots, n - 1)
                    dve.tensor_tensor(vc[:, u, :].rearrange("p (h d) -> p h d", d=MD),
                                      kv_ps[1][:, :].rearrange("p (h d) -> p h d", d=MD),
                                      wt[:, u, :].unsqueeze(2).to_broadcast([P, MH, MD]), ALU.mult).then_inc(v_done, 1)

                def add(n):
                    need(dve, dots, n + 1)
                    need(dve, added, n + 1)
                    dve.tensor_tensor(T.dots[:, :], T.dots[:, :], dot_ps[:, :], ALU.add).then_inc(added, 1)

                dve.memset(T.dots[:, :], 0.0).then_inc(added, 1)
                norm(0, 0)
                norm_end(0, 0)

                def step(n, u):
                    more = not isinstance(n, int) or n + 1 < NT
                    if more:
                        norm(n + 1, 1 - u)
                    mix(n, u)
                    if more:
                        norm_end(n + 1, 1 - u)
                    if not isinstance(n, int) or n > 0:
                        add(n - 1)
                    mix_end(n, u)
                steps(dve, NT, S, step, tail=1)
                add(NT - 1)
                dve.wait_ge(er_done, NT)
                split_er(dve, T, tmp[:, :, :], split, 0)

            @block.scalar
            def _(act):
                def root(n, u):
                    need(act, var_eps, n + 1)
                    need(act, inv, n - 1)
                    nc.scalar.activation(sd[:, u, 1:2], sd[:, u, 0:1], ACT.Sqrt).then_inc(rooted, 1)

                root(0, 0)

                def step(n, u):
                    need(act, turned, n + 1)
                    need(act, row_done, n - 1)
                    need(act, xt_stored[u], 16 * uses(n, u, S))
                    nc.scalar.activation(xt[:, u, :, :].rearrange("p c n -> p (c n)"), xt_ps[:, :],
                                         ACT.Copy).then_inc(xt_done, 1)
                    if not isinstance(n, int) or n + 1 < NT:
                        root(n + 1, 1 - u)
                    need(act, sums, n - 1)
                    need(act, kv_done, 2 * n + 1)
                    nc.scalar.activation(sq[:, u, 0:INNER], kv_ps[0][:, :], ACT.Square).then_inc(squared, 1)
                    need(act, kv_done, 2 * n + 2)
                    nc.scalar.activation(sq[:, u, INNER:2 * INNER], kv_ps[1][:, :], ACT.Square).then_inc(squared, 1)
                    need(act, dots, n - 1)
                    nc.scalar.activation(kc[:, u, :], kv_ps[0][:, :], ACT.Copy).then_inc(k_out, 1)
                    need(act, row_done, n + 1)
                    need(act, row_stored[u], 16 * uses(n, u, S))
                    nc.scalar.activation(rows[:, u, :], row_ps[:, 0:ROW], ACT.Copy).then_inc(row_out, 1)
                    nc.scalar.activation(T.er_flat[:, bass.ds(n * HEADS, HEADS)], row_ps[:, ROW:EXT],
                                         ACT.Copy).then_inc(er_done, 1)
                    need(act, sums2, n + 1)
                    need(act, inv2, n - 1)
                    nc.scalar.activation(dev[:, u, :], var[:, u, :], ACT.Sqrt).then_inc(rooted2, 1)
                steps(act, NT, S, step, tail=1)

            @block.tensor
            def _(pe):
                def step(n, u):
                    need(pe, xn_done, n + 1)
                    need(pe, xt_done, n)
                    for c in range(FC):
                        t = nc.tensor.transpose(xt_ps[:, c * P:(c + 1) * P], xn[:, u, c * P:(c + 1) * P], T.ident[:, :])
                    t.then_inc(turned, 1)
                    if not isinstance(n, int) or n > 0:
                        dot(n - 1, 1 - u)
                    need(pe, xt_done, n + 1)
                    need(pe, k_out, n)
                    need(pe, v_done, n)
                    for j in range(2):
                        for c in range(FC):
                            t = nc.tensor.matmul(kv_ps[j][:, :], xt[:, u, c, :],
                                                 T.wkv[:, c, j * INNER:(j + 1) * INNER],
                                                 start=(c == 0), stop=(c == FC - 1))
                        t.then_inc(kv_done, 1)
                    need(pe, row_out, n)
                    need(pe, er_done, n)
                    for c in range(FC):
                        t = nc.tensor.matmul(row_ps[:, :], xt[:, u, c, :], T.wext[:, 0, c, :],
                                             start=(c == 0), stop=(c == FC - 1))
                    t.then_inc(row_done, 1)

                def dot(n, u):
                    need(pe, v_done, n + 1)
                    need(pe, k_out, n + 1)
                    need(pe, added, n + 1)
                    for q in range(PAIRS):
                        t = nc.tensor.matmul(dot_ps[:, q * P:(q + 1) * P], vc[:, u, q * P:(q + 1) * P],
                                             kc[:, u, q * P:(q + 1) * P], start=True, stop=True)
                    t.then_inc(dots, 1)

                steps(pe, NT, S, step, tail=1)
                dot(NT - 1, (NT - 1) % S)


def mix_matrix(nc, T, wq, wo_t):
    with ExitStack() as ctx:
        def sb(name, shape, dt=F32):
            return ctx.enter_context(nc.sbuf_tensor(name, shape, dt))

        wq_sb = sb("wq_sb", [P, PAIRS, FEAT])
        wo_sb = sb("wo_sb", [P, PAIRS, FEAT])
        diag = sb("diag", [P, PAIRS, P])
        a_sb = sb("a_sb", [P, PAIRS, FEAT])
        a_ps = [ctx.enter_context(nc.psum_tensor(f"a_ps{q}", [P, FEAT], F32)) for q in range(PAIRS)]
        g_ps = [ctx.enter_context(nc.psum_tensor(f"g_ps{q}", [P, FEAT], F32)) for q in range(FC)]
        loaded, cleared, diag_done, a_done, a_out, g_done, g_out = [
            ctx.enter_context(nc.semaphore("m_" + s)) for s in
            ("loaded", "cleared", "diag", "a", "a_out", "g", "g_out")]
        with nc.Block() as block:
            @block.sync
            def _(sp):
                sp.dma_start(wq_sb[:, :, :], wq.rearrange("(q p) n -> p q n", p=P)).then_inc(loaded, 16)
                sp.dma_start(wo_sb[:, :, :], wo_t.rearrange("(q p) n -> p q n", p=P)).then_inc(loaded, 16)

            @block.vector
            def _(dve):
                dve.memset(diag[:, :, :], 0.0).then_inc(cleared, 1)
                dve.wait_ge(cleared, 1)
                d = T.dots[:, :].rearrange("p (q n) -> p q n", n=P)
                for h in range(2):
                    s = slice(h * MD, (h + 1) * MD)
                    dve.tensor_scalar(diag[s, :, s], d[s, :, s], 1.0 / NODES, None, ALU.mult).then_inc(diag_done, 1)
                for q in range(PAIRS):
                    dve.wait_ge(a_done, q + 1)
                    dve.tensor_copy(a_sb[:, q, :], a_ps[q][:, :]).then_inc(a_out, 1)
                for c in range(FC):
                    dve.wait_ge(g_done, c + 1)
                    dve.tensor_copy(T.mixw[:, c, :], g_ps[c][:, :]).then_inc(g_out, 1)

            @block.tensor
            def _(pe):
                pe.wait_ge(loaded, 32)
                pe.wait_ge(diag_done, 2)
                for q in range(PAIRS):
                    nc.tensor.matmul(a_ps[q][:, :], diag[:, q, :], wo_sb[:, q, :], start=True,
                                     stop=True).then_inc(a_done, 1)
                pe.wait_ge(a_out, PAIRS)
                for c in range(FC):
                    for q in range(PAIRS):
                        t = nc.tensor.matmul(g_ps[c][:, :], wq_sb[:, q, c * P:(c + 1) * P], a_sb[:, q, :],
                                             start=(q == 0), stop=(q == PAIRS - 1))
                    t.then_inc(g_done, 1)


def edge_pass(nc, T, S, l):
    N0 = l * NB
    GS = SLOTS

    def landed(n, u):
        return (NB // GS) * l + uses(n, u, GS) + 1

    with nc.Block() as block:
        @block.gpsimd
        def _(pool):
            def fetch_indices(n, u):
                if not isinstance(n, int) or landed(n, u) > 1:
                    need(pool, S.gathered[u], 16 * BT * (landed(n, u) - 1))
                pool.tensor_copy(S.idx[:, u, :], T.src_t[:, bass.ds(n, 1), :].rearrange("p a j -> p (a j)")
                                 ).then_inc(S.idx_ready, 1)

            if l == 0:
                pool.memset(T.acc[:, :], 0.0).then_inc(S.acc_cleared, 1)
            fetch_indices(0, 0)

            def step(n, u):
                if not isinstance(n, int) or n + 1 < NB:
                    fetch_indices(n + 1, (u + 1) % GS)
                need(pool, S.summed, N0 + n - GS + 1)
                need(pool, S.idx_ready, N0 + n + 1)
                pool.sem_inc(S.issuing, 1)
                for j in range(BT):
                    pool.indirect_dma_start(
                        S.rows[:, u, j, :], None, T.rows_d[l],
                        bass.IndirectOffsetOnAxis(ap=S.idx[:, u, j:j + 1].bitcast(U32), axis=0),
                    ).then_inc(S.gathered[u], 16)
            steps(pool, NB, GS, step, tail=1)

        @block.sync
        def _(sp):
            def step(n, u):
                need(sp, S.resc_made, N0 + n - GS + 1)
                sp.dma_start(S.loc_row[:, u, :], T.loc_d[bass.ds(n * BE, BE)][None, :].to_broadcast([P, BE])
                             ).then_inc(S.tables[u], 16)
                sp.dma_start(S.flags[:, u, :], T.flag_d[bass.ds(n * BE, BE + 1)][None, :]
                             .to_broadcast([HEADS, BE + 1])).then_inc(S.tables[u], 16)
            steps(sp, NB, GS, step, tail=1)

        @block.vector
        def _(dve):
            def one_hot_t(n, u):
                need(dve, S.tables[u], 32 * landed(n, u))
                need(dve, S.er_ready, N0 + n - 1)
                dve.tensor_scalar(S.hot_t[:, u % 2, :], S.loc_row[:, u, :], T.col[:, 0:1], None,
                                  ALU.is_equal).then_inc(S.hot_t_ready, 1)

            def er_by_edge(n, u):
                need(dve, S.er_ready, N0 + n + 1)
                dve.tensor_reduce(heads_of(S.er_e[:, :], HEADS).unsqueeze(3),
                                  S.er_ps[u % 2][:, 0:BT * 3 * HEADS].rearrange("p (v k h) -> p v h k", k=3, h=HEADS),
                                  AX.X, ALU.add).then_inc(S.er_summed, 1)

            def add_el(n, u):
                need(dve, S.er_summed, N0 + n + 1)
                need(dve, S.gathered[u], 16 * BT * landed(n, u))
                el = S.rows[:, u, :, :].rearrange("p v (h k) -> p v h k", k=HD + 1)[:, :, :, HD]
                dve.tensor_tensor(heads_of(S.pre[:, :], HEADS), el, heads_of(S.er_e[:, :], HEADS),
                                  ALU.add).then_inc(S.pre_ready, 1)

            def leaky(n, u):
                need(dve, S.pre_ready, N0 + n + 1)
                need(dve, S.below_ready, N0 + n - 1)
                dve.scalar_tensor_tensor(S.e[:, u % 2, :], S.pre[:, :], 0.2, S.pre[:, :], ALU.mult, ALU.max).then_inc(S.e_ready, 1)

            def maxima(n, u, ahead):
                m, b = S.fwd[:, u % 2, :], S.bwd[:, u % 2, :]
                first = isinstance(n, int) and n == 0
                need(dve, S.e_t_ready, N0 + n + 1)
                carry = S.fwd[:, 1 - u % 2, BE - 1:BE]
                dve.tensor_tensor_scan(m, S.flags[:, u, 0:BE], S.e_ps[0:HEADS, :], NEG if first else carry,
                                       ALU.add, ALU.max).then_inc(S.fwd_ready, 1)
                dve.tensor_scalar(S.goes_on[:, :], S.flags[:, u, 0:1], 0.0, None, ALU.is_equal).then_inc(S.flag_read, 1)
                need(dve, S.resc_ready, N0 + n)
                dve.tensor_tensor(S.hot0[:, :], T.row[0:HEADS, :], S.loc_row[0:HEADS, u, 0:1].to_broadcast([HEADS, P]),
                                  ALU.is_equal).then_inc(S.hot0_ready, 1)
                if ahead:
                    one_hot_t(n + 1, (u + 1) % GS)
                need(dve, S.fwd_ready, N0 + n + 1)
                need(dve, S.max_t_ready, N0 + n - 1)
                dve.tensor_tensor_scan(b[:, ::-1], S.flags[:, u, 1:BE + 1][:, ::-1], m[:, ::-1], NEG,
                                       ALU.add, ALU.max).then_inc(S.bwd_ready, 1)

            def drop_of(n, u):
                b = S.bwd[:, u % 2, :]
                first = isinstance(n, int) and n == 0
                carry = b[:, 0:1] if first else S.fwd[:, 1 - u % 2, BE - 1:BE]
                need(dve, S.bwd_ready, N0 + n + 1)
                dve.tensor_tensor(S.drop[:, :], carry, b[:, 0:1], ALU.subtract).then_inc(S.drop_ready, 1)
                need(dve, S.drop_ready, N0 + n + 1)
                need(dve, S.flag_read, N0 + n + 1)
                dve.tensor_scalar(S.drop_diag[:, :], T.ident[0:HEADS, 0:HEADS], S.drop[:, :], S.goes_on[:, :],
                                  ALU.mult, ALU.mult).then_inc(S.resc_made, 1)

            def below_max(n, u):
                need(dve, S.max_t_ready, N0 + n + 1)
                need(dve, S.exp_done, N0 + n - 1)
                dve.tensor_tensor(S.below[:, u % 2, :], S.e[:, u % 2, :], S.max_ps[:, 0:BT * HEADS],
                                  ALU.subtract).then_inc(S.below_ready, 1)

            def window_of(n):
                return dve.value_load(T.win[0:1, bass.ds(n, 1)], min_val=0, max_val=NT - 1)

            def rescale_sum(n, u, d):
                w = T.acc[:, bass.ds(d * ROW, ROW)]
                need(dve, S.resc_exp, N0 + n + 1)
                need(dve, S.added, 2 * (N0 + n))
                dve.tensor_tensor(heads_of(w, HD + 1), heads_of(w, HD + 1),
                                  S.resc[:, u % 2, :].unsqueeze(2).to_broadcast([P, HEADS, HD + 1]),
                                  ALU.mult).then_inc(S.added, 1)

            def add_sum(n, u, d):
                w = T.acc[:, bass.ds(d * ROW, ROW)]
                need(dve, S.summed, N0 + n + 1)
                need(dve, S.added, 2 * (N0 + n) + 1)
                dve.tensor_tensor(w, w, S.sum_ps[u % 2][:, 0:ROW], ALU.add).then_inc(S.added, 1)

            def weigh(n, u):
                need(dve, S.exp_done, N0 + n + 1)
                r = S.rows[:, u, :, :].rearrange("p v (h k) -> p (v h) k", k=HD + 1)
                dve.tensor_tensor(r[:, :, 0:HD], r[:, :, 0:HD], r[:, :, HD:HD + 1].to_broadcast([P, BT * HEADS, HD]),
                                  ALU.mult).then_inc(S.weighted, 1)

            def running(n, u, count):
                has = lambda k: not isinstance(n, int) or 0 <= n + k < count
                nxt, prv = (u + 1) % GS, (u - 2) % GS
                d = window_of(n - 2) if has(-2) else None
                if has(0):
                    maxima(n, u, has(1))
                    drop_of(n, u)
                if has(1):
                    er_by_edge(n + 1, nxt)
                if has(-2):
                    rescale_sum(n - 2, prv, d)
                if has(1):
                    add_el(n + 1, nxt)
                if has(0):
                    below_max(n, u)
                if has(-2):
                    add_sum(n - 2, prv, d)
                if has(1):
                    leaky(n + 1, nxt)

            dve.wait_ge(S.acc_cleared, l + 1)
            one_hot_t(0, 0)
            er_by_edge(0, 0)
            add_el(0, 0)
            leaky(0, 0)
            running(0, 0, NB)

            def step(n, u):
                weigh(n, u)
                running(n + 1, (u + 1) % GS, NB)
            steps(dve, NB, GS, step, tail=2)
            running(NB + 1, 1, NB)
            dve.wait_ge(S.added, 2 * (N0 + NB))

        @block.scalar
        def _(act):
            def one_hot(n, u):
                need(act, S.squares_read, N0 + n)
                for j in range(BT):
                    nc.scalar.activation(S.square[:, j, :], T.row[:, :], ACT.Square,
                                         bias=T.neg_loc[:, bass.ds(n, 1), j]).then_inc(S.squared, 1)
                need(act, S.squared, BT * (N0 + n + 1))
                need(act, S.summed, N0 + n - 1)
                nc.scalar.activation(S.hot[:, u % 2, :, :], S.square[:, :, :], ACT.Relu, scale=-1.0,
                                     bias=T.one[:, 0:1]).then_inc(S.squares_read, 1)

            def rescale(n, u):
                need(act, S.resc_ready, N0 + n + 1)
                need(act, S.added, 2 * (N0 + n - 2) + 1)
                nc.scalar.activation(S.resc[:, u % 2, :], S.resc_ps[:, 0:HEADS], ACT.Exp).then_inc(S.resc_exp, 1)

            def weights_of(n, u):
                need(act, S.below_ready, N0 + n + 1)
                w = S.rows[:, u, :, :].rearrange("p v (h k) -> p (v h) k", k=HD + 1)[:, :, HD]
                nc.scalar.activation(w, S.below[:, u % 2, :], ACT.Exp).then_inc(S.exp_done, 1)

            rescale(0, 0)
            one_hot(0, 0)

            def step(n, u):
                weights_of(n, u)
                if not isinstance(n, int) or n + 1 < NB:
                    one_hot(n + 1, (u + 1) % GS)
                    rescale(n + 1, (u + 1) % GS)
            steps(act, NB, GS, step, tail=1)

        @block.tensor
        def _(pe):
            def window_of(n):
                return pe.value_load(T.win[0:1, bass.ds(n, 1)], min_val=0, max_val=NT - 1)

            def er_by_edge(n, u, d):
                need(pe, S.er_summed, N0 + n - 1)
                need(pe, S.hot_t_ready, N0 + n + 1)
                for v in range(BT):
                    t = nc.tensor.matmul(S.er_ps[u % 2][:, v * 3 * HEADS:(v + 1) * 3 * HEADS],
                                         S.hot_t[:, u % 2, v * P:(v + 1) * P],
                                         T.er3_flat[:, bass.ds(d * 3 * HEADS, 3 * HEADS)], start=True, stop=True)
                t.then_inc(S.er_ready, 1)

            def turn_logits(n, u):
                need(pe, S.fwd_ready, N0 + n)
                need(pe, S.e_ready, N0 + n + 1)
                for v in range(BT):
                    t = nc.tensor.transpose(S.e_ps[0:HEADS, v * P:(v + 1) * P],
                                            S.e[:, u % 2, v * HEADS:(v + 1) * HEADS], T.ident[:, :])
                t.then_inc(S.e_t_ready, 1)

            def turn_maxima(n, u):
                need(pe, S.below_ready, N0 + n)
                need(pe, S.resc_exp, N0 + n)
                need(pe, S.bwd_ready, N0 + n + 1)
                need(pe, S.resc_made, N0 + n + 1)
                nc.tensor.matmul(S.resc_ps[:, 0:HEADS], S.hot0[:, :], S.drop_diag[:, :], start=True,
                                 stop=True).then_inc(S.resc_ready, 1)
                for v in range(BT):
                    t = nc.tensor.transpose(S.max_ps[:, v * HEADS:(v + 1) * HEADS],
                                            S.bwd[:, u % 2, v * P:(v + 1) * P], T.ident[0:HEADS, 0:HEADS])
                t.then_inc(S.max_t_ready, 1)

            def sum_up(n, u, v0, v1):
                if v0 == 0:
                    need(pe, S.squares_read, N0 + n + 1)
                    need(pe, S.weighted, N0 + n + 1)
                    need(pe, S.added, 2 * (N0 + n - 1))
                for v in range(v0, v1):
                    t = nc.tensor.matmul(S.sum_ps[u % 2][:, 0:ROW], S.hot[:, u % 2, v, :], S.rows[:, u, v, :],
                                         start=(v == 0), stop=(v == BT - 1))
                if v1 == BT:
                    t.then_inc(S.summed, 1)

            er_by_edge(0, 0, window_of(0))
            turn_logits(0, 0)
            er_by_edge(1, 1, window_of(1))
            turn_maxima(0, 0)

            def step(n, u):
                more = not isinstance(n, int) or n + 1 < NB
                nxt, prv = (u + 1) % GS, (u - 1) % GS
                if more:
                    turn_logits(n + 1, nxt)
                ahead = not isinstance(n, int) or n + 2 < NB
                d = window_of(n + 2) if ahead else None
                sum_up(n, u, 0, BT // 2)
                if ahead:
                    er_by_edge(n + 2, (u + 2) % GS, d)
                if more:
                    turn_maxima(n + 1, nxt)
                sum_up(n, u, BT // 2, BT)
            steps(pe, NB, GS, step, tail=2)


class EdgeBuffers:

    def __init__(self, nc, ctx):
        def sb(name, shape, dt=F32):
            return ctx.enter_context(nc.sbuf_tensor(name, shape, dt))

        def ps(name, cols=512):
            return ctx.enter_context(nc.psum_tensor(name, [P, cols], F32))

        def sem(name):
            return ctx.enter_context(nc.semaphore("e_" + name))

        self.idx = sb("idx", [P, SLOTS, BT], I32)
        self.rows = sb("g_rows", [P, SLOTS, BT, ROW])
        self.loc_row = sb("loc_row", [P, SLOTS, BE], BF16)
        self.flags = sb("flags", [HEADS, SLOTS, BE + 1])
        self.hot_t = sb("hot_t", [P, 2, BE], BF16)
        self.square = sb("square", [P, BT, P])
        self.hot = sb("hot", [P, 2, BT, P])
        self.er_e = sb("er_e", [P, BT * HEADS])
        self.pre = sb("pre", [P, BT * HEADS])
        self.e = sb("e", [P, 2, BT * HEADS])
        self.below = sb("below_m", [P, 2, BT * HEADS])
        self.fwd = sb("fwd", [HEADS, 2, BE])
        self.bwd = sb("bwd", [HEADS, 2, BE])
        self.goes_on = sb("goes_on", [HEADS, 1])
        self.drop = sb("drop", [HEADS, 1])
        self.drop_diag = sb("drop_diag", [HEADS, HEADS])
        self.hot0 = sb("hot0", [HEADS, P])
        self.resc = sb("resc", [P, 2, HEADS])
        self.e_ps = ps("e_ps", BE)
        self.er_ps = [ps(f"er_ps{i}") for i in range(2)]
        self.max_ps = ps("max_ps")
        self.resc_ps = ps("resc_ps")
        self.sum_ps = [ps(f"sum_ps{i}") for i in range(2)]
        self.acc_cleared = sem("acc_cleared")
        self.idx_ready = sem("idx_ready")
        self.issuing = sem("issuing")
        self.summed = sem("summed")
        self.hot_t_ready = sem("hot_t_ready")
        self.er_ready = sem("er_ready")
        self.er_summed = sem("er_summed")
        self.pre_ready = sem("pre_ready")
        self.e_ready = sem("e_ready")
        self.e_t_ready = sem("e_t_ready")
        self.fwd_ready = sem("fwd_ready")
        self.bwd_ready = sem("bwd_ready")
        self.flag_read = sem("flag_read")
        self.hot0_ready = sem("hot0_ready")
        self.resc_ready = sem("resc_ready")
        self.drop_ready = sem("drop_ready")
        self.resc_made = sem("resc_made")
        self.squared = sem("squared")
        self.squares_read = sem("squares_read")
        self.max_t_ready = sem("max_t_ready")
        self.below_ready = sem("below_ready")
        self.weighted = sem("weighted")
        self.exp_done = sem("exp_done")
        self.resc_exp = sem("resc_exp")
        self.added = sem("added")
        self.gathered = [sem(f"gathered{u}") for u in range(SLOTS)]
        self.tables = [sem(f"tables{u}") for u in range(SLOTS)]


def next_nodes(nc, T, S, l, bias):
    with ExitStack() as ctx:
        def sb(name, shape, dt=F32):
            return ctx.enter_context(nc.sbuf_tensor(f"u{l}_{name}", shape, dt))

        def sem(name):
            return ctx.enter_context(nc.semaphore(f"u{l}_{name}"))

        b_sb = sb("b", [P, FEAT])
        den = sb("den", [P, 2, HEADS])
        y = sb("y", [P, 2, FEAT])
        z = sb("z", [P, 2, FEAT])
        zt = sb("zt", [P, 2, FC, P])
        rows = sb("rows", [P, 2, ROW])
        tmp = sb("tmp", [P, NT, HEADS])
        zt_ps = [S.sum_ps[0], S.sum_ps[1]]
        row_ps = S.er_ps
        loaded, den1, den2, div, biased, leaky, turned, zt_done, row_done, row_out, er_done, split = map(sem, (
            "loaded", "den1", "den2", "div", "biased", "leaky", "turned", "zt", "row", "row_out", "er",
            "split"))
        stored = [sem("stored0"), sem("stored1")]
        with nc.Block() as block:
            @block.sync
            def _(sp):
                sp.dma_start(b_sb[:, :], bias[l:l + 1, :].to_broadcast([P, FEAT])).then_inc(loaded, 16)

                def step(n, u):
                    need(sp, row_out, n + 1)
                    sp.dma_start(T.rows_d[l + 1][bass.ds(n * P, P), :], rows[:, u, :]).then_inc(stored[u], 16)
                steps(sp, NT, 2, step)
                for u in range(2):
                    sp.wait_ge(stored[u], 16 * slot_total(NT, u, 2))

            @block.vector
            def _(dve):
                dve.wait_ge(loaded, 16)

                def step(n, u):
                    w = heads_of(T.acc[:, bass.ds(n * ROW, ROW)], HD + 1)
                    dve.tensor_scalar(den[:, u, :].unsqueeze(2), w[:, :, HD:HD + 1], 1e-30, None,
                                      ALU.max).then_inc(den1, 1)
                    need(dve, den1, n + 1)
                    dve.reciprocal(den[:, u, :], den[:, u, :]).then_inc(den2, 1)
                    need(dve, den2, n + 1)
                    dve.tensor_tensor(heads_of(y[:, u, :], HD), w[:, :, 0:HD],
                                      den[:, u, :].unsqueeze(2).to_broadcast([P, HEADS, HD]), ALU.mult).then_inc(div, 1)
                    need(dve, div, n + 1)
                    dve.tensor_tensor(y[:, u, :], y[:, u, :], b_sb[:, :], ALU.add).then_inc(biased, 1)
                    need(dve, biased, n + 1)
                    need(dve, turned, n - 1)
                    dve.scalar_tensor_tensor(z[:, u, :], y[:, u, :], 0.01, y[:, u, :], ALU.mult,
                                             ALU.max).then_inc(leaky, 1)
                steps(dve, NT, 2, step)
                dve.wait_ge(er_done, NT)
                split_er(dve, T, tmp[:, :, :], split, 0)

            @block.scalar
            def _(act):
                def step(n, u):
                    need(act, turned, n + 1)
                    need(act, row_done, n - 1)
                    nc.scalar.activation(zt[:, u, :, :].rearrange("p c n -> p (c n)"), zt_ps[u][:, 0:FEAT],
                                         ACT.Copy).then_inc(zt_done, 1)
                    need(act, row_done, n + 1)
                    need(act, stored[u], 16 * uses(n, u, 2))
                    nc.scalar.activation(rows[:, u, :], row_ps[u][:, 0:ROW], ACT.Copy).then_inc(row_out, 1)
                    nc.scalar.activation(T.er_flat[:, bass.ds(n * HEADS, HEADS)], row_ps[u][:, ROW:EXT],
                                         ACT.Copy).then_inc(er_done, 1)
                steps(act, NT, 2, step)

            @block.tensor
            def _(pe):
                def step(n, u):
                    turn(n, u)
                    if not isinstance(n, int) or n > 0:
                        row(n - 1, 1 - u)

                def turn(n, u):
                    need(pe, leaky, n + 1)
                    need(pe, zt_done, n - 1)
                    for c in range(FC):
                        t = nc.tensor.transpose(zt_ps[u][:, c * P:(c + 1) * P], z[:, u, c * P:(c + 1) * P],
                                                T.ident[:, :])
                    t.then_inc(turned, 1)

                def row(n, u):
                    need(pe, zt_done, n + 1)
                    need(pe, er_done, n - 1)
                    for c in range(FC):
                        t = nc.tensor.matmul(row_ps[u][:, 0:EXT], zt[:, u, c, :], T.wext[:, l + 1, c, :],
                                             start=(c == 0), stop=(c == FC - 1))
                    t.then_inc(row_done, 1)
                steps(pe, NT, 2, step)
                row(NT - 1, (NT - 1) % 2)

            @block.gpsimd
            def _(pool):
                pool.wait_ge(div, NT)
                pool.memset(T.acc[:, :], 0.0).then_inc(S.acc_cleared, 1)


def feed_forward(nc, T, bias, x, bout, router_t, w1, b1, w2, b2, out):
    with ExitStack() as ctx:
        T.tok_t = ctx.enter_context(nc.sbuf_tensor("tok_t", [P, FC, NODES_PAD], F32))
        T.comb = ctx.enter_context(nc.sbuf_tensor("comb", [P, NT, EXPERTS], F32))
        T.ps = [ctx.enter_context(nc.psum_tensor(f"f_ps{i}", [P, 2048], F32)) for i in range(2)]
        tokens(nc, T, bias, x, bout, router_t)
        experts(nc, T, w1, b1, w2, b2, out)


def tokens(nc, T, bias, x, bout, router_t):
    with ExitStack() as ctx:
        def sb(name, shape, dt=F32):
            return ctx.enter_context(nc.sbuf_tensor("k_" + name, shape, dt))

        def sem(name):
            return ctx.enter_context(nc.semaphore("k_" + name))

        G = CHUNK_TILES
        CHUNKS = NT // G
        LOTS = -(-G // 2)
        half = [(0, (G + 1) // 2), ((G + 1) // 2, G)]
        biases = sb("biases", [2, FEAT])
        ones = sb("ones", [2, P])
        rt_sb = sb("rt", [P, FC, EXPERTS])
        xin = sb("x", [P, 2, G, FEAT])
        xt = sb("xt", [P, 2, G, FEAT])
        den = sb("den", [P, G * HEADS])
        tok = sb("tok", [P, G, FEAT])
        st = sb("st", [P, G, 6])
        mv = sb("mv", [P, G, 2])
        sd = sb("sd", [P, G])
        inv = sb("inv", [P, G])
        lgt = sb("lgt", [EXPERTS, G * P])
        lg = sb("lg", [P, NT, EXPERTS])
        prob = sb("prob", [P, NT, EXPERTS])
        rank = sb("rank", [P, EXPERTS])
        pick = [sb(f"pick{i}", [P, NT, EXPERTS]) for i in range(2)]
        top = [sb(f"top{i}", [P, NT]) for i in range(2)]
        red = sb("red", [P, NT])
        mix_ps = T.ps[0]
        turn_ps, lgt_ps = T.ps[1][:, 0:1024], T.ps[1][:, 1024:2048]
        loaded, mixed, front, rooted, turned, tt_done, lgt_done, lgt_out, lg_done, lg_copied, exp_done, pick_step, \
            ready, passed = map(sem, ("loaded", "mixed", "front", "rooted", "turned", "tt", "lgt", "lgt_out",
                                      "lg", "lg_copied", "exp", "pick", "ready", "passed"))
        x_in = [sem("x_in0"), sem("x_in1")]
        K_MIX, K_VAR, K_TOK = 4, 6 + 2 * G, 7 + 3 * G
        K = K_TOK + 1

        with nc.Block() as block:
            @block.sync
            def _(sp):
                sp.dma_start(biases[0:1, :], bias[LAYERS - 1:LAYERS, :]).then_inc(loaded, 16)
                sp.dma_start(biases[1:2, :], bout[None, :]).then_inc(loaded, 16)
                sp.dma_start(rt_sb[:, :, :], router_t.rearrange("(c p) n -> p c n", p=P)).then_inc(loaded, 16)

                def step(n, u):
                    need(sp, front, K * (n - 1))
                    for to, rows in ((xin, x), (xt, T.xt_d)):
                        sp.dma_start(to[:, u, :, :], rows[bass.ds(n * G * P, G * P), :]
                                     .rearrange("(t p) f -> p t f", p=P)).then_inc(x_in[u], 16)
                steps(sp, CHUNKS, 2, step)

            @block.gpsimd
            def _(pool):
                pool.memset(ones[:, :], 1.0).then_inc(ready, 1)

            @block.vector
            def _(dve):
                def copy_logits(n):
                    need(dve, lg_done, n + 1)
                    dve.tensor_copy(lg[:, bass.ds(n * G, G), :], turn_ps[:, 0:G * EXPERTS]
                                    .rearrange("p (t e) -> p t e", e=EXPERTS)).then_inc(lg_copied, 1)

                def step(n, u):
                    k = [0]

                    def done(ins, wait=True):
                        k[0] += 1
                        ins.then_inc(front, 1)
                        if wait:
                            dve.wait_ge(front, K * n + k[0])

                    chunk = T.acc[:, bass.ds(n * G * ROW, G * ROW)]
                    w = heads_of(chunk, HD + 1)
                    y = xin[:, u, :, :]
                    done(dve.tensor_scalar(den[:, :].unsqueeze(2), w[:, :, HD:HD + 1], 1e-30, None, ALU.max))
                    done(dve.reciprocal(den[:, :], den[:, :]))
                    if not isinstance(n, int) or n > 0:
                        copy_logits(n - 1)
                    need(dve, turned, LOTS * n)
                    done(dve.tensor_tensor(tok[:, :, :].rearrange("p t (h k) -> p (t h) k", k=HD), w[:, :, 0:HD],
                                           den[:, :].unsqueeze(2).to_broadcast([P, G * HEADS, HD]), ALU.mult),
                         wait=False)
                    need(dve, x_in[u], (uses(n, u, 2) + 1) * 32)
                    need(dve, mixed, n + 1)
                    done(dve.tensor_tensor(y, y, mix_ps[:, 0:G * FEAT].rearrange("p (t f) -> p t f", f=FEAT), ALU.add))
                    assert k[0] == K_MIX
                    done(dve.tensor_tensor(y, y, tok[:, :, :], ALU.add))
                    for t in range(G):
                        done(dve.bn_stats(st[:, t, :], y[:, t, :]), wait=t == G - 1)
                    dve.sem_inc(passed, 1)
                    for t in range(G):
                        done(dve.bn_aggr(mv[:, t, :], st[:, t, :]), wait=t == G - 1)
                    done(dve.tensor_scalar(sd[:, :].unsqueeze(2), mv[:, :, 1:2], EPS, None, ALU.add), wait=False)
                    assert k[0] == K_VAR
                    need(dve, rooted, n + 1)
                    done(dve.reciprocal(inv[:, :], inv[:, :]))
                    for t in range(G):
                        done(dve.tensor_scalar(tok[:, t, :], y[:, t, :], mv[:, t, 0:1], inv[:, t:t + 1],
                                               ALU.subtract, ALU.mult), wait=t == G - 1)
                    assert k[0] == K_TOK
                    done(dve.tensor_tensor(chunk.rearrange("p (t r) -> p t r", r=ROW)[:, :, 0:FEAT], y, tok[:, :, :],
                                           ALU.add), wait=False)
                    assert k[0] == K
                dve.wait_ge(loaded, 48)
                steps(dve, CHUNKS, 2, step)
                copy_logits(CHUNKS - 1)
                dve.wait_ge(lg_copied, CHUNKS)

                def link(ins):
                    k[0] += 1
                    ins.then_inc(pick_step, 1)
                    dve.wait_ge(pick_step, k[0])

                k = [0]
                wide = [P, NT, EXPERTS]
                link(dve.tensor_reduce(red[:, :].unsqueeze(2), lg[:, :, :], AX.X, ALU.max))
                link(dve.tensor_tensor(lg[:, :, :], lg[:, :, :], red[:, :].unsqueeze(2).to_broadcast(wide),
                                       ALU.subtract))
                assert k[0] == 2
                dve.wait_ge(exp_done, 1)
                link(dve.tensor_reduce(red[:, :].unsqueeze(2), prob[:, :, :], AX.X, ALU.add))
                link(dve.reciprocal(red[:, :], red[:, :]))
                link(dve.tensor_tensor(prob[:, :, :], prob[:, :, :], red[:, :].unsqueeze(2).to_broadcast(wide),
                                       ALU.mult))
                link(dve.tensor_scalar(rank[:, :], T.row[:, 0:EXPERTS], float(EXPERTS), None, ALU.subtract))
                ranks = rank[:, :].unsqueeze(1).to_broadcast(wide)
                for i in range(2):
                    link(dve.tensor_reduce(top[i][:, :].unsqueeze(2), prob[:, :, :], AX.X, ALU.max))
                    link(dve.tensor_tensor(lg[:, :, :], prob[:, :, :], top[i][:, :].unsqueeze(2).to_broadcast(wide),
                                           ALU.is_equal))
                    link(dve.tensor_tensor(lg[:, :, :], lg[:, :, :], ranks, ALU.mult))
                    link(dve.tensor_reduce(red[:, :].unsqueeze(2), lg[:, :, :], AX.X, ALU.min))
                    link(dve.tensor_tensor(pick[i][:, :, :], ranks, red[:, :].unsqueeze(2).to_broadcast(wide),
                                           ALU.is_equal))
                    if i == 0:
                        link(dve.scalar_tensor_tensor(prob[:, :, :], pick[0][:, :, :], -2.0, prob[:, :, :],
                                                      ALU.mult, ALU.add))
                link(dve.tensor_tensor(red[:, :], top[0][:, :], top[1][:, :], ALU.add))
                link(dve.tensor_scalar(red[:, :], red[:, :], 1e-12, None, ALU.max))
                link(dve.reciprocal(red[:, :], red[:, :]))
                for i in range(2):
                    link(dve.tensor_tensor(top[i][:, :], top[i][:, :], red[:, :], ALU.mult))
                    link(dve.tensor_tensor(pick[i][:, :, :], pick[i][:, :, :],
                                           top[i][:, :].unsqueeze(2).to_broadcast(wide), ALU.mult))
                link(dve.tensor_tensor(T.comb[:, :, :], pick[0][:, :, :], pick[1][:, :, :], ALU.add))

            @block.scalar
            def _(act):
                def step(n, u):
                    need(act, front, K * n + K_VAR)
                    nc.scalar.activation(inv[:, :], sd[:, :], ACT.Sqrt).then_inc(rooted, 1)
                    for k in range(LOTS):
                        m = min(2, G - 2 * k)
                        need(act, turned, LOTS * n + k + 1)
                        nc.scalar.activation(T.tok_t[:, :, bass.ds((n * G + 2 * k) * P, m * P)],
                                             turn_ps[:, (k % 2) * 512:(k % 2) * 512 + FC * m * P]
                                             .rearrange("p (c n) -> p c n", c=FC), ACT.Copy).then_inc(tt_done, 1)
                    need(act, lgt_done, n + 1)
                    need(act, lg_done, n)
                    for j, (t0, t1) in enumerate(half):
                        nc.scalar.activation(lgt[:, t0 * P:t1 * P], lgt_ps[0:EXPERTS, j * 512:j * 512 + (t1 - t0) * P],
                                             ACT.Copy).then_inc(lgt_out, 1)
                steps(act, CHUNKS, 2, step)
                act.wait_ge(pick_step, 2)
                nc.scalar.activation(prob[:, :, :], lg[:, :, :], ACT.Exp).then_inc(exp_done, 1)

            @block.tensor
            def _(pe):
                def mix(n, u):
                    need(pe, x_in[u], (uses(n, u, 2) + 1) * 32)
                    need(pe, front, K * (n - 1) + K_MIX)
                    for t in range(G):
                        to = mix_ps[:, t * FEAT:(t + 1) * FEAT]
                        for c in range(FC):
                            nc.tensor.matmul(to, xt[:, u, t, c * P:(c + 1) * P], T.mixw[:, c, :], start=(c == 0),
                                             stop=False)
                        m = nc.tensor.matmul(to, ones[:, :], biases[:, :], start=False, stop=True)
                    m.then_inc(mixed, 1)

                pe.wait_ge(loaded, 48)
                pe.wait_ge(ready, 1)
                mix(0, 0)

                def step(n, u):
                    if not isinstance(n, int) or n + 1 < CHUNKS:
                        mix(n + 1, 1 - u)
                    need(pe, front, K * n + K_TOK)
                    need(pe, lg_copied, n)
                    pe.sem_inc(passed, 1)
                    for k in range(LOTS):
                        m = min(2, G - 2 * k)
                        if k >= 2 or not isinstance(n, int) or n > 0:
                            pe.wait_ge(tt_done, LOTS * n + k - 1)
                            pe.sem_inc(passed, 1)
                        for c in range(FC):
                            for t in range(m):
                                at = (k % 2) * 512 + (c * m + t) * P
                                i = nc.tensor.transpose(turn_ps[:, at:at + P], tok[:, 2 * k + t, c * P:(c + 1) * P],
                                                        T.ident[:, :])
                        i.then_inc(turned, 1)
                    need(pe, tt_done, LOTS * (n + 1))
                    need(pe, lgt_out, 2 * n)
                    for j, (t0, t1) in enumerate(half):
                        for c in range(FC):
                            i = nc.tensor.matmul(lgt_ps[0:EXPERTS, j * 512:j * 512 + (t1 - t0) * P], rt_sb[:, c, :],
                                                 T.tok_t[:, c, bass.ds((n * G + t0) * P, (t1 - t0) * P)],
                                                 start=(c == 0), stop=(c == FC - 1))
                    i.then_inc(lgt_done, 1)
                    need(pe, lgt_out, 2 * n + 2)
                    pe.sem_inc(passed, 1)
                    for t in range(G):
                        i = nc.tensor.transpose(turn_ps[:, t * EXPERTS:(t + 1) * EXPERTS], lgt[:, t * P:(t + 1) * P],
                                                T.ident[0:EXPERTS, 0:EXPERTS])
                    i.then_inc(lg_done, 1)
                steps(pe, CHUNKS, 2, step, tail=1)


def experts(nc, T, w1, b1, w2, b2, out):
    with ExitStack() as ctx:
        def sb(name, shape, dt=F32):
            return ctx.enter_context(nc.sbuf_tensor("f_" + name, shape, dt))

        def sem(name):
            return ctx.enter_context(nc.semaphore("f_" + name))

        B = 4
        G = CHUNK_TILES
        CHUNKS = NT // G
        FULL = NT // B
        REST = NT - FULL * B
        UNITS = FULL + 1
        assert REST in (1, 2) and FULL % 2 == 0
        w1_sb = sb("w1", [P, EXPERTS, FC, FEAT])
        w2_sb = sb("w2", [P, EXPERTS, FC, FEAT])
        b1_sb = sb("b1", [P, EXPERTS, FC])
        b2_sb = sb("b2", [EXPERTS, FEAT])
        share = sb("share", [P, 2, G * EXPERTS])
        share_t = sb("share_t", [EXPERTS, 2, G * P])
        hid = sb("hid", [P, 2, FC, B * P])
        h_ps, y_ps = T.ps
        loaded, share_in, share_turned, share_out, b2_done, b2_added, hidden, gelu, multiplied, added, stored, \
            passed = map(sem, ("loaded", "share_in", "share_turned", "share_out", "b2d", "b2_added", "hidden",
                               "gelu", "mult", "added", "stored", "passed"))
        w_in = [sem(f"w_in{e}") for e in range(EXPERTS)]

        def over_blocks(eng, e, unit):
            steps(eng, FULL, 2, lambda i, u: unit(i, (e * UNITS + u) % 2, B), tail=1)
            unit(FULL, (e * UNITS + FULL) % 2, REST)

        with nc.Block() as block:
            @block.sync
            def _(sp):
                sp.dma_start(b2_sb[:, :], b2).then_inc(loaded, 16)
                with nc.allow_non_contiguous_dma(reason="a bias by partition"):
                    sp.dma_start(b1_sb[:, :, :], b1.rearrange("e (c p) -> p e c", p=P)).then_inc(loaded, 16)
                for e in range(EXPERTS):
                    for to, w in ((w1_sb, w1), (w2_sb, w2)):
                        sp.dma_start(to[:, e, :, :], w[e].rearrange("(c p) n -> p c n", p=P)).then_inc(w_in[e], 16)

                last = (EXPERTS - 1) * UNITS

                def store(i, slot, tiles):
                    sp.wait_ge(added, B * (last + i + 1))
                    rows = heads_of(T.acc[:, bass.ds(i * B * ROW, tiles * ROW)], ROW)
                    if tiles == B:
                        sp.dma_start(out[bass.ds(i * B * P, B * P), :].rearrange("(t p) f -> p t f", p=P),
                                     rows[:, :, 0:FEAT]).then_inc(stored, 16)
                        return
                    for t in range(tiles):
                        at = (FULL * B + t) * P
                        k = min(NODES - at, P)
                        sp.dma_start(out[at:at + k, :], rows[0:k, t, 0:FEAT]).then_inc(stored, 16)
                over_blocks(sp, EXPERTS - 1, store)
                sp.wait_ge(stored, 16 * (FULL + REST))

            @block.vector
            def _(dve):
                def add_b2(n, u):
                    chunk = T.acc[:, bass.ds(n * G * ROW, G * ROW)].rearrange("p (t r) -> p t r", r=ROW)[:, :, 0:FEAT]
                    need(dve, b2_done, n + 1)
                    dve.tensor_tensor(chunk, chunk, y_ps[:, 0:G * FEAT].rearrange("p (t f) -> p t f", f=FEAT),
                                      ALU.add).then_inc(b2_added, 1)
                steps(dve, CHUNKS, 2, add_b2)
                dve.wait_ge(b2_added, CHUNKS)

                for e in range(EXPERTS):
                    def unit(i, slot, tiles):
                        k = e * UNITS + i
                        for t in range(tiles):
                            at = i * B + t
                            need(dve, multiplied, 2 * k + t // 2 + 1)
                            if e > 0:
                                need(dve, added, B * (k - UNITS + 1))
                            to = T.acc[:, bass.ds(at * ROW, FEAT)]
                            y = y_ps[:, slot * 1024 + t * FEAT:slot * 1024 + (t + 1) * FEAT]
                            share_e = T.comb[:, bass.ds(at, 1), e]
                            dve.scalar_tensor_tensor(to, y, share_e, to, ALU.mult, ALU.add
                                                     ).then_inc(added, 1 + (B - tiles) * (t == tiles - 1))
                    over_blocks(dve, e, unit)

            @block.scalar
            def _(act):
                def take(n, u):
                    need(act, share_turned, n - 1)
                    nc.scalar.activation(share[:, u, :], T.comb[:, bass.ds(n * G, G), :]
                                         .rearrange("p t e -> p (t e)"), ACT.Copy).then_inc(share_in, 1)

                take(0, 0)

                def step(n, u):
                    if not isinstance(n, int) or n + 1 < CHUNKS:
                        take(n + 1, 1 - u)
                    need(act, share_turned, n + 1)
                    need(act, b2_done, n - 1)
                    nc.scalar.activation(share_t[:, u, :], h_ps[0:EXPERTS, u * 1024:u * 1024 + G * P],
                                         ACT.Copy).then_inc(share_out, 1)
                steps(act, CHUNKS, 2, step, tail=1)
                act.wait_ge(loaded, 32)

                for e in range(EXPERTS):
                    def unit(i, slot, tiles):
                        k = e * UNITS + i
                        for j in range(FC):
                            need(act, hidden, FC * k + j + 1)
                            if j == 0:
                                need(act, multiplied, 2 * (k - 1))
                            at = slot * 1024 + j * 512
                            nc.scalar.activation(hid[:, slot, j, 0:tiles * P], h_ps[:, at:at + tiles * P], ACT.Gelu,
                                                 bias=b1_sb[:, e, j:j + 1]).then_inc(gelu, 1)
                    over_blocks(act, e, unit)

            @block.tensor
            def _(pe):
                def turn(n, u):
                    need(pe, share_in, n + 1)
                    need(pe, share_out, n - 1)
                    pe.sem_inc(passed, 1)
                    for t in range(G):
                        at = u * 1024 + t * P
                        i = nc.tensor.transpose(h_ps[0:EXPERTS, at:at + P], share[:, u, t * EXPERTS:(t + 1) * EXPERTS],
                                                T.ident[:, :])
                    i.then_inc(share_turned, 1)

                pe.wait_ge(loaded, 32)
                turn(0, 0)

                def step(n, u):
                    if not isinstance(n, int) or n + 1 < CHUNKS:
                        turn(n + 1, 1 - u)
                    need(pe, share_out, n + 1)
                    need(pe, b2_added, n)
                    for t in range(G):
                        i = nc.tensor.matmul(y_ps[:, t * FEAT:(t + 1) * FEAT], share_t[:, u, t * P:(t + 1) * P],
                                             b2_sb[:, :], start=True, stop=True)
                    i.then_inc(b2_done, 1)
                steps(pe, CHUNKS, 2, step, tail=1)

                def expand(e, i, slot, tiles):
                    k = e * UNITS + i
                    for j in range(FC):
                        need(pe, gelu, FC * (k - 2) + j + 1)
                        at = slot * 1024 + j * 512
                        for c in range(FC):
                            m = nc.tensor.matmul(h_ps[:, at:at + tiles * P], w1_sb[:, e, c, j * P:(j + 1) * P],
                                                 T.tok_t[:, c, bass.ds(i * B * P, tiles * P)],
                                                 start=(c == 0), stop=(c == FC - 1))
                        m.then_inc(hidden, 1)

                def contract(e, i, slot, tiles):
                    k = e * UNITS + i
                    need(pe, gelu, FC * (k + 1))
                    need(pe, added, B * (k - 1))
                    for t in range(tiles):
                        at = slot * 1024 + t * FEAT
                        for j in range(FC):
                            m = nc.tensor.matmul(y_ps[:, at:at + FEAT], hid[:, slot, j, t * P:(t + 1) * P],
                                                 w2_sb[:, e, j, :], start=(j == 0), stop=(j == FC - 1))
                        if tiles < B:
                            if t == tiles - 1:
                                m.then_inc(multiplied, 2)
                        elif t % 2:
                            m.then_inc(multiplied, 1)

                pe.wait_ge(share_out, CHUNKS)
                pe.wait_ge(b2_added, CHUNKS)
                pe.wait_ge(w_in[0], 32)
                expand(0, 0, 0, B)
                for e in range(EXPERTS):
                    def unit(i, slot, tiles):
                        if tiles < B:
                            if e + 1 < EXPERTS:
                                pe.wait_ge(w_in[e + 1], 32)
                                expand(e + 1, 0, 1 - slot, B)
                        else:
                            expand(e, i + 1, 1 - slot, REST if isinstance(i, int) and i + 1 == FULL else B)
                        contract(e, i, slot, tiles)
                    over_blocks(pe, e, unit)


class Shared:
    pass


def program(nc, x, src_groups, dst_groups, dst_last, W, al, ar, b, wkv_t, wq, wo_t, bout, router_t, w1, b1, w2, b2,
            out):
    T = Shared()
    T.rows_d = [nc.dram_tensor(f"rows{l}_d", (NODES_PAD, ROW), F32, kind="Internal").ap() for l in range(LAYERS)]
    T.xt_d = nc.dram_tensor("xt_d", (NODES_PAD, FEAT), F32, kind="Internal").ap()
    T.loc_d = nc.dram_tensor("loc_d", (VP * BE,), BF16, kind="Internal").ap()
    T.flag_d = nc.dram_tensor("flag_d", (VP * BE + 8,), F32, kind="Internal").ap()
    T.key_d = nc.dram_tensor("key_d", (VP * BE + 8,), F32, kind="Internal").ap()
    T.win_d = nc.dram_tensor("win_d", (VP,), I32, kind="Internal").ap()
    with ExitStack() as ctx:
        def sb(name, shape, dt=F32):
            return ctx.enter_context(nc.sbuf_tensor(name, shape, dt))

        T.ident = sb("ident", [P, P])
        T.row = sb("row", [P, P])
        T.col = sb("col", [P, 1])
        T.one = sb("one", [P, 1])
        T.wext = sb("wext", [P, LAYERS, FC, EXT])
        T.mixw = sb("mixw", [P, FC, FEAT])
        T.er = sb("er", [P, NT, HEADS])
        T.er_flat = T.er[:, :, :].rearrange("p t h -> p (t h)")
        T.er3 = sb("er3", [P, NT, 3, HEADS], BF16)
        T.er3_flat = T.er3[:, :, :, :].rearrange("p t k h -> p (t k h)")
        T.src_t = sb("src_t", [P, VP, BT], I32)
        T.neg_loc = sb("neg_loc", [P, VP, BT])
        T.win = sb("win", [1, VP], I32)
        constants(nc, T)
        edge_tables(nc, T, dst_last, src_groups, dst_groups)
        with ExitStack() as early:
            T.wkv = early.enter_context(nc.sbuf_tensor("wkv", [P, FC, 2 * INNER], F32))
            T.dots = early.enter_context(nc.sbuf_tensor("dots", [P, PAIRS * P], F32))
            weights(nc, T, W, al, ar, wkv_t)
            first_nodes(nc, T, x)
            mix_matrix(nc, T, wq, wo_t)
        T.acc = sb("acc", [P, NT * ROW])
        with ExitStack() as mid:
            S = EdgeBuffers(nc, mid)
            for l in range(LAYERS):
                edge_pass(nc, T, S, l)
                if l + 1 < LAYERS:
                    next_nodes(nc, T, S, l, b)
        feed_forward(nc, T, b, x, bout, router_t, w1, b1, w2, b2, out)


def kernel(x, src, dst, L0_gnn_W, L0_gnn_al, L0_gnn_ar, L0_gnn_b, L0_mix_Wqkv, L0_mix_Wout, L0_mix_bout,
           L0_ffn_router_w, L0_ffn_w1, L0_ffn_b1, L0_ffn_w2, L0_ffn_b2):
    import numpy as np
    import concourse.bacc as bacc
    from concourse.bass_utils import run_bass_kernel_spmd

    def laid(a):
        return np.ascontiguousarray(a)

    x, src, dst = np.asarray(x), np.asarray(src), np.asarray(dst)
    x_pad = np.zeros((NODES_PAD, FEAT), x.dtype)
    x_pad[:NODES] = x
    src_groups = np.zeros((GROUPS * BE,), src.dtype)
    src_groups[:EDGES] = src
    dst_groups = np.full((GROUPS * BE,), NODES_PAD - 1, dst.dtype)
    dst_groups[:EDGES] = dst
    src_groups, dst_groups = src_groups.reshape(GROUPS, BE), dst_groups.reshape(GROUPS, BE)
    wqkv = np.asarray(L0_mix_Wqkv)
    ins = {
        "x": x_pad, "src_groups": src_groups, "dst_groups": dst_groups, "dst_last": laid(dst_groups[:, BE - 1]),
        "W": laid(L0_gnn_W), "al": laid(L0_gnn_al), "ar": laid(L0_gnn_ar), "b": laid(L0_gnn_b),
        "wkv_t": laid(wqkv[INNER:].T), "wq": laid(wqkv[:INNER]), "wo_t": laid(np.asarray(L0_mix_Wout).T),
        "bout": laid(L0_mix_bout), "router_t": laid(np.asarray(L0_ffn_router_w).T),
        "w1": laid(L0_ffn_w1), "b1": laid(L0_ffn_b1), "w2": laid(L0_ffn_w2), "b2": laid(L0_ffn_b2),
    }
    nc = bacc.Bacc("TRN2", target_bir_lowering=False, num_devices=1)
    arrays = {f"in_{k}": a for k, a in ins.items()}
    args = {k: nc.dram_tensor(f"in_{k}", a.shape, mybir.dt.from_np(a.dtype), kind="ExternalInput").ap()
            for k, a in ins.items()}
    out = nc.dram_tensor("out", (NODES, FEAT), F32, kind="ExternalOutput").ap()
    program(nc, out=out, **args)
    r = run_bass_kernel_spmd(nc, [arrays], core_ids=[0])
    return r.results[0]["out"]
```
